# Optimizing a Trainium2 kernel written in Bass

```python
import numpy as np
import jax
import jax.numpy as jnp

def _softmax(x, axis=-1):
    return jax.nn.softmax(x, axis=axis)

def _gelu(x):
    return jax.nn.gelu(x, approximate=True)

def _silu(x):
    return jax.nn.silu(x)

def _sigmoid(x):
    return jax.nn.sigmoid(x)

def _layernorm(x, axis=-1, eps=1e-05):
    m = jnp.mean(x, axis=axis, keepdims=True)
    v = jnp.var(x, axis=axis, keepdims=True)
    return (x - m) / jnp.sqrt(v + eps)

def _scatter_add(tgt, idx, src, axis=0):
    return tgt.at[idx].add(src)

def _segment_sum(src, seg, n):
    return jax.ops.segment_sum(src, seg, n)
kernel_name = 'mk_gnn_preln_d4_gnn_r16_dd3f63'

def setup_inputs(seed: int=0):
    np.random.seed(seed)
    _w = jnp.asarray

    def _rec_inputs():
        import jax
        import jax.numpy as jnp
        _gk = jax.random.key(seed)
        x = -0.0001006 + 1 * jax.random.normal(jax.random.fold_in(_gk, 1), (3125, 96), jnp.float32)
        src = jax.random.randint(jax.random.fold_in(_gk, 2), (50000,), 0, 3125, jnp.int32)
        dst = jax.random.randint(jax.random.fold_in(_gk, 3), (50000,), 0, 3125, jnp.int32)
        _o = jnp.argsort(dst, stable=True)
        src = src[_o]
        dst = dst[_o]
        edge_weight = jax.random.uniform(jax.random.fold_in(_gk, 13), (50000,), jnp.float32, 0.0, 0.999999)
        return (x, src, dst, edge_weight)
    x, src, dst, edge_weight = _rec_inputs()

    def _L0_gnn_setup():
        import jax, jax.numpy as jnp
        import numpy as np
        N_NODES = 3125
        N_EDGES = 50000
        D_MODEL = 96
        HEADS = 4
        key = jax.random.key(seed)
        ks = jax.random.split(key, 6)
        scale = 1.0 / np.sqrt(D_MODEL)
        return {'embeds': jax.random.normal(ks[0], (N_NODES, D_MODEL), dtype=jnp.float32), 'qW': jax.random.normal(ks[1], (D_MODEL, D_MODEL), dtype=jnp.float32) * scale, 'kW': jax.random.normal(ks[2], (D_MODEL, D_MODEL), dtype=jnp.float32) * scale, 'vW': jax.random.normal(ks[3], (D_MODEL, D_MODEL), dtype=jnp.float32) * scale, 'rows': jax.random.randint(ks[4], (N_EDGES,), 0, N_NODES, dtype=jnp.int32), 'cols': jax.random.randint(ks[5], (N_EDGES,), 0, N_NODES, dtype=jnp.int32)}
    _L0_gnn_all = _L0_gnn_setup()
    _L0_gnn_in = {k: v for k, v in _L0_gnn_all.items() if k in ('qW', 'kW', 'vW')}
    del _L0_gnn_all

    def _L1_gnn_setup():
        import jax, jax.numpy as jnp
        import numpy as np
        N_NODES = 3125
        N_EDGES = 50000
        D_IN = 96
        D_HID = 96
        D_OUT = 96
        EPS = 1e-12

        def _sage_pool_layer(x, src, dst, Wp, bp, Ws, Wn, b, n_nodes):
            m = jax.nn.relu(x @ Wp + bp)
            msgs = m[src]
            agg = jax.ops.segment_max(msgs, dst, num_segments=n_nodes)
            agg = jnp.where(jnp.isfinite(agg), agg, 0.0)
            return x @ Ws + agg @ Wn + b

        def _l2norm(h):
            n = jnp.linalg.norm(h, axis=1, keepdims=True)
            return h / jnp.maximum(n, EPS)
        key = jax.random.key(seed)
        ks = jax.random.split(key, 16)
        x = jax.random.normal(ks[0], (N_NODES, D_IN), dtype=jnp.float32)
        src = jax.random.randint(ks[1], (N_EDGES,), 0, N_NODES)
        dst = jax.random.randint(ks[2], (N_EDGES,), 0, N_NODES)
        s = 1.0 / np.sqrt(D_IN)
        return {'x': x, 'src': src, 'dst': dst, 'Wp1': jax.random.normal(ks[3], (D_IN, D_IN), dtype=jnp.float32) * s, 'bp1': jnp.zeros((D_IN,), jnp.float32), 'Ws1': jax.random.normal(ks[4], (D_IN, D_HID), dtype=jnp.float32) * s, 'Wn1': jax.random.normal(ks[5], (D_IN, D_HID), dtype=jnp.float32) * s, 'b1': jnp.zeros((D_HID,), jnp.float32), 'Wp2': jax.random.normal(ks[6], (D_HID, D_HID), dtype=jnp.float32) * s, 'bp2': jnp.zeros((D_HID,), jnp.float32), 'Ws2': jax.random.normal(ks[7], (D_HID, D_OUT), dtype=jnp.float32) * s, 'Wn2': jax.random.normal(ks[8], (D_HID, D_OUT), dtype=jnp.float32) * s, 'b2': jnp.zeros((D_OUT,), jnp.float32)}
    _L1_gnn_all = _L1_gnn_setup()
    _L1_gnn_in = {k: v for k, v in _L1_gnn_all.items() if k in ('Wp1', 'bp1', 'Ws1', 'Wn1', 'b1', 'Wp2', 'bp2', 'Ws2', 'Wn2', 'b2')}
    del _L1_gnn_all

    def _L2_gnn_setup():
        import jax, jax.numpy as jnp
        import numpy as np
        N_NODES = 3125
        N_EDGES = 50000
        D = 96
        key = jax.random.key(seed)
        k1, k2, k3, k4, k5, k6 = jax.random.split(key, 6)
        x = jax.random.normal(k1, (N_NODES, D), dtype=jnp.float32)
        edge_row = jax.random.randint(k2, (N_EDGES,), 0, N_NODES, dtype=jnp.int32)
        edge_col = jax.random.randint(k3, (N_EDGES,), 0, N_NODES, dtype=jnp.int32)
        edge_val = jax.random.uniform(k4, (N_EDGES,), dtype=jnp.float32)
        stdv = 1.0 / np.sqrt(D)
        weight_G = jax.random.uniform(k5, (D, D), dtype=jnp.float32, minval=-stdv, maxval=stdv)
        bias_G = jax.random.uniform(k6, (D,), dtype=jnp.float32, minval=-stdv, maxval=stdv)
        return {'x': x, 'edge_row': edge_row, 'edge_col': edge_col, 'edge_val': edge_val, 'weight_G': weight_G, 'bias_G': bias_G}
    _L2_gnn_all = _L2_gnn_setup()
    _L2_gnn_in = {k: v for k, v in _L2_gnn_all.items() if k in ('weight_G', 'bias_G')}
    del _L2_gnn_all

    def _L3_gnn_setup():
        import jax, jax.numpy as jnp
        import numpy as np
        K = 16
        ALPHA = 0.1
        key = jax.random.key(seed)
        k1, k2 = jax.random.split(key)
        N, E, D = (3125, 50000, 96)
        x = jax.random.normal(k1, (N, D), dtype=jnp.float32)
        edge_index = jax.random.randint(k2, (2, E), 0, N, dtype=jnp.int64)
        return {'x': x, 'edge_index': edge_index}
    _L3_gnn_all = _L3_gnn_setup()
    _L3_gnn_in = {k: v for k, v in _L3_gnn_all.items() if k in ()}
    del _L3_gnn_all
    return {'x': x, 'src': src, 'dst': dst, 'edge_weight': edge_weight, 'L0_gnn_qW': _L0_gnn_in['qW'], 'L0_gnn_kW': _L0_gnn_in['kW'], 'L0_gnn_vW': _L0_gnn_in['vW'], 'L1_gnn_Wp1': _L1_gnn_in['Wp1'], 'L1_gnn_bp1': _L1_gnn_in['bp1'], 'L1_gnn_Ws1': _L1_gnn_in['Ws1'], 'L1_gnn_Wn1': _L1_gnn_in['Wn1'], 'L1_gnn_b1': _L1_gnn_in['b1'], 'L1_gnn_Wp2': _L1_gnn_in['Wp2'], 'L1_gnn_bp2': _L1_gnn_in['bp2'], 'L1_gnn_Ws2': _L1_gnn_in['Ws2'], 'L1_gnn_Wn2': _L1_gnn_in['Wn2'], 'L1_gnn_b2': _L1_gnn_in['b2'], 'L2_gnn_weight_G': _L2_gnn_in['weight_G'], 'L2_gnn_bias_G': _L2_gnn_in['bias_G']}

def reference(x, src, dst, edge_weight, L0_gnn_qW, L0_gnn_kW, L0_gnn_vW, L1_gnn_Wp1, L1_gnn_bp1, L1_gnn_Ws1, L1_gnn_Wn1, L1_gnn_b1, L1_gnn_Wp2, L1_gnn_bp2, L1_gnn_Ws2, L1_gnn_Wn2, L1_gnn_b2, L2_gnn_weight_G, L2_gnn_bias_G):
    import jax
    import jax.numpy as jnp

    def _L0_gnn_ref(embeds, qW, kW, vW, rows, cols):
        import jax, jax.numpy as jnp
        import numpy as np
        N_NODES = 3125
        N_EDGES = 50000
        D_MODEL = 96
        HEADS = 4
        nvar, d = embeds.shape
        dh = d // HEADS
        e = rows.shape[0]
        q = (embeds[rows] @ qW).reshape(e, HEADS, dh)
        k = (embeds[cols] @ kW).reshape(e, HEADS, dh)
        v = (embeds[cols] @ vW).reshape(e, HEADS, dh)
        scores = jnp.clip(jnp.einsum('ehd,ehd->eh', q, k), -10.0, 10.0)
        exp_s = jnp.exp(scores)
        norms = jax.ops.segment_sum(exp_s, rows, num_segments=nvar)[rows]
        w = exp_s / (norms + 1e-08)
        res = jax.ops.segment_sum(w[:, :, None] * v, rows, num_segments=nvar).reshape(nvar, d)
        return embeds + res

    def _L1_gnn_ref(x, src, dst, Wp1, bp1, Ws1, Wn1, b1, Wp2, bp2, Ws2, Wn2, b2):
        import jax, jax.numpy as jnp
        import numpy as np
        N_NODES = 3125
        N_EDGES = 50000
        D_IN = 96
        D_HID = 96
        D_OUT = 96
        EPS = 1e-12

        def _sage_pool_layer(x, src, dst, Wp, bp, Ws, Wn, b, n_nodes):
            m = jax.nn.relu(x @ Wp + bp)
            msgs = m[src]
            agg = jax.ops.segment_max(msgs, dst, num_segments=n_nodes)
            agg = jnp.where(jnp.isfinite(agg), agg, 0.0)
            return x @ Ws + agg @ Wn + b

        def _l2norm(h):
            n = jnp.linalg.norm(h, axis=1, keepdims=True)
            return h / jnp.maximum(n, EPS)
        n = x.shape[0]
        h = _sage_pool_layer(x, src, dst, Wp1, bp1, Ws1, Wn1, b1, n)
        h = jax.nn.relu(h)
        h = _l2norm(h)
        h = _sage_pool_layer(h, src, dst, Wp2, bp2, Ws2, Wn2, b2, n)
        h = _l2norm(h)
        return h

    def _L2_gnn_ref(x, edge_row, edge_col, edge_val, weight_G, bias_G):
        import jax, jax.numpy as jnp
        import numpy as np
        N_NODES = 3125
        N_EDGES = 50000
        D = 96
        support = x @ weight_G
        gathered = support[edge_col] * edge_val[:, None]
        out = jax.ops.segment_sum(gathered, edge_row, num_segments=x.shape[0])
        return out + bias_G

    def _L3_gnn_ref(x, edge_index):
        import jax, jax.numpy as jnp
        import numpy as np
        K = 16
        ALPHA = 0.1
        N = x.shape[0]
        loop = jnp.arange(N, dtype=edge_index.dtype)
        row = jnp.concatenate([edge_index[0], loop])
        col = jnp.concatenate([edge_index[1], loop])
        deg = jax.ops.segment_sum(jnp.ones_like(col, dtype=x.dtype), col, num_segments=N)
        deg_inv_sqrt = jnp.where(deg > 0, jax.lax.rsqrt(jnp.maximum(deg, 1e-30)), 0.0)
        norm = (deg_inv_sqrt[row] * deg_inv_sqrt[col])[:, None]
        h = x
        for _ in range(K):
            h_neighbors = jax.ops.segment_sum(norm * h[row], col, num_segments=N)
            h = (1.0 - ALPHA) * h_neighbors + ALPHA * x
        return h
    edge_index = jnp.stack([src, dst])
    h = jnp.maximum(_layernorm(x, axis=-1), 0.0)
    x = x + _L0_gnn_ref(h, L0_gnn_qW, L0_gnn_kW, L0_gnn_vW, src, dst)
    h = jnp.maximum(_layernorm(x, axis=-1), 0.0)
    x = x + _L1_gnn_ref(h, src, dst, L1_gnn_Wp1, L1_gnn_bp1, L1_gnn_Ws1, L1_gnn_Wn1, L1_gnn_b1, L1_gnn_Wp2, L1_gnn_bp2, L1_gnn_Ws2, L1_gnn_Wn2, L1_gnn_b2)
    h = jnp.maximum(_layernorm(x, axis=-1), 0.0)
    x = x + _L2_gnn_ref(h, src, dst, edge_weight, L2_gnn_weight_G, L2_gnn_bias_G)
    h = jnp.maximum(_layernorm(x, axis=-1), 0.0)
    x = x + _L3_gnn_ref(h, edge_index)
    return x

_drawn_inputs = setup_inputs


def setup_inputs(seed=0):
    import zlib

    import numpy as np

    out = dict(_drawn_inputs(seed))
    spreads = {'L1_gnn_bp1': (0.0, 0.1),
     'L1_gnn_b1': (0.0, 0.1),
     'L1_gnn_bp2': (0.0, 0.1),
     'L1_gnn_b2': (0.0, 0.1)}
    factors = {}
    for name, (base, spread) in spreads.items():
        noise = np.random.default_rng([zlib.crc32(name.encode()), seed]).standard_normal(out[name].shape)
        drawn = base * np.exp(spread * noise) if base else spread * noise
        out[name] = jnp.asarray(drawn.astype(out[name].dtype))
    for name, factor in factors.items():
        out[name] = (out[name] * factor).astype(out[name].dtype)
    return out
```

```python
from contextlib import ExitStack

import concourse.bass as bass
from concourse import mybir

F32 = mybir.dt.float32
F16 = mybir.dt.float16
I32 = mybir.dt.int32
ALU = mybir.AluOpType
ACT = mybir.ActivationFunctionType
AX = mybir.AxisListType

N = 3125
E = 50000
D = 96
HEADS = 4
DH = D // HEADS
P = 128
T = -(-N // P)
NP = T * P
LAST = N - (T - 1) * P

BLK = 4 * P
RING = 4
LOOPS = -(-E // (BLK * RING))
NBLK = LOOPS * RING
EP = NBLK * BLK
CHUNKS = EP // P
PAD_DST = 4000
EXT = EP + 2 * BLK
ZERO_ROW = EP

GROUP = 20
NGROUP = NP // GROUP
KEYS = GROUP * T
USED = -(-E // P)
STEPS = (USED + NGROUP - 1) | 1
STILES = -(-STEPS // P)
SPAD = STILES * P

K_PROP = 16
ALPHA = 0.1
GSCALE = 4096.0


class Consts:
    pass


def stack():
    return ExitStack()


def node_view(dram):
    return dram.rearrange("(t p) d -> p t d", p=P)


def clear_semaphores(nc):
    used = sorted(nc.released_uncleared_semaphores)
    with nc.Block() as block:
        @block.gpsimd
        def _(pool):
            first = 0
            for n in range(len(used)):
                if n + 1 == len(used) or used[n + 1] != used[n] + 1:
                    nc.gpsimd.sem_clear(range(used[first], used[n] + 1))
                    first = n + 1


def make_constants(nc, ctx):
    c = Consts()
    c.gather_sem = lambda name: ctx.enter_context(nc.semaphore(name))
    sb = lambda name, shape, dt: ctx.enter_context(nc.sbuf_tensor(name, shape, dt))
    c.ident = sb("ident", [P, P], F32)
    c.ident16 = sb("ident16", [P, P], F16)
    c.ones = sb("ones", [P, P], F32)
    c.ones16 = sb("ones16", [P, 1], F16)
    c.upper = sb("upper", [P, P], F32)
    c.iota16 = sb("iota16", [P, KEYS], F16)
    c.src_rows = sb("src_rows", [P, CHUNKS], I32)
    c.deg = sb("deg", [P, T], F32)
    c.end_row = sb("end_row", [P, T], I32)
    with (
        nc.semaphore("const_step") as const_step,
        nc.sbuf_tensor("iota_i", [P, KEYS], I32) as iota_i,
        nc.Block() as block,
    ):
        @block.gpsimd
        def _(pool):
            nc.gpsimd.memset(c.ident[:, :], 0.0)
            nc.gpsimd.memset(c.ones[:, :], 1.0)
            nc.gpsimd.memset(c.ones16[:, :], 1.0)
            nc.gpsimd.iota(iota_i[:, :], [[1, KEYS]], base=0, channel_multiplier=0).then_inc(const_step, 1)
            pool.wait_ge(const_step, 1)
            nc.gpsimd.affine_select(out=c.ident[:, :], in_=c.ident[:, :], compare_op=ALU.not_equal, fill=1.0,
                                    base=0, pattern=[[-1, P]], channel_multiplier=1)
            nc.gpsimd.affine_select(out=c.upper[:, :], in_=c.ones[:, :], compare_op=ALU.is_ge, fill=0.0,
                                    base=0, pattern=[[1, P]], channel_multiplier=-1)
            nc.gpsimd.tensor_copy(c.iota16[:, :], iota_i[:, :]).then_inc(const_step, 1)
            pool.wait_ge(const_step, 2)
            nc.gpsimd.tensor_copy(c.ident16[:, :], c.ident[:, :])
    return c


def layernorm_relu(nc, name, x, h, sq, to_store=()):
    with (
        nc.sbuf_tensor(name + "_mean", [P, T], F32) as mean,
        nc.sbuf_tensor(name + "_var", [P, T], F32) as var,
        nc.semaphore(name + "_dve") as dve_step,
        nc.semaphore(name + "_std") as std_ready,
        nc.semaphore(name + "_st") as stored,
        nc.Block() as block,
    ):
        steps = 6

        @block.vector
        def _(dve):
            nc.vector.tensor_reduce(mean[:, :], x[:, :, :], AX.X, ALU.add).then_inc(dve_step, 1)
            dve.wait_ge(dve_step, 1)
            nc.vector.tensor_scalar(mean[:, :], mean[:, :], 1.0 / D, None, ALU.mult).then_inc(dve_step, 1)
            dve.wait_ge(dve_step, 2)
            nc.vector.tensor_tensor(h[:, :, :], x[:, :, :], mean[:, :].unsqueeze(2).to_broadcast([P, T, D]), ALU.subtract).then_inc(dve_step, 1)
            dve.wait_ge(dve_step, 3)
            nc.vector.tensor_tensor(sq[:, :, :], h[:, :, :], h[:, :, :], ALU.mult).then_inc(dve_step, 1)
            dve.wait_ge(dve_step, 4)
            nc.vector.tensor_reduce(var[:, :], sq[:, :, :], AX.X, ALU.add).then_inc(dve_step, 1)
            dve.wait_ge(dve_step, 5)
            nc.vector.tensor_scalar(var[:, :], var[:, :], 1.0 / D, 1e-5, ALU.mult, ALU.add).then_inc(dve_step, 1)
            dve.wait_ge(std_ready, 1)
            nc.vector.reciprocal(var[:, :], var[:, :]).then_inc(dve_step, 1)
            dve.wait_ge(dve_step, steps + 1)
            nc.vector.tensor_tensor(h[:, :, :], h[:, :, :], var[:, :].unsqueeze(2).to_broadcast([P, T, D]),
                                    ALU.mult).then_inc(dve_step, 1)
            dve.wait_ge(dve_step, steps + 2)
            nc.vector.tensor_scalar(h[:, :, :], h[:, :, :], 0.0, None, ALU.max).then_inc(dve_step, 1)

        @block.scalar
        def _(act):
            act.wait_ge(dve_step, steps)
            nc.scalar.activation(var[:, :], var[:, :], ACT.Sqrt).then_inc(std_ready, 1)

        @block.sync
        def _(sp):
            if to_store:
                sp.wait_ge(dve_step, steps + 3)
                for dram, tile in to_store:
                    sp.dma_start(node_view(dram), tile[:, :, :]).then_inc(stored, 16)
                sp.wait_ge(stored, 16 * len(to_store))


def project(nc, c, name, pairs, bias_dram, out, to_store=None, relu=False):
    ns = len(pairs)
    with stack() as ctx:
        weights = [ctx.enter_context(nc.sbuf_tensor(f"{name}_w{i}", [D, D], F32)) for i in range(ns)]
        bias = ctx.enter_context(nc.sbuf_tensor(name + "_b", [P, D], F32))
        xT = ctx.enter_context(nc.sbuf_tensor(name + "_xT", [D, 4, P], F32))
        xT_ps = [ctx.enter_context(nc.psum_tensor(f"{name}_xTps{i}", [P, 512], F32)) for i in range(4)]
        sum_ps = [ctx.enter_context(nc.psum_tensor(f"{name}_sum{i}", [P, 512], F32)) for i in range(2)]
        loaded = ctx.enter_context(nc.semaphore(name + "_loaded"))
        transposed = ctx.enter_context(nc.semaphore(name + "_transposed"))
        copied = ctx.enter_context(nc.semaphore(name + "_copied"))
        summed = ctx.enter_context(nc.semaphore(name + "_summed"))
        drained = ctx.enter_context(nc.semaphore(name + "_drained"))
        stored = ctx.enter_context(nc.semaphore(name + "_stored"))
        block = ctx.enter_context(nc.Block())
        nload = 16 * (ns + (bias_dram is not None))

        @block.sync
        def _(sp):
            for w, (_, w_dram) in zip(weights, pairs):
                sp.dma_start(w[:, :], w_dram).then_inc(loaded, 16)
            if bias_dram is not None:
                sp.dma_start(bias[:, :], bias_dram.rearrange("(a d) -> a d", a=1).to_broadcast([P, D])).then_inc(loaded, 16)
            if to_store is not None:
                sp.wait_ge(drained, T + (1 if relu else 0))
                sp.dma_start(node_view(to_store), out[:, :, :]).then_inc(stored, 16)
                sp.wait_ge(stored, 16)

        @block.tensor
        def _(pe):
            def transpose_tile(t):
                for s in range(ns):
                    i = t * ns + s
                    if i >= 4:
                        pe.wait_ge(copied, i - 3)
                    nc.tensor.transpose(xT_ps[i % 4][0:D, 0:P], pairs[s][0][:, t, :], c.ident[:, :]).then_inc(transposed, 1)

            transpose_tile(0)
            pe.wait_ge(loaded, nload)
            for t in range(T):
                if t + 1 < T:
                    transpose_tile(t + 1)
                if t >= 2:
                    pe.wait_ge(drained, t - 1)
                pe.wait_ge(copied, (t + 1) * ns)
                for s in range(ns):
                    mm = nc.tensor.matmul(sum_ps[t % 2][:, 0:D], xT[:, (t * ns + s) % 4, :], weights[s][:, :],
                                          start=s == 0, stop=s == ns - 1)
                mm.then_inc(summed, 1)

        @block.scalar
        def _(act):
            for i in range(T * ns):
                act.wait_ge(transposed, i + 1)
                if i >= 4:
                    act.wait_ge(summed, (i - 4) // ns + 1)
                nc.scalar.activation(xT[:, i % 4, :], xT_ps[i % 4][0:D, 0:P], ACT.Copy).then_inc(copied, 1)

        @block.vector
        def _(dve):
            if bias_dram is not None:
                dve.wait_ge(loaded, nload)
            for t in range(T):
                dve.wait_ge(summed, t + 1)
                if bias_dram is None:
                    nc.vector.tensor_copy(out[:, t, :], sum_ps[t % 2][:, 0:D]).then_inc(drained, 1)
                else:
                    nc.vector.tensor_tensor(out[:, t, :], sum_ps[t % 2][:, 0:D], bias[:, :], ALU.add).then_inc(drained, 1)
            if relu:
                dve.wait_ge(drained, T)
                nc.vector.tensor_scalar(out[:, :, :], out[:, :, :], 0.0, None, ALU.max).then_inc(drained, 1)


def attention_inputs(nc, c, x_dram, qW, kW, vW, h_dram, q_dram, k_dram, v_dram):
    with stack() as ctx:
        sb = lambda name, shape, dt: ctx.enter_context(nc.sbuf_tensor(name, shape, dt))
        x = sb("x0", [P, T, D], F32)
        h = sb("h0", [P, T, D], F32)
        sq = sb("sq0", [P, T, D], F32)
        w_rep = [sb(f"w_rep{i}", [D, HEADS, 4, DH], F32) for i in range(2)]
        w_in = [sb(f"w_in{i}", [D, D], F32) for i in range(3)]
        row_i = sb("row_i", [D, 1], I32)
        row = sb("row", [D, 1], F32)
        step = sb("step", [D, 3], F32)
        neg_lo = sb("neg_lo", [D, 2], F32)
        hT = sb("hT", [D, 2, P], F32)
        hi = sb("hi", [D, 2, 512], F16)
        q_st = sb("q_st", [D, 2, 512], F16)
        k_st = sb("k_st", [D, 2, 512], F16)
        v_all = sb("v_all", [P, T, HEADS, DH + 1], F32)
        with (
            nc.semaphore("x_loaded") as x_loaded,
            nc.semaphore("pad_zeroed") as pad_zeroed,
            nc.semaphore("w_copied") as w_copied,
            nc.semaphore("row_made") as row_made,
            nc.Block() as block,
        ):
            @block.sync
            def _(sp):
                sp.dma_start(x[:, 0:T - 1, :], x_dram[0:(T - 1) * P, :].rearrange("(t p) d -> p t d", p=P)).then_inc(x_loaded, 16)
                sp.wait_ge(pad_zeroed, 1)
                sp.dma_start(x[0:LAST, T - 1, :], x_dram[(T - 1) * P:N, :]).then_inc(x_loaded, 16)
                for w, dram in zip(w_in, (qW, kW, vW)):
                    sp.dma_start(w[:, :], dram).then_inc(x_loaded, 16)
                sp.wait_ge(x_loaded, 80)

            @block.gpsimd
            def _(pool):
                nc.gpsimd.memset(v_all[:, :, :, :], 1.0)
                nc.gpsimd.iota(row_i[:, :], [[0, 1]], base=0, channel_multiplier=1).then_inc(row_made, 1)

            @block.vector
            def _(dve):
                nc.vector.memset(x[:, T - 1, :], 0.0).then_inc(pad_zeroed, 1)
                dve.wait_ge(row_made, 1)
                nc.vector.tensor_copy(row[:, :], row_i[:, :]).then_inc(w_copied, 1)
                dve.wait_ge(w_copied, 1)
                for j in range(3):
                    nc.vector.tensor_scalar(step[:, j:j + 1], row[:, :], float((j + 1) * DH), None, ALU.is_ge).then_inc(w_copied, 1)
                dve.wait_ge(w_copied, 4)
                nc.vector.tensor_tensor(neg_lo[:, 0:1], step[:, 1:2], step[:, 0:1], ALU.subtract).then_inc(w_copied, 1)
                nc.vector.tensor_scalar(neg_lo[:, 1:2], step[:, 1:2], -1.0, None, ALU.mult)
                dve.wait_ge(w_copied, 5)
                nc.vector.tensor_tensor(neg_lo[:, 0:1], neg_lo[:, 0:1], step[:, 2:3], ALU.subtract)
                dve.wait_ge(x_loaded, 80)
                for i in range(2):
                    for j in range(4):
                        nc.vector.tensor_copy(w_rep[i][:, :, j, :], w_in[i][:, :].rearrange("p (h f) -> p h f", h=HEADS))

        layernorm_relu(nc, "ln0", x, h, sq, to_store=((h_dram, h),))

        tr_ps = [ctx.enter_context(nc.psum_tensor(f"a_tr{i}", [P, 512], F32)) for i in range(2)]
        q_ps = ctx.enter_context(nc.psum_tensor("a_q", [P, 512], F32))
        k_ps = ctx.enter_context(nc.psum_tensor("a_k", [P, 512], F32))
        v_ps = ctx.enter_context(nc.psum_tensor("a_v", [P, 512], F32))
        sem = lambda name: ctx.enter_context(nc.semaphore(name))
        transposed, copied = sem("a_transposed"), sem("a_copied")
        q_made, k_made, v_made = sem("a_q_made"), sem("a_k_made"), sem("a_v_made")
        hi_made, parts_made, v_kept = sem("a_hi_made"), sem("a_parts_made"), sem("a_v_kept")
        qk_stored = [sem("a_qk_stored0"), sem("a_qk_stored1")]
        v_stored = sem("a_v_stored")
        block = ctx.enter_context(nc.Block())

        @block.tensor
        def _(pe):
            def transpose_tile(t):
                if t >= 2:
                    pe.wait_ge(copied, t - 1)
                nc.tensor.transpose(tr_ps[t % 2][0:D, 0:P], h[:, t, :], c.ident[:, :]).then_inc(transposed, 1)

            transpose_tile(0)
            for t in range(T):
                if t + 1 < T:
                    transpose_tile(t + 1)
                pe.wait_ge(copied, t + 1)
                if t >= 1:
                    pe.wait_ge(parts_made, 2 * t)
                for ps, w, made in ((q_ps, w_rep[0], q_made), (k_ps, w_rep[1], k_made)):
                    for hd in range(HEADS):
                        mm = nc.tensor.matmul(ps[0:D, hd * P:(hd + 1) * P], w[:, hd, :, :].rearrange("p j f -> p (j f)"),
                                              hT[:, t % 2, :], start=True, stop=True)
                    mm.then_inc(made, 1)
                if t >= 1:
                    pe.wait_ge(v_kept, t)
                nc.tensor.matmul(v_ps[:, 0:D], hT[:, t % 2, :], w_in[2][:, :], start=True, stop=True).then_inc(v_made, 1)

        @block.scalar
        def _(act):
            for t in range(T):
                act.wait_ge(transposed, t + 1)
                if t >= 2:
                    act.wait_ge(v_made, t - 1)
                nc.scalar.activation(hT[:, t % 2, :], tr_ps[t % 2][0:D, 0:P], ACT.Copy).then_inc(copied, 1)
                for j, (ps, made) in enumerate(((q_ps, q_made), (k_ps, k_made))):
                    act.wait_ge(made, t + 1)
                    if t >= 1:
                        act.wait_ge(parts_made, 2 * t - 1 + j)
                    nc.scalar.activation(hi[:, j, :], ps[0:D, :], ACT.Copy).then_inc(hi_made, 1)

        @block.vector
        def _(dve):
            for t in range(T):
                for j, (ps, st) in enumerate(((q_ps, q_st), (k_ps, k_st))):
                    dve.wait_ge(hi_made, 2 * t + j + 1)
                    if j == 0 and t >= 2:
                        dve.wait_ge(qk_stored[t % 2], 32 * (t // 2))
                    nc.vector.scalar_tensor_tensor(st[:, t % 2, :], hi[:, j, :], neg_lo[:, j:j + 1], ps[0:D, :],
                                                   ALU.mult, ALU.add).then_inc(parts_made, 1)
                dve.wait_ge(v_made, t + 1)
                nc.vector.tensor_copy(v_all[:, t, :, 0:DH], v_ps[:, 0:D].rearrange("p (h f) -> p h f", h=HEADS)).then_inc(v_kept, 1)

        @block.sync
        def _(sp):
            for t in range(T):
                sp.wait_ge(parts_made, 2 * t + 2)
                sp.dma_start(q_dram[:, t, :], q_st[:, t % 2, :]).then_inc(qk_stored[t % 2], 16)
                sp.dma_start(k_dram[:, t, :], k_st[:, t % 2, :]).then_inc(qk_stored[t % 2], 16)
            sp.wait_ge(v_kept, T)
            sp.dma_start(v_dram, v_all[:, :, :, :].rearrange("p t h f -> p (t h f)")).then_inc(v_stored, 16)
            sp.wait_ge(v_stored, 16)
            sp.wait_ge(qk_stored[0], 32 * ((T + 1) // 2))
            sp.wait_ge(qk_stored[1], 32 * (T // 2))


def edge_lists(nc, c, src, dst, weight, src_pad, dst_pad, dst_ext, w_pad, dst_cols, w_cols):
    npad = EP - E
    quarter = CHUNKS // 4
    with stack() as ctx:
        sb = lambda name, shape, dt: ctx.enter_context(nc.sbuf_tensor(name, shape, dt))
        zero_i, far, before, zero_f = (sb("zero_i", [1, npad], I32), sb("far", [1, EXT - E], I32),
                                       sb("before", [1, 1], I32), sb("zero_f", [1, EXT - E], F32))
        src_i, dst_i = sb("src_c", [quarter, 4, P], I32), sb("dst_c", [quarter, 4, P], I32)
        src_f, dst_f, w_f = (sb(n, [quarter, 4, P], F32) for n in ("src_cf", "dst_cf", "w_cf"))
        dst_t, w_t = sb("dst_t", [P, CHUNKS], I32), sb("w_t", [P, CHUNKS], F32)
        rows_ps = [ctx.enter_context(nc.psum_tensor(f"rows_ps{i}", [P, 512], F32)) for i in range(3)]
        sem = lambda name: ctx.enter_context(nc.semaphore(name))
        pads, padded, rows_loaded, rows_cast, turned = sem("pads"), sem("padded"), sem("rows_loaded"), sem("rows_cast"), sem("turned")
        block = ctx.enter_context(nc.Block())
        flat = lambda a: a.rearrange("(a e) -> a e", a=1)
        src_flat = src_pad.rearrange("c p -> (c p)")
        dst_flat = dst_pad.rearrange("c p -> (c p)")

        @block.vector
        def _(dve):
            nc.vector.memset(zero_i[:, :], 0)
            nc.vector.memset(far[:, :], PAD_DST)
            nc.vector.memset(before[:, :], -1)
            nc.vector.memset(zero_f[:, :], 0.0).then_inc(pads, 1)
            dve.wait_ge(rows_loaded, 48)
            nc.vector.tensor_copy(src_f[:, :, :], src_i[:, :, :]).then_inc(rows_cast, 1)
            nc.vector.tensor_copy(dst_f[:, :, :], dst_i[:, :, :]).then_inc(rows_cast, 1)
            dve.wait_ge(turned, 12)
            nc.vector.tensor_copy(c.src_rows[:, :], rows_ps[0][:, 0:CHUNKS])
            nc.vector.tensor_scalar(dst_t[:, :], rows_ps[1][:, 0:CHUNKS], float(NP - 1), None, ALU.min).then_inc(rows_cast, 1)
            nc.vector.tensor_copy(w_t[:, :], rows_ps[2][:, 0:CHUNKS]).then_inc(rows_cast, 1)

        @block.sync
        def _(sp):
            sp.dma_start(flat(src_flat[0:E]), flat(src)).then_inc(padded, 16)
            sp.dma_start(flat(dst_flat[0:E]), flat(dst)).then_inc(padded, 16)
            sp.dma_start(flat(dst_ext[1:1 + E]), flat(dst)).then_inc(padded, 16)
            sp.dma_start(flat(w_pad[0:E]), flat(weight)).then_inc(padded, 16)
            sp.wait_ge(pads, 1)
            sp.dma_start(flat(src_flat[E:EP]), zero_i[:, :]).then_inc(padded, 16)
            sp.dma_start(flat(dst_flat[E:EP]), far[:, 0:npad]).then_inc(padded, 16)
            sp.dma_start(flat(dst_ext[1 + E:1 + EXT]), far[:, :]).then_inc(padded, 16)
            sp.dma_start(flat(dst_ext[0:1]), before[:, :]).then_inc(padded, 16)
            sp.dma_start(flat(w_pad[E:EXT]), zero_f[:, :]).then_inc(padded, 16)
            sp.wait_ge(padded, 9 * 16)
            chunks = lambda a: a.rearrange("(a q) p -> q a p", q=quarter)
            sp.dma_start(src_i[:, :, :], chunks(src_pad)).then_inc(rows_loaded, 16)
            sp.dma_start(dst_i[:, :, :], chunks(dst_pad)).then_inc(rows_loaded, 16)
            sp.dma_start(w_f[:, :, :], chunks(w_pad[0:EP].rearrange("(c p) -> c p", p=P))).then_inc(rows_loaded, 16)
            sp.wait_ge(rows_cast, 4)
            sp.dma_start(dst_cols, dst_t[:, :]).then_inc(rows_loaded, 16)
            sp.dma_start(w_cols, w_t[:, :]).then_inc(rows_loaded, 16)
            sp.wait_ge(rows_loaded, 80)

        @block.tensor
        def _(pe):
            pe.wait_ge(rows_cast, 2)
            for rows, ps in zip((src_f, dst_f, w_f), rows_ps):
                for a in range(4):
                    nc.tensor.transpose(ps[:, a * quarter:(a + 1) * quarter], rows[:, a, :],
                                        c.ident[0:quarter, 0:quarter]).then_inc(turned, 1)


def adjacency_schedule(nc, c, src_pad, dst_pad, group_dram, key_of, lane_of, group_row):
    with stack() as ctx:
        sb = lambda name, shape, dt: ctx.enter_context(nc.sbuf_tensor(name, shape, dt))
        dst_i, dst_f = sb("dst_i", [P, CHUNKS], I32), sb("dst_f", [P, CHUNKS], F32)
        below = sb("below", [P, CHUNKS], F32)
        o_i, o_f, limit = sb("o_i", [P, NGROUP], I32), sb("o_f", [P, NGROUP], F32), sb("limit", [P, NGROUP], F32)
        count = sb("count", [P, NGROUP], F32)
        first_i, first = sb("first_i", [P, NGROUP], I32), sb("first", [P, NGROUP], F32)
        s_i, s_f = sb("s_i", [P, STILES], I32), sb("s_f", [P, STILES], F32)
        group, offset = sb("group", [P, STILES], F32), sb("offset", [P, STILES], F32)
        chunk_f, chunk_i = sb("chunk_f", [P, STILES], F32), sb("chunk_i", [P, STILES], I32)
        src_g, dst_g = sb("src_g", [P, STILES, P], I32), sb("dst_g", [P, STILES, P], I32)
        tile_i, tile_f = sb("tile_i", [P, STILES, P], I32), sb("tile_f", [P, STILES, P], F32)
        lane_i, lane_f = sb("lane_i", [P, STILES, P], I32), sb("lane_f", [P, STILES, P], F32)
        key_f = sb("key_f", [P, STILES, P], F32)
        group_i = sb("group_i", [STILES, P], I32)
        ps = [ctx.enter_context(nc.psum_tensor(f"sched_ps{i}", [P, 512], F32)) for i in range(6)]
        sem = lambda name: ctx.enter_context(nc.semaphore(name))
        loaded, iotas, d_step, counted, summed = sem("sch_loaded"), sem("sch_iotas"), sem("sch_step"), sem("sch_counted"), sem("sch_summed")
        chunk_ready, gathered, keyed, turned, o_turned, o_cast, o_stored = (
            sem("sch_chunk"), c.gather_sem("sch_gathered"), sem("sch_keyed"), sem("sch_turned"), sem("sch_oturned"), sem("sch_ocast"), sem("sch_ostored"))
        block = ctx.enter_context(nc.Block())

        @block.sync
        def _(sp):
            sp.dma_start(dst_i[:, :], dst_pad.rearrange("c p -> (c p)").rearrange("(p c) -> p c", p=P)).then_inc(loaded, 16)
            sp.wait_ge(o_cast, 1)
            sp.dma_start(group_dram.rearrange("(t p) -> t p", p=P), group_i[:, :]).then_inc(o_stored, 16)
            sp.wait_ge(o_stored, 16)
            sp.dma_start(group_row[:, :], group_dram.rearrange("(a s) -> a s", a=1)).then_inc(o_stored, 16)
            sp.wait_ge(o_stored, 32)

        @block.gpsimd
        def _(pool):
            nc.gpsimd.iota(o_i[:, :], [[1, NGROUP]], base=0, channel_multiplier=0)
            nc.gpsimd.iota(s_i[:, :], [[P, STILES]], base=0, channel_multiplier=1).then_inc(iotas, 1)
            pool.wait_ge(chunk_ready, 1)
            for t in range(STILES):
                nc.gpsimd.indirect_dma_start(src_g[:, t, :], None, src_pad, bass.IndirectOffsetOnAxis(ap=chunk_i[:, t:t + 1], axis=0)).then_inc(gathered, 16)
                nc.gpsimd.indirect_dma_start(dst_g[:, t, :], None, dst_pad, bass.IndirectOffsetOnAxis(ap=chunk_i[:, t:t + 1], axis=0)).then_inc(gathered, 16)
            pool.wait_ge(gathered, 32 * STILES)

        @block.vector
        def _(dve):
            done = [0]

            def then_wait(ins):
                done[0] += 1
                ins.then_inc(d_step, 1)
                dve.wait_ge(d_step, done[0])

            dve.wait_ge(iotas, 1)
            nc.vector.tensor_copy(s_f[:, :], s_i[:, :])
            then_wait(nc.vector.tensor_copy(o_f[:, :], o_i[:, :]))
            then_wait(nc.vector.tensor_scalar(limit[:, :], o_f[:, :], float(GROUP), None, ALU.mult))
            dve.wait_ge(loaded, 16)
            then_wait(nc.vector.tensor_copy(dst_f[:, :], dst_i[:, :]))
            with dve.Fori(0, NGROUP) as o:
                nc.vector.tensor_scalar(below[:, :], dst_f[:, :], limit[:, bass.ds(o, 1)], None, ALU.is_lt, ALU.add,
                                        accum_out=count[:, bass.ds(o, 1)]).then_inc(counted, 1)
                dve.wait_ge(counted, o + 1)
            dve.wait_ge(summed, 1)
            then_wait(nc.vector.tensor_copy(first_i[:, :], ps[0][:, 0:NGROUP]))
            then_wait(nc.vector.tensor_scalar(first_i[:, :], first_i[:, :], 7, None, ALU.logical_shift_right))
            then_wait(nc.vector.tensor_copy(first[:, :], first_i[:, :]))
            then_wait(nc.vector.tensor_tensor(first[:, :], first[:, :], o_f[:, :], ALU.add))
            for t in range(STILES):
                then_wait(nc.vector.tensor_scalar(below[:, 1:NGROUP], first[:, 1:NGROUP], s_f[:, t:t + 1], None, ALU.is_le, ALU.add,
                                                  accum_out=group[:, t:t + 1]))
            then_wait(nc.vector.tensor_tensor(chunk_f[:, :], s_f[:, :], group[:, :], ALU.subtract))
            then_wait(nc.vector.tensor_scalar(chunk_f[:, :], chunk_f[:, :], float(CHUNKS - 1), None, ALU.min))
            nc.vector.tensor_copy(chunk_i[:, :], chunk_f[:, :]).then_inc(chunk_ready, 1)
            then_wait(nc.vector.tensor_scalar(offset[:, :], group[:, :], float(-KEYS), None, ALU.mult))
            then_wait(nc.vector.tensor_scalar(group[:, :], group[:, :], float(GROUP), None, ALU.mult))
            nc.vector.tensor_copy(chunk_f[:, :], group[:, :]).then_inc(keyed, 1)
            dve.wait_ge(o_turned, 1)
            nc.vector.tensor_copy(group_i[:, :], ps[1][0:STILES, 0:P]).then_inc(o_cast, 1)
            dve.wait_ge(gathered, 32 * STILES)
            nc.vector.tensor_scalar(tile_i[:, :, :], src_g[:, :, :], 7, None, ALU.logical_shift_right)
            then_wait(nc.vector.tensor_scalar(lane_i[:, :, :], src_g[:, :, :], P - 1, None, ALU.bitwise_and))
            nc.vector.tensor_copy(lane_f[:, :, :], lane_i[:, :, :])
            nc.vector.tensor_copy(tile_f[:, :, :], tile_i[:, :, :])
            then_wait(nc.vector.tensor_copy(key_f[:, :, :], dst_g[:, :, :]))
            for t in range(STILES):
                then_wait(nc.vector.scalar_tensor_tensor(key_f[:, t, :], key_f[:, t, :], float(T), tile_f[:, t, :], ALU.mult, ALU.add))
                nc.vector.tensor_scalar(key_f[:, t, :], key_f[:, t, :], offset[:, t:t + 1], None, ALU.add).then_inc(keyed, 1)
            for t in range(STILES):
                dve.wait_ge(turned, 2 * STILES)
                bank = 2 + (t // 4) * 2
                nc.vector.tensor_copy(key_of[:, t * P:(t + 1) * P], ps[bank][:, (t % 4) * P:(t % 4 + 1) * P])
                nc.vector.tensor_copy(lane_of[:, t * P:(t + 1) * P], ps[bank + 1][:, (t % 4) * P:(t % 4 + 1) * P])

        @block.tensor
        def _(pe):
            pe.wait_ge(counted, NGROUP)
            nc.tensor.matmul(ps[0][:, 0:NGROUP], c.ones[:, :], count[:, :], start=True, stop=True).then_inc(summed, 1)
            pe.wait_ge(keyed, 1)
            nc.tensor.transpose(ps[1][0:STILES, 0:P], chunk_f[:, :], c.ident[:, :]).then_inc(o_turned, 1)
            for t in range(STILES):
                pe.wait_ge(keyed, t + 2)
                bank = 2 + (t // 4) * 2
                nc.tensor.transpose(ps[bank][:, (t % 4) * P:(t % 4 + 1) * P], key_f[:, t, :], c.ident[:, :]).then_inc(turned, 1)
                nc.tensor.transpose(ps[bank + 1][:, (t % 4) * P:(t % 4 + 1) * P], lane_f[:, t, :], c.ident[:, :]).then_inc(turned, 1)


def build_adjacency(nc, c, adj, key_of, lane_of, group_row):
    pairs = (STEPS - 1) // 2
    assert STEPS == 2 * pairs + 1
    with stack() as ctx:
        sb = lambda name, shape, dt: ctx.enter_context(nc.sbuf_tensor(name, shape, dt))
        lane_hot = [sb(f"lane_hot{i}", [P, P], F16) for i in range(2)]
        key_hot = [sb(f"key_hot{i}", [P, KEYS], F16) for i in range(2)]
        part_ps = [ctx.enter_context(nc.psum_tensor(f"part{i}", [P, 512], F32)) for i in range(2)]
        sem = lambda name: ctx.enter_context(nc.semaphore(name))
        zeroed, hot_ready, part_ready, added = sem("adj_zeroed"), sem("hot_ready"), sem("part_ready"), sem("adj_added")
        block = ctx.enter_context(nc.Block())
        half = T // 2

        @block.gpsimd
        def _(pool):
            nc.gpsimd.memset(adj[:, 0:half, :], 0.0).then_inc(zeroed, 1)

        @block.tensor
        def _(pe):
            def product(s, b, first):
                pe.wait_ge(hot_ready, s + 1)
                if not first:
                    pe.wait_ge(added, s - 1)
                nc.tensor.matmul(part_ps[b][:, 0:KEYS], lane_hot[b][:, :], key_hot[b][:, :],
                                 start=True, stop=True).then_inc(part_ready, 1)

            product(0, 0, True)
            product(1, 1, True)
            with pe.Fori(1, pairs) as i:
                product(2 * i, 0, False)
                product(2 * i + 1, 1, False)
            product(STEPS - 1, 0, False)

        @block.vector
        def _(dve):
            def one_hot(s, b, first):
                if not first:
                    dve.wait_ge(part_ready, s - 1)
                nc.vector.tensor_scalar(lane_hot[b][:, :], c.iota16[:, 0:P], lane_of[:, bass.ds(s, 1)], None, ALU.is_equal)
                nc.vector.tensor_scalar(key_hot[b][:, :], c.iota16[:, :], key_of[:, bass.ds(s, 1)], None, ALU.is_equal).then_inc(hot_ready, 1)

            def add(s, b, first=False):
                g = nc.values_load(group_row[0:1, bass.ds(s, 1)], engines=(mybir.EngineType.DVE,), min_val=0, max_val=NP - GROUP,
                                   skip_runtime_bounds_check_because="a step's group is below NGROUP")
                columns = adj[:, :, bass.ds(g, GROUP)]
                dve.wait_ge(part_ready, s + 1)
                if not first:
                    dve.wait_ge(added, s)
                nc.vector.tensor_tensor(columns, columns, part_ps[b][:, 0:KEYS].rearrange("p (d k) -> p k d", d=GROUP),
                                        ALU.add).then_inc(added, 1)

            nc.vector.memset(adj[:, half:T, :], 0.0).then_inc(zeroed, 1)
            dve.wait_ge(zeroed, 2)
            one_hot(0, 0, True)
            one_hot(1, 1, True)
            add(0, 0, True)
            one_hot(2, 0, False)
            add(1, 1)
            with dve.Fori(1, pairs) as i:
                one_hot(2 * i + 1, 1, False)
                add(2 * i, 0)
                one_hot(2 * i + 2, 0, False)
                add(2 * i + 1, 1)
            add(STEPS - 1, 0)


def degrees(nc, c, adj):
    with stack() as ctx:
        sb = lambda name, shape, dt: ctx.enter_context(nc.sbuf_tensor(name, shape, dt))
        total, before, last, has = sb("total", [P, T], F32), sb("before_t", [P, T], F32), sb("last", [P, T], F32), sb("has", [P, T], F32)
        deg_ps = ctx.enter_context(nc.psum_tensor("deg_ps", [P, 512], F32))
        cum_ps = ctx.enter_context(nc.psum_tensor("cum_ps", [P, 512], F32))
        tot_ps = ctx.enter_context(nc.psum_tensor("tot_ps", [P, 512], F32))
        sem = lambda name: ctx.enter_context(nc.semaphore(name))
        deg_ready, deg_kept, cum_ready, d_step = sem("deg_ready"), sem("deg_kept"), sem("cum_ready"), sem("deg_step")
        block = ctx.enter_context(nc.Block())

        @block.tensor
        def _(pe):
            for t in range(T):
                for k in range(T):
                    mm = nc.tensor.matmul(deg_ps[:, t:t + 1], adj[:, k, t * P:(t + 1) * P], c.ones16[:, :], start=k == 0, stop=k == T - 1)
            mm.then_inc(deg_ready, 1)
            pe.wait_ge(deg_kept, 1)
            nc.tensor.matmul(cum_ps[:, 0:T], c.upper[:, :], c.deg[:, :], start=True, stop=True).then_inc(cum_ready, 1)
            nc.tensor.matmul(tot_ps[:, 0:T], c.ones[:, :], c.deg[:, :], start=True, stop=True).then_inc(cum_ready, 1)

        @block.vector
        def _(dve):
            done = [0]

            def then_wait(ins):
                done[0] += 1
                ins.then_inc(d_step, 1)
                dve.wait_ge(d_step, done[0])

            dve.wait_ge(deg_ready, 1)
            nc.vector.tensor_copy(c.deg[:, :], deg_ps[:, 0:T]).then_inc(deg_kept, 1)
            dve.wait_ge(cum_ready, 2)
            then_wait(nc.vector.tensor_copy(total[:, :], tot_ps[:, 0:T]))
            then_wait(nc.vector.tensor_tensor_scan(before[:, :], c.ones[:, 0:T], total[:, :], 0.0, ALU.mult, ALU.add))
            then_wait(nc.vector.tensor_tensor(before[:, :], before[:, :], total[:, :], ALU.subtract))
            then_wait(nc.vector.tensor_tensor(last[:, :], before[:, :], cum_ps[:, 0:T], ALU.add))
            nc.vector.tensor_scalar(has[:, :], c.deg[:, :], 0.0, None, ALU.is_gt)
            then_wait(nc.vector.tensor_scalar(last[:, :], last[:, :], float(-1 - ZERO_ROW), None, ALU.add))
            then_wait(nc.vector.tensor_tensor(last[:, :], last[:, :], has[:, :], ALU.mult))
            then_wait(nc.vector.tensor_scalar(last[:, :], last[:, :], float(ZERO_ROW), None, ALU.add))
            nc.vector.tensor_copy(c.end_row[:, :], last[:, :])


def attention(nc, c, adj, q_dram, k_dram, v_dram, res_dram):
    SR, AR = 3, 2
    with stack() as ctx:
        sb = lambda name, shape, dt: ctx.enter_context(nc.sbuf_tensor(name, shape, dt))
        k_st = sb("k_all", [D, T, 512], F16)
        v_all = sb("v_all2", [P, T, HEADS, DH + 1], F32)
        q_st = sb("q_tile", [D, 512], F16)
        e = sb("e", [P, SR, 512], F32)
        o_sb = sb("o_sb", [DH + 1, 512], F32)
        inv = sb("inv", [P, HEADS], F32)
        res = sb("res", [P, HEADS, DH], F32)
        s_ps = [ctx.enter_context(nc.psum_tensor(f"s_ps{i}", [P, 512], F32)) for i in range(SR)]
        a_ps = [ctx.enter_context(nc.psum_tensor(f"a_ps{i}", [P, 1024], F16)) for i in range(AR)]
        o_ps = ctx.enter_context(nc.psum_tensor("o_ps", [P, 512], F32))
        r_ps = ctx.enter_context(nc.psum_tensor("r_ps", [P, 512], F32))
        sem = lambda name: ctx.enter_context(nc.semaphore(name))
        kv_loaded, q_loaded, scored, clipped, exped, weighted, summed, o_kept, o_turned, res_ready, res_stored, d_step, turn_begun = (
            sem("kv_loaded"), sem("q_loaded"), sem("scored"), sem("clipped"), sem("exped"), sem("weighted"), sem("summed"),
            sem("o_kept"), sem("o_turned"), sem("res_ready"), sem("res_stored"), sem("att_step"), sem("turn_begun"))
        block = ctx.enter_context(nc.Block())

        def before(t, ring):
            return t - ring if t >= ring else max(u for u in range(T) if u % ring == t % ring)

        @block.sync
        def _(sp):
            sp.dma_start(k_st[:, :, :], k_dram).then_inc(kv_loaded, 16)
            sp.dma_start(v_all[:, :, :, :].rearrange("p t h f -> p (t h f)"), v_dram).then_inc(kv_loaded, 16)
            with sp.Fori(0, T) as i:
                sp.wait_ge(scored, T * (i + 1))
                sp.dma_start(q_st[:, :], q_dram[:, bass.ds(i, 1), :].rearrange("p a n -> p (a n)")).then_inc(q_loaded, 16)
                sp.wait_ge(res_ready, i + 1)
                sp.dma_start(res_dram[bass.ds(i * P, P), :], res[:, :, :].rearrange("p h f -> p (h f)")).then_inc(res_stored, 16)
            sp.wait_ge(res_stored, 16 * (T + 1))

        @block.tensor
        def _(pe):
            pe.sem_inc(scored, T)
            pe.sem_inc(summed, T)
            pe.wait_ge(kv_loaded, 32)
            with pe.Fori(0, T) as i:
                def score(t):
                    pe.wait_ge(weighted, T * i + before(t, AR) + 1 + (T if t >= AR else 0))
                    nc.tensor.transpose(a_ps[t % AR][:, 0:P], adj[:, bass.ds(i, 1), t * P:(t + 1) * P].rearrange("p a n -> p (a n)"), c.ident16[:, :])
                    pe.wait_ge(clipped, T * i + before(t, SR) + 1 + (T if t >= SR else 0))
                    for hd in range(HEADS):
                        mm = nc.tensor.matmul(s_ps[t % SR][:, hd * P:(hd + 1) * P], k_st[:, t, hd * P:(hd + 1) * P],
                                              q_st[:, hd * P:(hd + 1) * P], start=True, stop=True)
                    mm.then_inc(scored, 1)

                def value(t):
                    pe.wait_ge(weighted, T * i + T + t + 1)
                    if t == 0:
                        pe.wait_ge(o_kept, i + 1)
                    for hd in range(HEADS):
                        mm = nc.tensor.matmul(o_ps[0:DH + 1, hd * P:(hd + 1) * P], v_all[:, t, hd, :], e[:, t % SR, hd * P:(hd + 1) * P],
                                              start=t == 0 and hd == 0, stop=t == T - 1 and hd == HEADS - 1, skip_group_check=True)
                    mm.then_inc(summed, 1)

                pe.wait_ge(q_loaded, 16 * (i + 1))
                score(0)
                score(1)
                for t in range(T):
                    if t + 2 < T:
                        score(t + 2)
                    value(t)
                pe.wait_ge(o_kept, i + 2)
                pe.sem_inc(turn_begun, 1)
                for hd in range(HEADS):
                    tr = nc.tensor.transpose(r_ps[:, hd * (DH + 1):(hd + 1) * (DH + 1)], o_sb[:, hd * P:(hd + 1) * P], c.ident[0:DH + 1, 0:DH + 1])
                tr.then_inc(o_turned, 1)

        @block.scalar
        def _(act):
            act.sem_inc(o_kept, 1)
            with act.Fori(0, T) as i:
                for t in range(T):
                    act.wait_ge(clipped, T * i + T + t + 1)
                    nc.scalar.activation(e[:, t % SR, :], e[:, t % SR, :], ACT.Exp).then_inc(exped, 1)
                act.wait_ge(summed, T * (i + 2))
                nc.scalar.activation(o_sb[:, :], o_ps[0:DH + 1, :], ACT.Copy).then_inc(o_kept, 1)

        @block.vector
        def _(dve):
            dve.sem_inc(clipped, T)
            dve.sem_inc(weighted, T)
            with dve.Fori(0, T) as i:
                def clip(t):
                    dve.wait_ge(scored, T * i + T + t + 1)
                    dve.wait_ge(summed, T * i + before(t, SR) + 1 + (T if t >= SR else 0))
                    nc.vector.tensor_scalar(e[:, t % SR, :], s_ps[t % SR][:, :], 10.0, -10.0, ALU.min, ALU.max).then_inc(clipped, 1)

                def weight(t):
                    dve.wait_ge(exped, T * i + t + 1)
                    tile = e[:, t % SR, :].rearrange("p (h n) -> p h n", h=HEADS)
                    nc.vector.tensor_tensor(tile, tile, a_ps[t % AR][:, 0:P].unsqueeze(1).to_broadcast([P, HEADS, P]),
                                            ALU.mult).then_inc(weighted, 1)

                clip(0)
                for t in range(T):
                    if t + 1 < T:
                        clip(t + 1)
                    weight(t)
                dve.wait_ge(o_turned, i + 1)
                sums = r_ps[:, 0:HEADS * (DH + 1)].rearrange("p (h f) -> p h f", h=HEADS)
                nc.vector.tensor_scalar(inv[:, :], sums[:, :, DH], 1e-8, None, ALU.add).then_inc(d_step, 1)
                dve.wait_ge(d_step, 2 * i + 1)
                nc.vector.reciprocal(inv[:, :], inv[:, :]).then_inc(d_step, 1)
                dve.wait_ge(d_step, 2 * i + 2)
                dve.wait_ge(res_stored, 16 * (i + 1))
                nc.vector.tensor_tensor(res[:, :, :], sums[:, :, 0:DH], inv[:, :].unsqueeze(2).to_broadcast([P, HEADS, DH]),
                                        ALU.mult).then_inc(res_ready, 1)

        @block.gpsimd
        def _(pool):
            pool.sem_inc(res_stored, 16)


def max_pass(nc, c, name, table_dram, dst_ext, rows_dram):
    with stack() as ctx:
        sb = lambda n, shape, dt: ctx.enter_context(nc.sbuf_tensor(f"{name}_{n}", shape, dt))
        ps = lambda n: ctx.enter_context(nc.psum_tensor(f"{name}_{n}", [P, 512], F32))
        sem = lambda n: ctx.enter_context(nc.semaphore(f"{name}_{n}"))
        index = [sb(f"index{i}", [P, 8], I32) for i in range(2)]
        row = [sb(f"row{i}", [P, 4, D], F32) for i in range(RING)]
        dst_row = [sb(f"dst{i}", [D, BLK + 1], I32) for i in range(2)]
        same = [sb(f"same{i}", [D, BLK], F32) for i in range(2)]
        run = [sb(f"run{i}", [D, BLK], F32) for i in range(2)]
        out = [sb(f"out{i}", [P, 4, D], F32) for i in range(2)]
        zero = sb("zero", [1, D], F32)
        col_ps = [ps(f"col{i}") for i in range(2)]
        back_ps = [ps(f"back{i}") for i in range(2)]
        index_ready = [sem("index_ready0"), sem("index_ready1")]
        gathered = [c.gather_sem(f"{name}_gathered{i}") for i in range(RING)]
        listed = [sem(f"listed{i}") for i in range(2)]
        written = [sem(f"written{i}") for i in range(2)]
        turned, scanned, same_ready, back, kept, zeroed, zero_out, gather_begun = (
            sem("turned"), sem("scanned"), sem("same_ready"), sem("back"), sem("kept"), sem("zeroed"), sem("zero_out"), sem("gather_begun"))
        block = ctx.enter_context(nc.Block())

        @block.gpsimd
        def _(pool):
            with pool.Fori(0, LOOPS) as i:
                for b in range(RING):
                    if b % 2 == 0:
                        pool.wait_ge(index_ready[b // 2], i + 1)
                    pool.wait_ge(turned, RING * i + b + 1)
                    pool.sem_inc(gather_begun, 1)
                    for j in range(4):
                        nc.gpsimd.indirect_dma_start(row[b][:, j, :], None, table_dram,
                                                     bass.IndirectOffsetOnAxis(ap=index[b // 2][:, 4 * (b % 2) + j:4 * (b % 2) + j + 1], axis=0)
                                                     ).then_inc(gathered[b], 16)
            for b in range(RING):
                pool.wait_ge(gathered[b], 64 * LOOPS)

        @block.tensor
        def _(pe):
            pe.sem_inc(turned, RING)
            pe.sem_inc(back, 2)
            with pe.Fori(0, LOOPS) as i:
                for b in range(RING):
                    n = RING * i + b
                    pe.wait_ge(gathered[b], 64 * (i + 1))
                    pe.wait_ge(scanned, n + 1)
                    for j in range(4):
                        tr = nc.tensor.transpose(col_ps[b % 2][0:D, j * P:(j + 1) * P], row[b][:, j, :], c.ident[:, :])
                    tr.then_inc(turned, 1)
                    pe.wait_ge(scanned, n + 3)
                    pe.wait_ge(kept, n + 1)
                    for j in range(4):
                        tr = nc.tensor.transpose(back_ps[b % 2][:, j * D:(j + 1) * D], run[b % 2][:, j * P:(j + 1) * P], c.ident[0:D, 0:D])
                    tr.then_inc(back, 1)

        @block.vector
        def _(dve):
            nc.vector.memset(zero[:, :], 0.0).then_inc(zeroed, 1)
            nc.vector.memset(run[1][:, BLK - 1:BLK], 0.0).then_inc(scanned, 2)
            dve.wait_ge(scanned, 2)
            with dve.Fori(0, LOOPS) as i:
                for b in range(RING):
                    n = RING * i + b
                    dve.wait_ge(listed[b % 2], 16 * (2 * i + b // 2 + 1))
                    dve.wait_ge(scanned, n + 1)
                    nc.vector.tensor_tensor(same[b % 2][:, :], dst_row[b % 2][:, 1:BLK + 1], dst_row[b % 2][:, 0:BLK],
                                            ALU.is_equal).then_inc(same_ready, 1)
                    dve.wait_ge(turned, n + RING + 1)
                    dve.wait_ge(same_ready, n + 1)
                    dve.wait_ge(back, n + 1)
                    dve.wait_ge(scanned, n + 2)
                    nc.vector.tensor_tensor_scan(run[b % 2][:, :], same[b % 2][:, :], col_ps[b % 2][0:D, :],
                                                 run[1 - b % 2][:, BLK - 1:BLK], ALU.mult, ALU.max).then_inc(scanned, 1)

        @block.scalar
        def _(act):
            act.sem_inc(kept, 2)
            with act.Fori(0, LOOPS) as i:
                for b in range(0, RING, 2):
                    act.wait_ge(turned, RING * i + b + 2)
                    nc.scalar.activation(index[b // 2][:, :], c.src_rows[:, bass.ds(RING * 4 * i + 4 * b, 8)], ACT.Copy).then_inc(index_ready[b // 2], 1)
                for b in range(RING):
                    act.wait_ge(back, RING * i + b + 3)
                    act.wait_ge(written[b % 2], 16 * (2 * i + b // 2 + 1))
                    nc.scalar.activation(out[b % 2][:, :, :].rearrange("p j d -> p (j d)"), back_ps[b % 2][:, 0:4 * D], ACT.Copy).then_inc(kept, 1)

        @block.sync
        def _(sp):
            sp.sem_inc(written[0], 16)
            sp.sem_inc(written[1], 16)
            sp.wait_ge(zeroed, 1)
            sp.dma_start(rows_dram[ZERO_ROW:ZERO_ROW + 1, :], zero[:, :]).then_inc(zero_out, 16)

            def load_list(n, b):
                sp.dma_start(dst_row[b][:, :], dst_ext[bass.ds(n * BLK, BLK + 1)].rearrange("(a e) -> a e", a=1).to_broadcast([D, BLK + 1])).then_inc(listed[b], 16)

            load_list(0, 0)
            load_list(1, 1)
            with sp.Fori(0, LOOPS) as i:
                for b in range(RING):
                    n = RING * i + b
                    sp.wait_ge(kept, n + 3)
                    sp.dma_start(rows_dram[bass.ds(n * BLK, BLK), :].rearrange("(j p) d -> p j d", p=P), out[b % 2][:, :, :]).then_inc(written[b % 2], 16)
                    load_list(n + 2, b % 2)
            for b in range(2):
                sp.wait_ge(written[b], 16 * (1 + NBLK // 2))
                sp.wait_ge(listed[b], 16 * (1 + NBLK // 2))
            sp.wait_ge(zero_out, 16)


SUM_SCALE = 1024.0


def sum_pass(nc, c, table_dram, dst_cols, w_cols, total):
    banks = [(n, min(512, NP - n)) for n in range(0, NP, 512)]
    with stack() as ctx:
        sb = lambda n, shape, dt: ctx.enter_context(nc.sbuf_tensor(f"sum_{n}", shape, dt))
        sem = lambda n: ctx.enter_context(nc.semaphore(f"sum_{n}"))
        index = [sb(f"index{i}", [P, 8], I32) for i in range(2)]
        row = [sb(f"row{i}", [P, 4, D], F32) for i in range(RING)]
        term = [sb(f"term{i}", [P, D], F32) for i in range(2)]
        hi = [sb(f"hi{i}", [P, D], F16) for i in range(2)]
        lo = [sb(f"lo{i}", [P, D], F16) for i in range(2)]
        hots = sb("hots", [P, 2, NP], F16)
        hot = [hots[:, i, :] for i in range(2)]
        nodes = sb("nodes", [P, NP], F16)
        nodes_i = hots[:, :, :].rearrange("p a n -> p (a n)").bitcast(I32)
        src_mid = sb("src_mid", [P, CHUNKS], F32)
        dst_rows, w_rows = sb("dst_rows", [P, CHUNKS], I32), sb("w_rows", [P, CHUNKS], F32)
        no_term = sb("no_term", [P, D], F16)
        sums_ps = [ctx.enter_context(nc.psum_tensor(f"sums{n}", [P, 512], F32)) for n in range(len(banks))]
        back_ps = ctx.enter_context(nc.psum_tensor("sums_back", [P, 512], F32))
        index_ready = [sem("index_ready0"), sem("index_ready1")]
        gathered = [c.gather_sem(f"sum_gathered{i}") for i in range(RING)]
        ready, terms, split, used, gather_begun, kept, turned, drained, numbers = (
            sem("ready"), sem("terms"), sem("split"), sem("used"), sem("gather_begun"), sem("kept"), sem("turned"), sem("drained"), sem("numbers"))
        listed = sem("listed")
        block = ctx.enter_context(nc.Block())
        sumsT = hots[0:D, :, :].rearrange("p a n -> p (a n)").bitcast(F32)

        @block.gpsimd
        def _(pool):
            nc.gpsimd.iota(nodes_i, [[1, NP]], base=-NP // 2, channel_multiplier=0).then_inc(numbers, 1)
            with pool.Fori(0, LOOPS) as i:
                for b in range(RING):
                    if b % 2 == 0:
                        pool.wait_ge(index_ready[b // 2], i + 1)
                    pool.wait_ge(terms, 16 * i + 4 * b + 4)
                    pool.sem_inc(gather_begun, 1)
                    for j in range(4):
                        nc.gpsimd.indirect_dma_start(row[b][:, j, :], None, table_dram,
                                                     bass.IndirectOffsetOnAxis(ap=index[b // 2][:, 4 * (b % 2) + j:4 * (b % 2) + j + 1], axis=0)
                                                     ).then_inc(gathered[b], 16)
            for b in range(RING):
                pool.wait_ge(gathered[b], 64 * LOOPS)

        @block.sync
        def _(sp):
            sp.dma_start(dst_rows[:, :], dst_cols).then_inc(listed, 16)
            sp.dma_start(w_rows[:, :], w_cols).then_inc(listed, 16)

        @block.scalar
        def _(act):
            act.wait_ge(listed, 32)
            with act.Fori(0, LOOPS) as i:
                for b in range(0, RING, 2):
                    act.wait_ge(terms, 16 * i + 4 * b + 8)
                    nc.scalar.activation(index[b // 2][:, :], dst_rows[:, bass.ds(RING * 4 * i + 4 * b, 8)], ACT.Copy).then_inc(index_ready[b // 2], 1)

        @block.vector
        def _(dve):
            dve.sem_inc(terms, 16)
            dve.wait_ge(listed, 32)
            dve.wait_ge(numbers, 1)
            nc.vector.tensor_copy(nodes[:, :], nodes_i).then_inc(drained, 1)
            nc.vector.tensor_copy(src_mid[:, :], c.src_rows[:, :]).then_inc(drained, 1)
            nc.vector.memset(no_term[:, :], 0.0).then_inc(ready, 1)
            dve.wait_ge(drained, 2)
            nc.vector.tensor_scalar(src_mid[:, :], src_mid[:, :], float(-NP // 2), None, ALU.add).then_inc(drained, 1)
            dve.wait_ge(drained, 3)
            with dve.Fori(0, LOOPS) as i:
                for b in range(RING):
                    for j in range(4):
                        k = 4 * b + j
                        chunk = 16 * i + k
                        dve.wait_ge(used, chunk + 1)
                        nc.vector.tensor_scalar(hot[k % 2][:, :], nodes[:, :], src_mid[:, bass.ds(chunk, 1)], None, ALU.is_equal)
                        if j == 0:
                            dve.wait_ge(gathered[b], 64 * (i + 1))
                        t = nc.vector.tensor_scalar(term[k % 2][:, :], row[b][:, j, :], w_rows[:, bass.ds(chunk, 1)], SUM_SCALE, ALU.mult, ALU.mult)
                        t.then_inc(terms, 1)
                        dve.wait_ge(terms, chunk + 17)
                        nc.vector.tensor_copy(hi[k % 2][:, :], term[k % 2][:, :]).then_inc(split, 1)
                        dve.wait_ge(split, chunk + 1)
                        nc.vector.tensor_tensor(lo[k % 2][:, :], term[k % 2][:, :], hi[k % 2][:, :], ALU.subtract).then_inc(ready, 1)
            dve.wait_ge(used, CHUNKS + 3)
            for n, (first, size) in enumerate(banks):
                nc.vector.tensor_scalar(sumsT[:, first:first + size], sums_ps[n][0:D, 0:size], 1.0 / SUM_SCALE, None, ALU.mult).then_inc(kept, 1)
            for t in range(T):
                dve.wait_ge(turned, t + 1)
                nc.vector.tensor_copy(total[:, t, :], back_ps[:, 0:D] if t % 2 == 0 else sums_ps[0][:, 0:D]).then_inc(drained, 1)

        @block.tensor
        def _(pe):
            pe.sem_inc(used, 2)
            pe.wait_ge(ready, 1)
            for n, (first, size) in enumerate(banks):
                nc.tensor.matmul(sums_ps[n][0:D, 0:size], no_term[:, :], nodes[:, first:first + size], start=True, stop=False, skip_group_check=True)
            with pe.Fori(0, LOOPS) as i:
                for k in range(16):
                    chunk = 16 * i + k
                    pe.wait_ge(ready, chunk + 2)
                    for part in (hi, lo):
                        for n, (first, size) in enumerate(banks):
                            mm = nc.tensor.matmul(sums_ps[n][0:D, 0:size], part[k % 2][:, :], hot[k % 2][:, first:first + size],
                                                  start=False, stop=False, skip_group_check=True)
                    mm.then_inc(used, 1)
            for n, (first, size) in enumerate(banks):
                mm = nc.tensor.matmul(sums_ps[n][0:D, 0:size], no_term[:, :], nodes[:, first:first + size], start=False, stop=True, skip_group_check=True)
            mm.then_inc(used, 1)
            pe.wait_ge(kept, len(banks))
            for t in range(T):
                if t >= 2:
                    pe.wait_ge(drained, 3 + t - 1)
                ps = back_ps if t % 2 == 0 else sums_ps[0]
                nc.tensor.transpose(ps[:, 0:D], sumsT[:, t * P:(t + 1) * P], c.ident[0:D, 0:D]).then_inc(turned, 1)


def load_nodes(nc, c, name, pairs, rows_dram=None, agg=None):
    with (
        nc.semaphore(name + "_loaded") as loaded,
        nc.Block() as block,
    ):
        picked = c.gather_sem(name + "_picked") if rows_dram is not None else None

        @block.sync
        def _(sp):
            for tile, dram in pairs:
                sp.dma_start(tile[:, :, :], node_view(dram)).then_inc(loaded, 16)
            sp.wait_ge(loaded, 16 * len(pairs))

        @block.gpsimd
        def _(pool):
            if rows_dram is not None:
                for t in range(T):
                    nc.gpsimd.indirect_dma_start(agg[:, t, :], None, rows_dram, bass.IndirectOffsetOnAxis(ap=c.end_row[:, t:t + 1], axis=0)).then_inc(picked, 16)
                pool.wait_ge(picked, 16 * T)


def add_nodes(nc, name, x, terms, store=None, bias_dram=None):
    with (
        nc.sbuf_tensor(name + "_bias", [P, D], F32) as bias,
        nc.semaphore(name + "_added") as added,
        nc.semaphore(name + "_bias_loaded") as bias_loaded,
        nc.semaphore(name + "_stored") as stored,
        nc.Block() as block,
    ):
        steps = len(terms) + (bias_dram is not None)

        @block.sync
        def _(sp):
            if bias_dram is not None:
                sp.dma_start(bias[:, :], bias_dram.rearrange("(a d) -> a d", a=1).to_broadcast([P, D])).then_inc(bias_loaded, 16)
            sp.wait_ge(added, steps)
            if store is not None:
                sp.dma_start(node_view(store), x[:, :, :]).then_inc(stored, 16)
                sp.wait_ge(stored, 16)

        @block.vector
        def _(dve):
            for n, term in enumerate(terms[1:]):
                if n:
                    dve.wait_ge(added, n)
                nc.vector.tensor_tensor(terms[0][:, :, :], terms[0][:, :, :], term[:, :, :], ALU.add).then_inc(added, 1)
            n = len(terms) - 1
            if bias_dram is not None:
                dve.wait_ge(bias_loaded, 16)
                if n:
                    dve.wait_ge(added, n)
                nc.vector.tensor_tensor(terms[0][:, :, :], terms[0][:, :, :], bias[:, :].unsqueeze(1).to_broadcast([P, T, D]), ALU.add).then_inc(added, 1)
                n += 1
            if n:
                dve.wait_ge(added, n)
            nc.vector.tensor_tensor(x[:, :, :], x[:, :, :], terms[0][:, :, :], ALU.add).then_inc(added, 1)


def l2_normalise(nc, name, h, sq, relu, store=None):
    with (
        nc.sbuf_tensor(name + "_norm", [P, T], F32) as norm,
        nc.semaphore(name + "_dve") as dve_step,
        nc.semaphore(name + "_root") as root_ready,
        nc.semaphore(name + "_stored") as stored,
        nc.Block() as block,
    ):
        r = 1 if relu else 0

        @block.vector
        def _(dve):
            if relu:
                nc.vector.tensor_scalar(h[:, :, :], h[:, :, :], 0.0, None, ALU.max).then_inc(dve_step, 1)
                dve.wait_ge(dve_step, 1)
            nc.vector.tensor_tensor(sq[:, :, :], h[:, :, :], h[:, :, :], ALU.mult).then_inc(dve_step, 1)
            dve.wait_ge(dve_step, r + 1)
            nc.vector.tensor_reduce(norm[:, :], sq[:, :, :], AX.X, ALU.add).then_inc(dve_step, 1)
            dve.wait_ge(root_ready, 1)
            nc.vector.tensor_scalar(norm[:, :], norm[:, :], 1e-12, None, ALU.max).then_inc(dve_step, 1)
            dve.wait_ge(dve_step, r + 3)
            nc.vector.reciprocal(norm[:, :], norm[:, :]).then_inc(dve_step, 1)
            dve.wait_ge(dve_step, r + 4)
            nc.vector.tensor_tensor(h[:, :, :], h[:, :, :], norm[:, :].unsqueeze(2).to_broadcast([P, T, D]), ALU.mult).then_inc(dve_step, 1)

        @block.scalar
        def _(act):
            act.wait_ge(dve_step, r + 2)
            nc.scalar.activation(norm[:, :], norm[:, :], ACT.Sqrt).then_inc(root_ready, 1)

        @block.sync
        def _(sp):
            if store is not None:
                sp.wait_ge(dve_step, r + 5)
                sp.dma_start(node_view(store), h[:, :, :]).then_inc(stored, 16)
                sp.wait_ge(stored, 16)


def propagate_setup(nc, c, adj, h, base, g, state, coef, root):
    with stack() as ctx:
        sb = lambda n, shape, dt: ctx.enter_context(nc.sbuf_tensor(n, shape, dt))
        inv = sb("inv_deg", [P, T], F32)
        sem = lambda n: ctx.enter_context(nc.semaphore(n))
        d_step, rooted = sem("ps_step"), sem("ps_rooted")
        block = ctx.enter_context(nc.Block())

        @block.gpsimd
        def _(pool):
            for t in range(T):
                own = adj[:, t, t * P:(t + 1) * P]
                nc.gpsimd.tensor_tensor(own, own, c.ident16[:, :], ALU.add)

        @block.vector
        def _(dve):
            done = [0]

            def then_wait(ins):
                done[0] += 1
                ins.then_inc(d_step, 1)
                dve.wait_ge(d_step, done[0])

            then_wait(nc.vector.tensor_scalar(inv[:, :], c.deg[:, :], 1.0, None, ALU.add))
            dve.wait_ge(rooted, 1)
            then_wait(nc.vector.reciprocal(inv[:, :], inv[:, :]))
            then_wait(nc.vector.tensor_scalar(coef[:, :], inv[:, :], 1.0 - ALPHA, None, ALU.mult))
            then_wait(nc.vector.reciprocal(inv[:, :], root[:, :]))
            then_wait(nc.vector.tensor_tensor(state[:, :, :], h[:, :, :], inv[:, :].unsqueeze(2).to_broadcast([P, T, D]), ALU.mult))
            then_wait(nc.vector.tensor_scalar(state[:, :, :], state[:, :, :], GSCALE, None, ALU.mult))
            then_wait(nc.vector.tensor_scalar(root[:, :], root[:, :], 1.0 / GSCALE, None, ALU.mult))
            then_wait(nc.vector.tensor_copy(g[:, :, 0, :], state[:, :, :]))
            then_wait(nc.vector.tensor_tensor(g[:, :, 1, :], state[:, :, :], g[:, :, 0, :], ALU.subtract))
            then_wait(nc.vector.tensor_scalar(base[:, :, :], state[:, :, :], ALPHA, None, ALU.mult))

        @block.scalar
        def _(act):
            act.wait_ge(d_step, 1)
            nc.scalar.activation(root[:, :], inv[:, :], ACT.Sqrt).then_inc(rooted, 1)


def propagate(nc, c, adj, base, g, state, coef):
    BANKS = 5
    with stack() as ctx:
        ps = [ctx.enter_context(nc.psum_tensor(f"prop{i}", [P, 512], F32)) for i in range(BANKS)]
        part = ctx.enter_context(nc.sbuf_tensor("part", [P, 2, D], F32))
        sem = lambda n: ctx.enter_context(nc.semaphore(n))
        summed, low_added, state_ready, hi_ready, updated = sem("pr_summed"), sem("pr_low"), sem("pr_state"), sem("pr_hi"), sem("pr_updated")
        block = ctx.enter_context(nc.Block())

        @block.tensor
        def _(pe):
            with pe.Fori(0, K_PROP // 2) as i:
                for half in range(2):
                    step = 2 * i + half
                    for t in range(T):
                        pe.wait_ge(state_ready, T * step + T + t - BANKS + 1)
                        for k in range(T):
                            if t == 0:
                                pe.wait_ge(updated, T * step + k + 1)
                            mm = nc.tensor.matmul(ps[t % BANKS][:, 0:2 * D], adj[:, k, t * P:(t + 1) * P],
                                                  g[half][:, k, :, :].rearrange("p a d -> p (a d)"), start=k == 0, stop=k == T - 1)
                        mm.then_inc(summed, 1)

        @block.vector
        def _(dve):
            dve.sem_inc(updated, T)
            dve.sem_inc(state_ready, T)
            with dve.Fori(0, K_PROP // 2) as i:
                for half in range(2):
                    step = 2 * i + half

                    def new_state(t):
                        dve.wait_ge(summed, T * step + t + 1)
                        nc.vector.scalar_tensor_tensor(part[:, t % 2, :], ps[t % BANKS][:, D:2 * D], coef[:, t:t + 1], base[:, t, :], ALU.mult, ALU.add).then_inc(low_added, 1)
                        dve.wait_ge(low_added, T * step + t + 1)
                        nc.vector.scalar_tensor_tensor(state[:, t, :], ps[t % BANKS][:, 0:D], coef[:, t:t + 1], part[:, t % 2, :], ALU.mult, ALU.add).then_inc(state_ready, 1)

                    def low_part(t):
                        dve.wait_ge(hi_ready, T * step + t + 1)
                        nc.vector.tensor_tensor(g[1 - half][:, t, 1, :], state[:, t, :], g[1 - half][:, t, 0, :], ALU.subtract).then_inc(updated, 1)

                    for t in range(T):
                        new_state(t)
                        low_part(t)

        @block.scalar
        def _(act):
            with act.Fori(0, K_PROP // 2) as i:
                for half in range(2):
                    for t in range(T):
                        act.wait_ge(state_ready, T * (2 * i + half) + T + t + 1)
                        nc.scalar.activation(g[1 - half][:, t, 0, :], state[:, t, :], ACT.Copy).then_inc(hi_ready, 1)


def finish(nc, x, state, root, x_dram, out):
    with (
        nc.semaphore("x_back") as x_back,
        nc.semaphore("scaled") as scaled,
        nc.semaphore("out_written") as out_written,
        nc.Block() as block,
    ):
        @block.sync
        def _(sp):
            sp.dma_start(x, node_view(x_dram)).then_inc(x_back, 16)
            sp.wait_ge(scaled, 2)
            sp.dma_start(out[0:(T - 1) * P, :].rearrange("(t p) d -> p t d", p=P), state[:, 0:T - 1, :]).then_inc(out_written, 16)
            sp.dma_start(out[(T - 1) * P:N, :], state[0:LAST, T - 1, :]).then_inc(out_written, 16)
            sp.wait_ge(out_written, 32)

        @block.vector
        def _(dve):
            nc.vector.tensor_tensor(state[:, :, :], state[:, :, :], root[:, :].unsqueeze(2).to_broadcast([P, T, D]), ALU.mult).then_inc(scaled, 1)
            dve.wait_ge(scaled, 1)
            dve.wait_ge(x_back, 16)
            nc.vector.tensor_tensor(state[:, :, :], state[:, :, :], x, ALU.add).then_inc(scaled, 1)


def gnn(nc, x, src, dst, edge_weight, qW, kW, vW, Wp1, bp1, Ws1, Wn1, b1, Wp2, bp2, Ws2, Wn2, b2, G, bG, out):
    scratch = lambda name, shape, dt=F32: nc.dram_tensor(name, shape, dt).ap()
    src_pad, dst_pad = scratch("src_pad", (CHUNKS, P), I32), scratch("dst_pad", (CHUNKS, P), I32)
    dst_ext = scratch("dst_ext", (1 + EXT,), I32)
    w_pad = scratch("w_pad", (EXT,))
    dst_cols, w_cols = scratch("dst_cols", (P, CHUNKS), I32), scratch("w_cols", (P, CHUNKS))
    group_dram = scratch("group_dram", (SPAD,), I32)
    q_dram, k_dram = scratch("q_dram", (D, T, 512), F16), scratch("k_dram", (D, T, 512), F16)
    v_dram = scratch("v_dram", (P, T * HEADS * (DH + 1)))
    h_dram, res_dram, x_dram, table = (scratch(n, (NP, D)) for n in ("h_dram", "res_dram", "x_dram", "table"))
    rows_dram = scratch("rows_dram", (EP + 1, D))

    with stack() as ctx:
        c = make_constants(nc, ctx)
        attention_inputs(nc, c, x, qW, kW, vW, h_dram, q_dram, k_dram, v_dram)
        edge_lists(nc, c, src, dst, edge_weight, src_pad, dst_pad, dst_ext, w_pad, dst_cols, w_cols)
        adj = ctx.enter_context(nc.sbuf_tensor("adj", [P, T, NP], F16))
        with stack() as own:
            key_of = own.enter_context(nc.sbuf_tensor("key_of", [P, SPAD], F32))
            lane_of = own.enter_context(nc.sbuf_tensor("lane_of", [P, SPAD], F32))
            group_row = own.enter_context(nc.sbuf_tensor("group_row", [1, SPAD], I32))
            adjacency_schedule(nc, c, src_pad, dst_pad, group_dram, key_of, lane_of, group_row)
            build_adjacency(nc, c, adj, key_of, lane_of, group_row)
        degrees(nc, c, adj)
        attention(nc, c, adj, q_dram, k_dram, v_dram, res_dram)

        def node_tiles(own, name, n):
            return [own.enter_context(nc.sbuf_tensor(f"{name}{i}", [P, T, D], F32)) for i in range(n)]

        with stack() as own:
            xt, h, r = node_tiles(own, "n1_", 3)
            with nc.semaphore("x_in") as x_in, nc.semaphore("x_zeroed") as x_zeroed, nc.Block() as block:
                @block.vector
                def _(dve):
                    nc.vector.memset(xt[:, T - 1, :], 0.0).then_inc(x_zeroed, 1)

                @block.sync
                def _(sp):
                    sp.dma_start(xt[:, 0:T - 1, :], x[0:(T - 1) * P, :].rearrange("(t p) d -> p t d", p=P)).then_inc(x_in, 16)
                    sp.wait_ge(x_zeroed, 1)
                    sp.dma_start(xt[0:LAST, T - 1, :], x[(T - 1) * P:N, :]).then_inc(x_in, 16)
                    sp.wait_ge(x_in, 32)
            load_nodes(nc, c, "ld1", ((h, h_dram), (r, res_dram)))
            add_nodes(nc, "add1", xt, (h, r), store=x_dram)
            layernorm_relu(nc, "ln1", xt, h, r, to_store=((h_dram, h),))
            project(nc, c, "pool1", ((h, Wp1),), bp1, r, to_store=table, relu=True)
        clear_semaphores(nc)
        max_pass(nc, c, "max1", table, dst_ext, rows_dram)
        with stack() as own:
            h, agg, o = node_tiles(own, "n2_", 3)
            load_nodes(nc, c, "ld2", ((h, h_dram),), rows_dram, agg)
            project(nc, c, "sage1", ((h, Ws1), (agg, Wn1)), b1, o)
            l2_normalise(nc, "l2a", o, h, relu=True, store=h_dram)
            project(nc, c, "pool2", ((o, Wp2),), bp2, agg, to_store=table, relu=True)
        max_pass(nc, c, "max2", table, dst_ext, rows_dram)
        with stack() as own:
            h, agg, o = node_tiles(own, "n3_", 3)
            load_nodes(nc, c, "ld3", ((h, h_dram),), rows_dram, agg)
            project(nc, c, "sage2", ((h, Ws2), (agg, Wn2)), b2, o)
            l2_normalise(nc, "l2b", o, h, relu=False)
            load_nodes(nc, c, "ld4", ((h, x_dram),))
            add_nodes(nc, "add2", h, (o,), store=x_dram)
            layernorm_relu(nc, "ln2", h, o, agg)
            project(nc, c, "support", ((o, G),), None, agg, to_store=table)
        clear_semaphores(nc)
        with stack() as own:
            state, = node_tiles(own, "n4_", 1)
            sum_pass(nc, c, table, dst_cols, w_cols, state)
            base, = node_tiles(own, "n6_", 1)
            coef, root = (own.enter_context(nc.sbuf_tensor(n, [P, T], F32)) for n in ("coef", "root"))
            with stack() as ln:
                h, = node_tiles(ln, "n5_", 1)
                load_nodes(nc, c, "ld5", ((h, x_dram),))
                add_nodes(nc, "add3", h, (state,), store=x_dram, bias_dram=bG)
                layernorm_relu(nc, "ln3", h, base, state)
            g = [own.enter_context(nc.sbuf_tensor(f"g{i}", [P, T, 2, D], F16)) for i in range(2)]
            propagate_setup(nc, c, adj, base, base, g[0], state, coef, root)
            propagate(nc, c, adj, base, g, state, coef)
            xb = g[1][:, :, :, :].rearrange("p t a d -> p (t a d)").bitcast(F32).rearrange("p (t d) -> p t d", t=T)
            finish(nc, xb, state, root, x_dram, out)


_INS = ["x", "src", "dst", "edge_weight", "L0_gnn_qW", "L0_gnn_kW", "L0_gnn_vW", "L1_gnn_Wp1", "L1_gnn_bp1", "L1_gnn_Ws1",
        "L1_gnn_Wn1", "L1_gnn_b1", "L1_gnn_Wp2", "L1_gnn_bp2", "L1_gnn_Ws2", "L1_gnn_Wn2", "L1_gnn_b2",
        "L2_gnn_weight_G", "L2_gnn_bias_G"]


def kernel(**inputs):
    import numpy as np
    import concourse.bacc as bacc
    from concourse.bass_utils import run_bass_kernel_spmd

    nc = bacc.Bacc("TRN2", target_bir_lowering=False, num_devices=1)
    arrays, args = {}, []
    for name in _INS:
        a = np.ascontiguousarray(inputs[name])
        arrays[f"in_{name}_dram"] = a
        args.append(nc.dram_tensor(f"in_{name}_dram", a.shape, mybir.dt.from_np(a.dtype), kind="ExternalInput").ap())
    out = nc.dram_tensor("out_0_dram", (N, D), F32, kind="ExternalOutput").ap()
    gnn(nc, *args, out)
    r = run_bass_kernel_spmd(nc, [arrays], core_ids=[0])
    return r.results[0]["out_0_dram"]
```

```python
import math
from contextlib import ExitStack

import concourse.bass as bass
from concourse import mybir

F32 = mybir.dt.float32
F16 = mybir.dt.float16
I32 = mybir.dt.int32
ALU = mybir.AluOpType
ACT = mybir.ActivationFunctionType
AX = mybir.AxisListType

N = 3125
E = 50000
D = 96
HEADS = 4
DH = D // HEADS
P = 128
T = -(-N // P)
NP = T * P
LAST = N - (T - 1) * P

BLK = 4 * P
RING = 4
LOOPS = -(-E // (BLK * RING))
NBLK = LOOPS * RING
EP = NBLK * BLK
CHUNKS = EP // P
PAD_DST = 4000
EXT = EP + 2 * BLK
ZERO_ROW = EP

GROUP = 16
NGROUP = NP // GROUP
KEYS = GROUP * T
WIN = 3
PHASES = 4
WROWS = CHUNKS * PHASES
NSTEP = NGROUP * WIN
GT = -(-NGROUP // P)
USED = -(-E // P)
STEPS = (USED + NGROUP - 1) | 1
STILES = -(-STEPS // P)
SPAD = STILES * P

W_SCALE = 1024.0
K_PROP = 16
ALPHA = 0.1
GSCALE = 4096.0


class Consts:
    pass


def stack():
    return ExitStack()


def node_view(dram):
    return dram.rearrange("(t p) d -> p t d", p=P)


def clear_semaphores(nc):
    used = sorted(nc.released_uncleared_semaphores)
    with nc.Block() as block:
        @block.gpsimd
        def _(pool):
            first = 0
            for n in range(len(used)):
                if n + 1 == len(used) or used[n + 1] != used[n] + 1:
                    nc.gpsimd.sem_clear(range(used[first], used[n] + 1))
                    first = n + 1


def make_constants(nc, ctx):
    c = Consts()
    c.gather_sem = lambda name: ctx.enter_context(nc.semaphore(name))
    sb = lambda name, shape, dt: ctx.enter_context(nc.sbuf_tensor(name, shape, dt))
    c.ident = sb("ident", [P, P], F32)
    c.ident16 = sb("ident16", [P, P], F16)
    c.ones = sb("ones", [P, P], F32)
    c.ones16 = sb("ones16", [P, 1], F16)
    c.iota16 = sb("iota16", [P, KEYS], F16)
    c.deg = sb("deg", [P, T], F32)
    c.end_row = sb("end_row", [P, T], I32)
    with (
        nc.semaphore("const_step") as const_step,
        nc.sbuf_tensor("iota_i", [P, KEYS], I32) as iota_i,
        nc.Block() as block,
    ):
        @block.gpsimd
        def _(pool):
            nc.gpsimd.memset(c.ident[:, :], 0.0)
            nc.gpsimd.memset(c.ones[:, :], 1.0)
            nc.gpsimd.memset(c.ones16[:, :], 1.0)
            nc.gpsimd.iota(iota_i[:, :], [[1, KEYS]], base=0, channel_multiplier=0).then_inc(const_step, 1)
            pool.wait_ge(const_step, 1)
            nc.gpsimd.affine_select(out=c.ident[:, :], in_=c.ident[:, :], compare_op=ALU.not_equal, fill=1.0,
                                    base=0, pattern=[[-1, P]], channel_multiplier=1)
            nc.gpsimd.tensor_copy(c.iota16[:, :], iota_i[:, :]).then_inc(const_step, 1)
            pool.wait_ge(const_step, 2)
            nc.gpsimd.tensor_copy(c.ident16[:, :], c.ident[:, :])
    return c


def layernorm_relu(nc, name, x, h, sq, to_store=()):
    with (
        nc.sbuf_tensor(name + "_mean", [P, T], F32) as mean,
        nc.sbuf_tensor(name + "_var", [P, T], F32) as var,
        nc.semaphore(name + "_dve") as dve_step,
        nc.semaphore(name + "_std") as std_ready,
        nc.semaphore(name + "_st") as stored,
        nc.Block() as block,
    ):
        steps = 6

        @block.vector
        def _(dve):
            nc.vector.tensor_reduce(mean[:, :], x[:, :, :], AX.X, ALU.add).then_inc(dve_step, 1)
            dve.wait_ge(dve_step, 1)
            nc.vector.tensor_scalar(mean[:, :], mean[:, :], 1.0 / D, None, ALU.mult).then_inc(dve_step, 1)
            dve.wait_ge(dve_step, 2)
            nc.vector.tensor_tensor(h[:, :, :], x[:, :, :], mean[:, :].unsqueeze(2).to_broadcast([P, T, D]), ALU.subtract).then_inc(dve_step, 1)
            dve.wait_ge(dve_step, 3)
            nc.vector.tensor_tensor(sq[:, :, :], h[:, :, :], h[:, :, :], ALU.mult).then_inc(dve_step, 1)
            dve.wait_ge(dve_step, 4)
            nc.vector.tensor_reduce(var[:, :], sq[:, :, :], AX.X, ALU.add).then_inc(dve_step, 1)
            dve.wait_ge(dve_step, 5)
            nc.vector.tensor_scalar(var[:, :], var[:, :], 1.0 / D, 1e-5, ALU.mult, ALU.add).then_inc(dve_step, 1)
            dve.wait_ge(std_ready, 1)
            nc.vector.reciprocal(var[:, :], var[:, :]).then_inc(dve_step, 1)
            dve.wait_ge(dve_step, steps + 1)
            nc.vector.tensor_tensor(h[:, :, :], h[:, :, :], var[:, :].unsqueeze(2).to_broadcast([P, T, D]),
                                    ALU.mult).then_inc(dve_step, 1)
            dve.wait_ge(dve_step, steps + 2)
            nc.vector.tensor_scalar(h[:, :, :], h[:, :, :], 0.0, None, ALU.max).then_inc(dve_step, 1)

        @block.scalar
        def _(act):
            act.wait_ge(dve_step, steps)
            nc.scalar.activation(var[:, :], var[:, :], ACT.Sqrt).then_inc(std_ready, 1)

        @block.sync
        def _(sp):
            if to_store:
                sp.wait_ge(dve_step, steps + 3)
                for dram, tile in to_store:
                    sp.dma_start(node_view(dram), tile[:, :, :]).then_inc(stored, 16)
                sp.wait_ge(stored, 16 * len(to_store))


def project(nc, c, name, pairs, bias_dram, out, to_store=None, relu=False):
    ns = len(pairs)
    with stack() as ctx:
        weights = [ctx.enter_context(nc.sbuf_tensor(f"{name}_w{i}", [D, D], F32)) for i in range(ns)]
        bias = ctx.enter_context(nc.sbuf_tensor(name + "_b", [P, D], F32))
        xT = ctx.enter_context(nc.sbuf_tensor(name + "_xT", [D, 4, P], F32))
        xT_ps = [ctx.enter_context(nc.psum_tensor(f"{name}_xTps{i}", [P, 512], F32)) for i in range(4)]
        sum_ps = [ctx.enter_context(nc.psum_tensor(f"{name}_sum{i}", [P, 512], F32)) for i in range(2)]
        loaded = ctx.enter_context(nc.semaphore(name + "_loaded"))
        transposed = ctx.enter_context(nc.semaphore(name + "_transposed"))
        copied = ctx.enter_context(nc.semaphore(name + "_copied"))
        summed = ctx.enter_context(nc.semaphore(name + "_summed"))
        drained = ctx.enter_context(nc.semaphore(name + "_drained"))
        stored = ctx.enter_context(nc.semaphore(name + "_stored"))
        block = ctx.enter_context(nc.Block())
        nload = 16 * (ns + (bias_dram is not None))

        @block.sync
        def _(sp):
            for w, (_, w_dram) in zip(weights, pairs):
                sp.dma_start(w[:, :], w_dram).then_inc(loaded, 16)
            if bias_dram is not None:
                sp.dma_start(bias[:, :], bias_dram.rearrange("(a d) -> a d", a=1).to_broadcast([P, D])).then_inc(loaded, 16)
            if to_store is not None:
                sp.wait_ge(drained, T + (1 if relu else 0))
                sp.dma_start(node_view(to_store), out[:, :, :]).then_inc(stored, 16)
                sp.wait_ge(stored, 16)

        @block.tensor
        def _(pe):
            def transpose_tile(t):
                for s in range(ns):
                    i = t * ns + s
                    if i >= 4:
                        pe.wait_ge(copied, i - 3)
                    nc.tensor.transpose(xT_ps[i % 4][0:D, 0:P], pairs[s][0][:, t, :], c.ident[:, :]).then_inc(transposed, 1)

            transpose_tile(0)
            pe.wait_ge(loaded, nload)
            for t in range(T):
                if t + 1 < T:
                    transpose_tile(t + 1)
                if t >= 2:
                    pe.wait_ge(drained, t - 1)
                pe.wait_ge(copied, (t + 1) * ns)
                for s in range(ns):
                    mm = nc.tensor.matmul(sum_ps[t % 2][:, 0:D], xT[:, (t * ns + s) % 4, :], weights[s][:, :],
                                          start=s == 0, stop=s == ns - 1)
                mm.then_inc(summed, 1)

        @block.scalar
        def _(act):
            for i in range(T * ns):
                act.wait_ge(transposed, i + 1)
                if i >= 4:
                    act.wait_ge(summed, (i - 4) // ns + 1)
                nc.scalar.activation(xT[:, i % 4, :], xT_ps[i % 4][0:D, 0:P], ACT.Copy).then_inc(copied, 1)

        @block.vector
        def _(dve):
            if bias_dram is not None:
                dve.wait_ge(loaded, nload)
            for t in range(T):
                dve.wait_ge(summed, t + 1)
                if bias_dram is None:
                    nc.vector.tensor_copy(out[:, t, :], sum_ps[t % 2][:, 0:D]).then_inc(drained, 1)
                else:
                    nc.vector.tensor_tensor(out[:, t, :], sum_ps[t % 2][:, 0:D], bias[:, :], ALU.add).then_inc(drained, 1)
            if relu:
                dve.wait_ge(drained, T)
                nc.vector.tensor_scalar(out[:, :, :], out[:, :, :], 0.0, None, ALU.max).then_inc(drained, 1)


def attention_inputs(nc, c, x_dram, qW, kW, vW, h_dram, q_dram, k_dram, v_dram):
    with stack() as ctx:
        sb = lambda name, shape, dt: ctx.enter_context(nc.sbuf_tensor(name, shape, dt))
        x = sb("x0", [P, T, D], F32)
        h = sb("h0", [P, T, D], F32)
        sq = sb("sq0", [P, T, D], F32)
        w_rep = [sb(f"w_rep{i}", [D, HEADS, 4, DH], F32) for i in range(2)]
        w_in = [sb(f"w_in{i}", [D, D], F32) for i in range(3)]
        row_i = sb("row_i", [D, 1], I32)
        row = sb("row", [D, 1], F32)
        step = sb("step", [D, 3], F32)
        neg_lo = sb("neg_lo", [D, 2], F32)
        hT = sb("hT", [D, 2, P], F32)
        hi = sb("hi", [D, 2, 512], F16)
        q_st = sb("q_st", [D, 2, 512], F16)
        k_st = sb("k_st", [D, 2, 512], F16)
        v_all = sb("v_all", [P, T, HEADS, DH + 1], F32)
        with (
            nc.semaphore("x_loaded") as x_loaded,
            nc.semaphore("pad_zeroed") as pad_zeroed,
            nc.semaphore("w_copied") as w_copied,
            nc.semaphore("row_made") as row_made,
            nc.Block() as block,
        ):
            @block.sync
            def _(sp):
                sp.dma_start(x[:, 0:T - 1, :], x_dram[0:(T - 1) * P, :].rearrange("(t p) d -> p t d", p=P)).then_inc(x_loaded, 16)
                sp.wait_ge(pad_zeroed, 1)
                sp.dma_start(x[0:LAST, T - 1, :], x_dram[(T - 1) * P:N, :]).then_inc(x_loaded, 16)
                for w, dram in zip(w_in, (qW, kW, vW)):
                    sp.dma_start(w[:, :], dram).then_inc(x_loaded, 16)
                sp.wait_ge(x_loaded, 80)

            @block.gpsimd
            def _(pool):
                nc.gpsimd.memset(v_all[:, :, :, :], 1.0)
                nc.gpsimd.iota(row_i[:, :], [[0, 1]], base=0, channel_multiplier=1).then_inc(row_made, 1)

            @block.vector
            def _(dve):
                nc.vector.memset(x[:, T - 1, :], 0.0).then_inc(pad_zeroed, 1)
                dve.wait_ge(row_made, 1)
                nc.vector.tensor_copy(row[:, :], row_i[:, :]).then_inc(w_copied, 1)
                dve.wait_ge(w_copied, 1)
                for j in range(3):
                    nc.vector.tensor_scalar(step[:, j:j + 1], row[:, :], float((j + 1) * DH), None, ALU.is_ge).then_inc(w_copied, 1)
                dve.wait_ge(w_copied, 4)
                nc.vector.tensor_tensor(neg_lo[:, 0:1], step[:, 1:2], step[:, 0:1], ALU.subtract).then_inc(w_copied, 1)
                nc.vector.tensor_scalar(neg_lo[:, 1:2], step[:, 1:2], -1.0, None, ALU.mult)
                dve.wait_ge(w_copied, 5)
                nc.vector.tensor_tensor(neg_lo[:, 0:1], neg_lo[:, 0:1], step[:, 2:3], ALU.subtract)
                dve.wait_ge(x_loaded, 80)
                for i in range(2):
                    for j in range(4):
                        nc.vector.tensor_copy(w_rep[i][:, :, j, :], w_in[i][:, :].rearrange("p (h f) -> p h f", h=HEADS))

        layernorm_relu(nc, "ln0", x, h, sq, to_store=((h_dram, h),))

        tr_ps = [ctx.enter_context(nc.psum_tensor(f"a_tr{i}", [P, 512], F32)) for i in range(2)]
        q_ps = ctx.enter_context(nc.psum_tensor("a_q", [P, 512], F32))
        k_ps = ctx.enter_context(nc.psum_tensor("a_k", [P, 512], F32))
        v_ps = ctx.enter_context(nc.psum_tensor("a_v", [P, 512], F32))
        sem = lambda name: ctx.enter_context(nc.semaphore(name))
        transposed, copied = sem("a_transposed"), sem("a_copied")
        q_made, k_made, v_made = sem("a_q_made"), sem("a_k_made"), sem("a_v_made")
        hi_made, parts_made, v_kept = sem("a_hi_made"), sem("a_parts_made"), sem("a_v_kept")
        qk_stored = [sem("a_qk_stored0"), sem("a_qk_stored1")]
        v_stored = sem("a_v_stored")
        block = ctx.enter_context(nc.Block())

        @block.tensor
        def _(pe):
            def transpose_tile(t):
                if t >= 2:
                    pe.wait_ge(copied, t - 1)
                nc.tensor.transpose(tr_ps[t % 2][0:D, 0:P], h[:, t, :], c.ident[:, :]).then_inc(transposed, 1)

            transpose_tile(0)
            for t in range(T):
                if t + 1 < T:
                    transpose_tile(t + 1)
                pe.wait_ge(copied, t + 1)
                if t >= 1:
                    pe.wait_ge(parts_made, 2 * t)
                for ps, w, made in ((q_ps, w_rep[0], q_made), (k_ps, w_rep[1], k_made)):
                    for hd in range(HEADS):
                        mm = nc.tensor.matmul(ps[0:D, hd * P:(hd + 1) * P], w[:, hd, :, :].rearrange("p j f -> p (j f)"),
                                              hT[:, t % 2, :], start=True, stop=True)
                    mm.then_inc(made, 1)
                if t >= 1:
                    pe.wait_ge(v_kept, t)
                nc.tensor.matmul(v_ps[:, 0:D], hT[:, t % 2, :], w_in[2][:, :], start=True, stop=True).then_inc(v_made, 1)

        @block.scalar
        def _(act):
            for t in range(T):
                act.wait_ge(transposed, t + 1)
                if t >= 2:
                    act.wait_ge(v_made, t - 1)
                nc.scalar.activation(hT[:, t % 2, :], tr_ps[t % 2][0:D, 0:P], ACT.Copy).then_inc(copied, 1)
                for j, (ps, made) in enumerate(((q_ps, q_made), (k_ps, k_made))):
                    act.wait_ge(made, t + 1)
                    if t >= 1:
                        act.wait_ge(parts_made, 2 * t - 1 + j)
                    nc.scalar.activation(hi[:, j, :], ps[0:D, :], ACT.Copy).then_inc(hi_made, 1)

        @block.vector
        def _(dve):
            for t in range(T):
                for j, (ps, st) in enumerate(((q_ps, q_st), (k_ps, k_st))):
                    dve.wait_ge(hi_made, 2 * t + j + 1)
                    if j == 0 and t >= 2:
                        dve.wait_ge(qk_stored[t % 2], 32 * (t // 2))
                    nc.vector.scalar_tensor_tensor(st[:, t % 2, :], hi[:, j, :], neg_lo[:, j:j + 1], ps[0:D, :],
                                                   ALU.mult, ALU.add).then_inc(parts_made, 1)
                dve.wait_ge(v_made, t + 1)
                nc.vector.tensor_copy(v_all[:, t, :, 0:DH], v_ps[:, 0:D].rearrange("p (h f) -> p h f", h=HEADS)).then_inc(v_kept, 1)

        @block.sync
        def _(sp):
            for t in range(T):
                sp.wait_ge(parts_made, 2 * t + 2)
                sp.dma_start(q_dram[:, t, :], q_st[:, t % 2, :]).then_inc(qk_stored[t % 2], 16)
                sp.dma_start(k_dram[:, t, :], k_st[:, t % 2, :]).then_inc(qk_stored[t % 2], 16)
            sp.wait_ge(v_kept, T)
            sp.dma_start(v_dram, v_all[:, :, :, :].rearrange("p t h f -> p (t h f)")).then_inc(v_stored, 16)
            sp.wait_ge(v_stored, 16)
            sp.wait_ge(qk_stored[0], 32 * ((T + 1) // 2))
            sp.wait_ge(qk_stored[1], 32 * (T // 2))


def edge_lists(nc, c, src, dst, weight, src_pad, dst_pad, dst_ext, w_pad, src_cols, dst_cols, w_cols, same_dram, win_dram, first_row):
    npad = EP + P - E
    quarter = CHUNKS // 4
    with stack() as ctx:
        sb = lambda name, shape, dt: ctx.enter_context(nc.sbuf_tensor(name, shape, dt))
        zero_i, far, before = sb("zero_i", [1, EXT - E], I32), sb("far", [1, EXT - E], I32), sb("before", [1, 1], I32)
        zero_f = zero_i[:, :].bitcast(F32)
        src_i, dst_i, before_i = (sb(n, [quarter, 4, P], I32) for n in ("src_c", "dst_c", "before_c"))
        same = sb("same_c", [quarter, 4, P], F16)
        src_f, dst_f, w_f = (sb(n, [quarter, 4, P], F32) for n in ("src_cf", "dst_cf", "w_cf"))
        src_t, dst_t, w_t = sb("src_t", [P, CHUNKS], I32), sb("dst_t", [P, CHUNKS], I32), sb("w_t", [P, CHUNKS], F32)
        rows_ps = [ctx.enter_context(nc.psum_tensor(f"rows_ps{i}", [P, 512], F32)) for i in range(3)]
        sem = lambda name: ctx.enter_context(nc.semaphore(name))
        pads, padded, rows_loaded, rows_cast, turned = sem("pads"), sem("padded"), sem("rows_loaded"), sem("rows_cast"), sem("turned")
        windowed, same_made, rows_stored = sem("windowed"), sem("same_made"), sem("rows_stored")
        block = ctx.enter_context(nc.Block())
        flat = lambda a: a.rearrange("(a e) -> a e", a=1)
        src_flat = src_pad.rearrange("c p -> (c p)")
        dst_flat = dst_pad.rearrange("c p -> (c p)")

        @block.vector
        def _(dve):
            nc.vector.memset(zero_i[:, :], 0)
            nc.vector.memset(far[:, :], PAD_DST)
            nc.vector.memset(before[:, :], -1).then_inc(pads, 1)
            dve.wait_ge(rows_loaded, 64)
            nc.vector.tensor_copy(src_f[:, :, :], src_i[:, :, :]).then_inc(rows_cast, 1)
            nc.vector.tensor_copy(dst_f[:, :, :], dst_i[:, :, :]).then_inc(rows_cast, 1)
            nc.vector.tensor_tensor(same[:, :, :], dst_i[:, :, :], before_i[:, :, :], ALU.is_equal).then_inc(same_made, 1)
            dve.wait_ge(turned, 12)
            nc.vector.tensor_copy(src_t[:, :], rows_ps[0][:, 0:CHUNKS]).then_inc(rows_cast, 1)
            for j in range(PHASES):
                nc.vector.tensor_copy(first_row[:, j, :], rows_ps[1][j * P // PHASES:j * P // PHASES + 1, 0:CHUNKS])
            nc.vector.tensor_scalar(dst_t[:, :], rows_ps[1][:, 0:CHUNKS], float(NP - 1), None, ALU.min).then_inc(rows_cast, 1)
            nc.vector.tensor_copy(w_t[:, :], rows_ps[2][:, 0:CHUNKS]).then_inc(rows_cast, 1)

        @block.sync
        def _(sp):
            sp.dma_start(flat(src_flat[0:E]), flat(src)).then_inc(padded, 16)
            sp.dma_start(flat(dst_flat[0:E]), flat(dst)).then_inc(padded, 16)
            sp.dma_start(flat(dst_ext[1:1 + E]), flat(dst)).then_inc(padded, 16)
            sp.dma_start(flat(w_pad[0:E]), flat(weight)).then_inc(padded, 16)
            sp.wait_ge(pads, 1)
            sp.dma_start(flat(src_flat[E:EP + P]), zero_i[:, 0:npad]).then_inc(padded, 16)
            sp.dma_start(flat(dst_flat[E:EP + P]), far[:, 0:npad]).then_inc(padded, 16)
            sp.dma_start(flat(dst_ext[1 + E:1 + EXT]), far[:, :]).then_inc(padded, 16)
            sp.dma_start(flat(dst_ext[0:1]), before[:, :]).then_inc(padded, 16)
            sp.dma_start(flat(w_pad[E:EXT]), zero_f).then_inc(padded, 16)
            sp.wait_ge(padded, 9 * 16)
            chunks = lambda a: a.rearrange("(a q) p -> q a p", q=quarter)
            sp.dma_start(src_i[:, :, :], chunks(src_pad[0:CHUNKS, :])).then_inc(rows_loaded, 16)
            sp.dma_start(dst_i[:, :, :], chunks(dst_pad[0:CHUNKS, :])).then_inc(rows_loaded, 16)
            sp.dma_start(w_f[:, :, :], chunks(w_pad[0:EP].rearrange("(c p) -> c p", p=P))).then_inc(rows_loaded, 16)
            sp.dma_start(before_i[:, :, :], chunks(dst_ext[0:EP].rearrange("(c p) -> c p", p=P))).then_inc(rows_loaded, 16)
            sp.dma_start(flat(same_dram[EP:EXT]), zero_i[:, 0:(EXT - EP) // 2].bitcast(F16)).then_inc(rows_stored, 16)
            sp.wait_ge(same_made, 1)
            sp.dma_start(chunks(same_dram[0:EP].rearrange("(c p) -> c p", p=P)), same[:, :, :]).then_inc(rows_stored, 16)
            sp.wait_ge(rows_cast, 5)
            sp.dma_start(src_cols, src_t[:, :]).then_inc(rows_stored, 16)
            sp.dma_start(dst_cols, dst_t[:, :]).then_inc(rows_stored, 16)
            sp.dma_start(w_cols, w_t[:, :]).then_inc(rows_stored, 16)
            sp.wait_ge(rows_stored, 80)

        @block.scalar
        def _(act):
            act.wait_ge(padded, 9 * 16)
            by_phase = win_dram.rearrange("(c j) l p -> j l c p", j=PHASES)
            for n, edges in enumerate((src_flat, dst_flat, w_pad.bitcast(I32))):
                for j in range(PHASES):
                    begin = j * P // PHASES
                    act.dma_start(by_phase[j, n, :, :], edges[begin:begin + EP].rearrange("(c p) -> c p", p=P)).then_inc(windowed, 16)
            act.wait_ge(windowed, 16 * 3 * PHASES)

        @block.tensor
        def _(pe):
            pe.wait_ge(rows_cast, 2)
            for rows, ps in zip((src_f, dst_f, w_f), rows_ps):
                for a in range(4):
                    nc.tensor.transpose(ps[:, a * quarter:(a + 1) * quarter], rows[:, a, :],
                                        c.ident[0:quarter, 0:quarter]).then_inc(turned, 1)


def adjacency_windows(nc, c, win_dram, first_row, tables, tables_dram, overflow):
    with stack() as ctx:
        sb = lambda name, shape, dt: ctx.enter_context(nc.sbuf_tensor("win_" + name, shape, dt))
        o_i, o_f = sb("o_i", [P, GT], I32), sb("o_f", [P, GT], F32)
        low, high = sb("low", [P, GT], F32), sb("high", [P, GT], F32)
        begin, end, over = sb("begin", [P, GT], F32), sb("end", [P, GT], F32), sb("over", [P, GT], F32)
        any_over = sb("any_over", [P, 1], F32)
        offset, below = sb("offset", [P, GT], F32), sb("below", [P, PHASES, CHUNKS], F16)
        row_f, row_i = sb("row_f", [P, GT, WIN], F32), sb("row_i", [P, GT, WIN], I32)
        edges = sb("edges", [P, GT, WIN, 3, P], I32)
        shape = [P, GT, WIN, P]
        int_part, tile_f = sb("int_part", shape, I32), sb("tile_f", shape, F32)
        lane_f, key_f = sb("lane_f", shape, F32), sb("key_f", shape, F32)
        weight16 = sb("weight16", [P, NSTEP], F16)
        first_ps = ctx.enter_context(nc.psum_tensor("win_first_ps", [P, PHASES, 512], F32))
        over_ps = ctx.enter_context(nc.psum_tensor("win_over_ps", [P, 512], F32))
        more_ps = [ctx.enter_context(nc.psum_tensor(f"win_more_ps{u}", [P, 512], F32)) for u in range(2)]
        turned_ps = [first_ps[:, n, :] for n in range(4)] + [ps[:, :] for ps in more_ps]
        sem = lambda name: ctx.enter_context(nc.semaphore("win_" + name))
        numbered, first_ready, d_step, over_kept, over_summed, row_ready, lanes_ready, keys_ready, turned, tables_kept, tables_stored = (
            sem("numbered"), sem("first_ready"), sem("step"), sem("over_kept"), sem("over_summed"), sem("row_ready"),
            sem("lanes_ready"), sem("keys_ready"), sem("turned"), sem("tables_kept"), sem("tables_stored"))
        gathered = c.gather_sem("win_gathered")
        block = ctx.enter_context(nc.Block())

        @block.gpsimd
        def _(pool):
            nc.gpsimd.iota(o_i[:, :], [[P, GT]], base=0, channel_multiplier=1).then_inc(numbered, 1)
            pool.wait_ge(row_ready, 1)
            for u in range(GT):
                for w in range(WIN):
                    nc.gpsimd.indirect_dma_start(edges[:, u, w, :, :].rearrange("p l e -> p (l e)"), None, win_dram.rearrange("r l p -> r (l p)"),
                                                 bass.IndirectOffsetOnAxis(ap=row_i[:, u, w:w + 1], axis=0)).then_inc(gathered, 16)
            pool.wait_ge(gathered, 16 * GT * WIN)

        @block.sync
        def _(sp):
            sp.wait_ge(tables_kept, 1)
            sp.dma_start(tables_dram, tables[:, :, :]).then_inc(tables_stored, 16)
            sp.wait_ge(tables_stored, 16)

        @block.vector
        def _(dve):
            done = [0]

            def then_wait(*ins):
                for i in ins:
                    done[0] += 1
                    i.then_inc(d_step, 1)
                dve.wait_ge(d_step, done[0])

            dve.wait_ge(numbered, 1)
            then_wait(nc.vector.tensor_copy(o_f[:, :], o_i[:, :]))
            then_wait(nc.vector.tensor_scalar(high[:, :], o_f[:, :], float(GROUP), float(GROUP), ALU.mult, ALU.add),
                      nc.vector.tensor_scalar(offset[:, :], o_f[:, :], float(-KEYS), None, ALU.mult),
                      nc.vector.tensor_scalar(low[:, :], o_f[:, :], float(GROUP), None, ALU.mult))
            then_wait(nc.vector.tensor_scalar(high[:, :], high[:, :], float(NP), None, ALU.min))
            dve.wait_ge(first_ready, 1)
            for limit, row in ((low, begin), (high, end)):
                for u in range(GT):
                    then_wait(nc.vector.tensor_scalar(below[:, :, :], first_ps[:, :, 0:CHUNKS], limit[:, u:u + 1], None, ALU.is_lt, ALU.add,
                                                      accum_out=row[:, u:u + 1]))
                then_wait(nc.vector.tensor_scalar(row[:, :], row[:, :], -1.0, 0.0, ALU.add, ALU.max))
            then_wait(*[nc.vector.tensor_scalar(row_f[:, :, w], begin[:, :], float(PHASES * w), float(WROWS - 1), ALU.add, ALU.min)
                        for w in range(WIN)])
            nc.vector.tensor_copy(row_i[:, :, :], row_f[:, :, :]).then_inc(row_ready, 1)
            then_wait(nc.vector.tensor_tensor(over[:, :], end[:, :], begin[:, :], ALU.subtract))
            then_wait(nc.vector.tensor_scalar(over[:, :], over[:, :], float(PHASES * WIN), None, ALU.is_ge))
            nc.vector.tensor_reduce(any_over[:, :], over[:, :], AX.X, ALU.add).then_inc(over_kept, 1)
            dve.wait_ge(over_summed, 1)
            nc.vector.tensor_copy(overflow[:, :], over_ps[0:1, 0:1])
            dve.wait_ge(gathered, 16 * GT * WIN)
            then_wait(nc.vector.tensor_scalar(int_part[:, :, :, :], edges[:, :, :, 0, :], P - 1, None, ALU.bitwise_and))
            then_wait(nc.vector.tensor_copy(lane_f[:, :, :, :], int_part[:, :, :, :]))
            dve.sem_inc(lanes_ready, 1)
            then_wait(nc.vector.tensor_scalar(int_part[:, :, :, :], edges[:, :, :, 0, :], 7, None, ALU.logical_shift_right))
            then_wait(nc.vector.tensor_copy(tile_f[:, :, :, :], int_part[:, :, :, :]),
                      nc.vector.tensor_copy(key_f[:, :, :, :], edges[:, :, :, 1, :]))
            for u in range(GT):
                then_wait(nc.vector.scalar_tensor_tensor(key_f[:, u, :, :], key_f[:, u, :, :], float(T), tile_f[:, u, :, :], ALU.mult, ALU.add))
                nc.vector.tensor_scalar(key_f[:, u, :, :], key_f[:, u, :, :], offset[:, u:u + 1], None, ALU.add).then_inc(keys_ready, 1)

            def keep(u, n, ps, table, scale):
                g = min(P, NGROUP - u * P)
                out = tables[:, table, u * P * WIN:(u * P + g) * WIN].rearrange("p (o w) -> p w o", w=WIN)
                return nc.vector.tensor_scalar(out, ps[:, 0:WIN * P].rearrange("p (w o) -> p w o", w=WIN)[:, :, 0:g], scale, None, ALU.mult)

            dve.wait_ge(turned, 3 * GT * WIN)
            then_wait(*[keep(u, n, turned_ps[n * GT + u], table, scale)
                        for n, (table, scale) in enumerate(((1, 1.0), (0, 1.0), (3, W_SCALE))) for u in range(GT)])
            then_wait(nc.vector.tensor_copy(weight16[:, :], tables[:, 3, :]))
            then_wait(nc.vector.tensor_copy(tables[:, 2, :], weight16[:, :]))
            then_wait(nc.vector.tensor_tensor(tables[:, 3, :], tables[:, 3, :], tables[:, 2, :], ALU.subtract))
            dve.sem_inc(tables_kept, 1)

        @block.tensor
        def _(pe):
            for j in range(PHASES):
                mm = nc.tensor.matmul(first_ps[:, j, 0:CHUNKS], c.ones[0:1, :], first_row[:, j, :], start=True, stop=True)
            mm.then_inc(first_ready, 1)
            pe.wait_ge(over_kept, 1)
            nc.tensor.matmul(over_ps[:, 0:1], c.ones[:, :], any_over[:, :], start=True, stop=True).then_inc(over_summed, 1)
            weight_f = edges[:, :, :, 2, :].bitcast(F32)
            for n, (table, ready, count) in enumerate(((lane_f, lanes_ready, 1), (key_f, keys_ready, GT), (weight_f, keys_ready, GT))):
                pe.wait_ge(ready, count)
                for u in range(GT):
                    for w in range(WIN):
                        nc.tensor.transpose(turned_ps[n * GT + u][:, w * P:(w + 1) * P], table[:, u, w, :], c.ident[:, :]).then_inc(turned, 1)


def build_adjacency(nc, c, adj, tables):
    TURN = 4
    with stack() as ctx:
        sb = lambda name, shape, dt: ctx.enter_context(nc.sbuf_tensor(name, shape, dt))
        lane_hot, key_hot = sb("lane_hot", [P, 2, WIN, P], F16), sb("key_hot", [P, 2, WIN, KEYS], F16)
        count_ps = [ctx.enter_context(nc.psum_tensor(f"count{i}", [P, 512], F32)) for i in range(2)]
        sem = lambda name: ctx.enter_context(nc.semaphore(name))
        hot_ready, counted, kept = sem("hot_ready"), sem("adj_counted"), sem("adj_kept")
        block = ctx.enter_context(nc.Block())

        @block.vector
        def _(dve):
            with dve.Fori(0, NGROUP // TURN) as i:
                for b in range(TURN):
                    dve.wait_ge(counted, TURN * i + b + 1)
                    for w in range(WIN):
                        at = bass.ds(TURN * WIN * i + WIN * b + w, 1)
                        nc.vector.tensor_scalar(lane_hot[:, b % 2, w, :], c.iota16[:, 0:P], tables[:, 1, at], None, ALU.is_equal)
                        nc.vector.tensor_scalar(key_hot[:, b % 2, w, :], c.iota16[:, :], tables[:, 0, at], None, ALU.is_equal).then_inc(hot_ready, 1)

        @block.tensor
        def _(pe):
            pe.sem_inc(counted, 2)
            with pe.Fori(0, NGROUP // TURN) as i:
                for b in range(TURN):
                    pe.wait_ge(kept, TURN * i + b + 1)
                    for w in range(WIN):
                        pe.wait_ge(hot_ready, TURN * WIN * i + WIN * b + w + 1)
                        mm = nc.tensor.matmul(count_ps[b % 2][:, 0:KEYS], lane_hot[:, b % 2, w, :], key_hot[:, b % 2, w, :], start=w == 0, stop=w == WIN - 1)
                    mm.then_inc(counted, 1)

        @block.scalar
        def _(act):
            act.sem_inc(kept, 2)
            with act.Fori(0, NGROUP // TURN) as i:
                for b in range(TURN):
                    act.wait_ge(counted, TURN * i + b + 3)
                    nc.scalar.activation(adj[:, :, bass.ds(TURN * GROUP * i + GROUP * b, GROUP)],
                                         count_ps[b % 2][:, 0:KEYS].rearrange("p (d k) -> p k d", d=GROUP), ACT.Copy).then_inc(kept, 1)


def walk_adjacency(nc, c, adj, overflow, src_pad, dst_pad, group_dram):
    pairs = (STEPS - 1) // 2
    assert STEPS == 2 * pairs + 1
    half = T // 2
    with stack() as ctx:
        sb = lambda name, shape, dt: ctx.enter_context(nc.sbuf_tensor("walk_" + name, shape, dt))
        key_of, lane_of, group_row = sb("key_of", [P, SPAD], F32), sb("lane_of", [P, SPAD], F32), sb("group_row", [1, SPAD], I32)
        lane_hot = [sb(f"lane_hot{i}", [P, P], F16) for i in range(2)]
        key_hot = [sb(f"key_hot{i}", [P, KEYS], F16) for i in range(2)]
        dst_i, dst_f = sb("dst_i", [P, CHUNKS], I32), sb("dst_f", [P, CHUNKS], F32)
        below = sb("below", [P, CHUNKS], F32)
        o_i, o_f, limit = sb("o_i", [P, NGROUP], I32), sb("o_f", [P, NGROUP], F32), sb("limit", [P, NGROUP], F32)
        count = sb("count", [P, NGROUP], F32)
        first_i, first = sb("first_i", [P, NGROUP], I32), sb("first", [P, NGROUP], F32)
        s_i, s_f = sb("s_i", [P, STILES], I32), sb("s_f", [P, STILES], F32)
        group, offset = sb("group", [P, STILES], F32), sb("offset", [P, STILES], F32)
        chunk_f, chunk_i = sb("chunk_f", [P, STILES], F32), sb("chunk_i", [P, STILES], I32)
        src_g, dst_g = sb("src_g", [P, STILES, P], I32), sb("dst_g", [P, STILES, P], I32)
        tile_i, tile_f = sb("tile_i", [P, STILES, P], I32), sb("tile_f", [P, STILES, P], F32)
        lane_i, lane_f = sb("lane_i", [P, STILES, P], I32), sb("lane_f", [P, STILES, P], F32)
        key_f = sb("key_f", [P, STILES, P], F32)
        group_i = sb("group_i", [STILES, P], I32)
        ps = [ctx.enter_context(nc.psum_tensor(f"walk_ps{i}", [P, 512], F32)) for i in range(6)]
        part_ps = [ctx.enter_context(nc.psum_tensor(f"walk_part{i}", [P, 512], F32)) for i in range(2)]
        sem = lambda name: ctx.enter_context(nc.semaphore("walk_" + name))
        loaded, numbered, d_step, counted, summed, chunk_ready, keyed, turned, o_turned, o_cast, o_stored = (
            sem("loaded"), sem("numbered"), sem("step"), sem("counted"), sem("summed"), sem("chunk"), sem("keyed"),
            sem("turned"), sem("oturned"), sem("ocast"), sem("ostored"))
        zeroed, hot_ready, part_ready, added = sem("zeroed"), sem("hot_ready"), sem("part_ready"), sem("added")
        gathered = c.gather_sem("walk_gathered")
        block = ctx.enter_context(nc.Block())
        taken = lambda eng: eng.value_load(overflow[0:1, 0:1], min_val=0, max_val=NP) > 0

        @block.sync
        def _(sp):
            with sp.If(taken(sp)):
                sp.dma_start(dst_i[:, :], dst_pad[0:CHUNKS, :].rearrange("c p -> (c p)").rearrange("(p c) -> p c", p=P)).then_inc(loaded, 16)
                sp.wait_ge(o_cast, 1)
                sp.dma_start(group_dram.rearrange("(t p) -> t p", p=P), group_i[:, :]).then_inc(o_stored, 16)
                sp.wait_ge(o_stored, 16)
                sp.dma_start(group_row[:, :], group_dram.rearrange("(a s) -> a s", a=1)).then_inc(o_stored, 16)
                sp.wait_ge(o_stored, 32)

        @block.gpsimd
        def _(pool):
            with pool.If(taken(pool)):
                nc.gpsimd.memset(adj[:, 0:half, :], 0.0).then_inc(zeroed, 1)
                nc.gpsimd.iota(o_i[:, :], [[1, NGROUP]], base=0, channel_multiplier=0).then_inc(numbered, 1)
                nc.gpsimd.iota(s_i[:, :], [[P, STILES]], base=0, channel_multiplier=1).then_inc(numbered, 1)
                pool.wait_ge(chunk_ready, 1)
                for t in range(STILES):
                    at = bass.IndirectOffsetOnAxis(ap=chunk_i[:, t:t + 1], axis=0)
                    nc.gpsimd.indirect_dma_start(src_g[:, t, :], None, src_pad, at).then_inc(gathered, 16)
                    nc.gpsimd.indirect_dma_start(dst_g[:, t, :], None, dst_pad, at).then_inc(gathered, 16)
                pool.wait_ge(gathered, 32 * STILES)

        @block.vector
        def _(dve):
            done = [0]

            def then_wait(ins):
                done[0] += 1
                ins.then_inc(d_step, 1)
                dve.wait_ge(d_step, done[0])

            def schedule():
                dve.wait_ge(numbered, 2)
                nc.vector.tensor_copy(s_f[:, :], s_i[:, :])
                then_wait(nc.vector.tensor_copy(o_f[:, :], o_i[:, :]))
                then_wait(nc.vector.tensor_scalar(limit[:, :], o_f[:, :], float(GROUP), None, ALU.mult))
                dve.wait_ge(loaded, 16)
                then_wait(nc.vector.tensor_copy(dst_f[:, :], dst_i[:, :]))
                with dve.Fori(0, NGROUP) as o:
                    nc.vector.tensor_scalar(below[:, :], dst_f[:, :], limit[:, bass.ds(o, 1)], None, ALU.is_lt, ALU.add,
                                            accum_out=count[:, bass.ds(o, 1)]).then_inc(counted, 1)
                    dve.wait_ge(counted, o + 1)
                dve.wait_ge(summed, 1)
                then_wait(nc.vector.tensor_copy(first_i[:, :], ps[0][:, 0:NGROUP]))
                then_wait(nc.vector.tensor_scalar(first_i[:, :], first_i[:, :], 7, None, ALU.logical_shift_right))
                then_wait(nc.vector.tensor_copy(first[:, :], first_i[:, :]))
                then_wait(nc.vector.tensor_tensor(first[:, :], first[:, :], o_f[:, :], ALU.add))
                for t in range(STILES):
                    then_wait(nc.vector.tensor_scalar(below[:, 1:NGROUP], first[:, 1:NGROUP], s_f[:, t:t + 1], None, ALU.is_le, ALU.add,
                                                      accum_out=group[:, t:t + 1]))
                then_wait(nc.vector.tensor_tensor(chunk_f[:, :], s_f[:, :], group[:, :], ALU.subtract))
                then_wait(nc.vector.tensor_scalar(chunk_f[:, :], chunk_f[:, :], float(CHUNKS - 1), None, ALU.min))
                then_wait(nc.vector.tensor_copy(chunk_i[:, :], chunk_f[:, :]))
                dve.sem_inc(chunk_ready, 1)
                then_wait(nc.vector.tensor_scalar(offset[:, :], group[:, :], float(-KEYS), None, ALU.mult))
                then_wait(nc.vector.tensor_scalar(group[:, :], group[:, :], float(GROUP), None, ALU.mult))
                nc.vector.tensor_copy(chunk_f[:, :], group[:, :]).then_inc(keyed, 1)
                dve.wait_ge(o_turned, 1)
                nc.vector.tensor_copy(group_i[:, :], ps[1][0:STILES, 0:P]).then_inc(o_cast, 1)
                dve.wait_ge(gathered, 32 * STILES)
                nc.vector.tensor_scalar(tile_i[:, :, :], src_g[:, :, :], 7, None, ALU.logical_shift_right)
                then_wait(nc.vector.tensor_scalar(lane_i[:, :, :], src_g[:, :, :], P - 1, None, ALU.bitwise_and))
                nc.vector.tensor_copy(lane_f[:, :, :], lane_i[:, :, :])
                nc.vector.tensor_copy(tile_f[:, :, :], tile_i[:, :, :])
                then_wait(nc.vector.tensor_copy(key_f[:, :, :], dst_g[:, :, :]))
                for t in range(STILES):
                    then_wait(nc.vector.scalar_tensor_tensor(key_f[:, t, :], key_f[:, t, :], float(T), tile_f[:, t, :], ALU.mult, ALU.add))
                    nc.vector.tensor_scalar(key_f[:, t, :], key_f[:, t, :], offset[:, t:t + 1], None, ALU.add).then_inc(keyed, 1)
                dve.wait_ge(turned, 2 * STILES)
                for t in range(STILES):
                    bank = 2 + (t // 4) * 2
                    nc.vector.tensor_copy(lane_of[:, t * P:(t + 1) * P], ps[bank + 1][:, (t % 4) * P:(t % 4 + 1) * P])
                    then_wait(nc.vector.tensor_copy(key_of[:, t * P:(t + 1) * P], ps[bank][:, (t % 4) * P:(t % 4 + 1) * P]))
                dve.wait_ge(o_stored, 32)

            def one_hot(s, b, first):
                if not first:
                    dve.wait_ge(part_ready, s - 1)
                nc.vector.tensor_scalar(lane_hot[b][:, :], c.iota16[:, 0:P], lane_of[:, bass.ds(s, 1)], None, ALU.is_equal)
                nc.vector.tensor_scalar(key_hot[b][:, :], c.iota16[:, :], key_of[:, bass.ds(s, 1)], None, ALU.is_equal).then_inc(hot_ready, 1)

            def add(s, b, first=False):
                g = nc.values_load(group_row[0:1, bass.ds(s, 1)], engines=(mybir.EngineType.DVE,), min_val=0, max_val=NP - GROUP,
                                   skip_runtime_bounds_check_because="a step's group is below NGROUP")
                columns = adj[:, :, bass.ds(g, GROUP)]
                dve.wait_ge(part_ready, s + 1)
                if not first:
                    dve.wait_ge(added, s)
                nc.vector.tensor_tensor(columns, columns, part_ps[b][:, 0:KEYS].rearrange("p (d k) -> p k d", d=GROUP),
                                        ALU.add).then_inc(added, 1)

            with dve.If(taken(dve)):
                nc.vector.memset(adj[:, half:T, :], 0.0).then_inc(zeroed, 1)
                schedule()
                dve.wait_ge(zeroed, 2)
                one_hot(0, 0, True)
                one_hot(1, 1, True)
                add(0, 0, True)
                one_hot(2, 0, False)
                add(1, 1)
                with dve.Fori(1, pairs) as i:
                    one_hot(2 * i + 1, 1, False)
                    add(2 * i, 0)
                    one_hot(2 * i + 2, 0, False)
                    add(2 * i + 1, 1)
                add(STEPS - 1, 0)

        @block.tensor
        def _(pe):
            def product(s, b, first):
                pe.wait_ge(hot_ready, s + 1)
                if not first:
                    pe.wait_ge(added, s - 1)
                nc.tensor.matmul(part_ps[b][:, 0:KEYS], lane_hot[b][:, :], key_hot[b][:, :],
                                 start=True, stop=True).then_inc(part_ready, 1)

            with pe.If(taken(pe)):
                pe.wait_ge(counted, NGROUP)
                nc.tensor.matmul(ps[0][:, 0:NGROUP], c.ones[:, :], count[:, :], start=True, stop=True).then_inc(summed, 1)
                pe.wait_ge(keyed, 1)
                nc.tensor.transpose(ps[1][0:STILES, 0:P], chunk_f[:, :], c.ident[:, :]).then_inc(o_turned, 1)
                for t in range(STILES):
                    pe.wait_ge(keyed, t + 2)
                    bank = 2 + (t // 4) * 2
                    nc.tensor.transpose(ps[bank][:, (t % 4) * P:(t % 4 + 1) * P], key_f[:, t, :], c.ident[:, :]).then_inc(turned, 1)
                    nc.tensor.transpose(ps[bank + 1][:, (t % 4) * P:(t % 4 + 1) * P], lane_f[:, t, :], c.ident[:, :]).then_inc(turned, 1)
                product(0, 0, True)
                product(1, 1, True)
                with pe.Fori(1, pairs) as i:
                    product(2 * i, 0, False)
                    product(2 * i + 1, 1, False)
                product(STEPS - 1, 0, False)


def degrees(nc, c, adj):
    with stack() as ctx:
        sb = lambda name, shape, dt: ctx.enter_context(nc.sbuf_tensor(name, shape, dt))
        upper = sb("upper", [P, P], F32)
        total, before, last, has = sb("total", [P, T], F32), sb("before_t", [P, T], F32), sb("last", [P, T], F32), sb("has", [P, T], F32)
        deg_ps = ctx.enter_context(nc.psum_tensor("deg_ps", [P, 512], F32))
        cum_ps = ctx.enter_context(nc.psum_tensor("cum_ps", [P, 512], F32))
        tot_ps = ctx.enter_context(nc.psum_tensor("tot_ps", [P, 512], F32))
        sem = lambda name: ctx.enter_context(nc.semaphore(name))
        deg_ready, deg_kept, cum_ready, d_step = sem("deg_ready"), sem("deg_kept"), sem("cum_ready"), sem("deg_step")
        upper_made = sem("upper_made")
        block = ctx.enter_context(nc.Block())

        @block.gpsimd
        def _(pool):
            nc.gpsimd.affine_select(out=upper[:, :], in_=c.ones[:, :], compare_op=ALU.is_ge, fill=0.0,
                                    base=0, pattern=[[1, P]], channel_multiplier=-1).then_inc(upper_made, 1)

        @block.tensor
        def _(pe):
            for t in range(T):
                for k in range(T):
                    mm = nc.tensor.matmul(deg_ps[:, t:t + 1], adj[:, k, t * P:(t + 1) * P], c.ones16[:, :], start=k == 0, stop=k == T - 1)
            mm.then_inc(deg_ready, 1)
            pe.wait_ge(deg_kept, 1)
            pe.wait_ge(upper_made, 1)
            nc.tensor.matmul(cum_ps[:, 0:T], upper[:, :], c.deg[:, :], start=True, stop=True).then_inc(cum_ready, 1)
            nc.tensor.matmul(tot_ps[:, 0:T], c.ones[:, :], c.deg[:, :], start=True, stop=True).then_inc(cum_ready, 1)

        @block.vector
        def _(dve):
            done = [0]

            def then_wait(ins):
                done[0] += 1
                ins.then_inc(d_step, 1)
                dve.wait_ge(d_step, done[0])

            dve.wait_ge(deg_ready, 1)
            nc.vector.tensor_copy(c.deg[:, :], deg_ps[:, 0:T]).then_inc(deg_kept, 1)
            dve.wait_ge(cum_ready, 2)
            then_wait(nc.vector.tensor_copy(total[:, :], tot_ps[:, 0:T]))
            then_wait(nc.vector.tensor_tensor_scan(before[:, :], c.ones[:, 0:T], total[:, :], 0.0, ALU.mult, ALU.add))
            then_wait(nc.vector.tensor_tensor(before[:, :], before[:, :], total[:, :], ALU.subtract))
            then_wait(nc.vector.tensor_tensor(last[:, :], before[:, :], cum_ps[:, 0:T], ALU.add))
            nc.vector.tensor_scalar(has[:, :], c.deg[:, :], 0.0, None, ALU.is_gt)
            then_wait(nc.vector.tensor_scalar(last[:, :], last[:, :], float(-1 - ZERO_ROW), None, ALU.add))
            then_wait(nc.vector.tensor_tensor(last[:, :], last[:, :], has[:, :], ALU.mult))
            then_wait(nc.vector.tensor_scalar(last[:, :], last[:, :], float(ZERO_ROW), None, ALU.add))
            nc.vector.tensor_copy(c.end_row[:, :], last[:, :])


def attention(nc, c, adj, q_dram, k_dram, v_dram, res_dram):
    RINGS, E_RINGS = 3, 5

    def ring(n):
        buf = [t % n for t in range(T)]
        if buf[T - 1] == 0:
            buf[T - 1] = next(b for b in range(1, n) if b not in buf[T + 1 - n:T - 1])
        return buf

    def last_use(buf, t):
        return max(u for u in range(t - T, t) if buf[u % T] == buf[t])

    buf, e_buf = ring(RINGS), ring(E_RINGS)
    GIVEN = 6
    with stack() as ctx:
        sb = lambda name, shape, dt: ctx.enter_context(nc.sbuf_tensor(name, shape, dt))
        k_st = sb("k_all", [D, T, 512], F16)
        v_all = sb("v_all2", [P, T, HEADS, DH + 1], F32)
        q_st = sb("q_tile", [D, 2, 512], F16)
        e = sb("e", [P, E_RINGS, 512], F32)
        o_sb = sb("o_sb", [DH + 1, 512], F32)
        first_exp = sb("first_exp", [P, 1], F32)
        inv = sb("inv", [P, HEADS], F32)
        res = sb("res", [P, HEADS, DH], F32)
        s_ps = [ctx.enter_context(nc.psum_tensor(f"s_ps{i}", [P, 512], F32)) for i in range(RINGS)]
        a_ps = [ctx.enter_context(nc.psum_tensor(f"a_ps{i}", [P, 1024], F16)) for i in range(RINGS)]
        o_ps = ctx.enter_context(nc.psum_tensor("o_ps", [P, 512], F32))
        r_ps = ctx.enter_context(nc.psum_tensor("r_ps", [P, 512], F32))
        sem = lambda name: ctx.enter_context(nc.semaphore(name))
        kv_loaded, q_loaded, scored, clipped, exped, weighted, summed, o_kept, o_turned, res_ready, res_stored, d_step, turn_begun = (
            sem("kv_loaded"), sem("q_loaded"), sem("scored"), sem("clipped"), sem("exped"), sem("weighted"), sem("summed"),
            sem("o_kept"), sem("o_turned"), sem("res_ready"), sem("res_stored"), sem("att_step"), sem("turn_begun"))
        block = ctx.enter_context(nc.Block())

        @block.sync
        def _(sp):
            sp.dma_start(k_st[:, :, :], k_dram).then_inc(kv_loaded, 16)
            sp.dma_start(v_all[:, :, :, :].rearrange("p t h f -> p (t h f)"), v_dram).then_inc(kv_loaded, 16)
            sp.dma_start(q_st[:, 0, :], q_dram[:, 0, :]).then_inc(q_loaded, 16)
            with sp.Fori(0, T) as i:
                sp.wait_ge(scored, T * i + GIVEN)
                sp.wait_ge(q_loaded, 16 * (i + 1))
                sp.dma_start(q_st[:, bass.ds((i + 1) % 2, 1), :].rearrange("p a n -> p (a n)"),
                             q_dram[:, bass.ds((i + 1) % T, 1), :].rearrange("p a n -> p (a n)")).then_inc(q_loaded, 16)
                sp.wait_ge(res_ready, i + 1)
                sp.dma_start(res_dram[bass.ds(i * P, P), :], res[:, :, :].rearrange("p h f -> p (h f)")).then_inc(res_stored, 16)
            sp.wait_ge(res_ready, T + 1)
            sp.dma_start(res_dram[T * P:(T + 1) * P, :], res[:, :, :].rearrange("p h f -> p (h f)")).then_inc(res_stored, 16)
            sp.wait_ge(res_stored, 16 * (T + 2))
            sp.wait_ge(q_loaded, 16 * (T + 1))

        @block.gpsimd
        def _(pool):
            pool.sem_inc(res_stored, 16)

        @block.tensor
        def _(pe):
            def score(i, t, given):
                pe.wait_ge(weighted, given + last_use(buf, t) + 1 + GIVEN)
                nc.tensor.transpose(a_ps[buf[t]][:, 0:P], adj[:, bass.ds(i, 1), t * P:(t + 1) * P].rearrange("p a n -> p (a n)"), c.ident16[:, :])
                pe.wait_ge(exped, given + last_use(buf, t) + 1 + GIVEN)
                q = q_st[:, bass.ds(i % 2, 1), :].rearrange("p a n -> p (a n)")
                for hd in range(HEADS):
                    mm = nc.tensor.matmul(s_ps[buf[t]][:, hd * P:(hd + 1) * P], k_st[:, t, hd * P:(hd + 1) * P],
                                          q[:, hd * P:(hd + 1) * P], start=True, stop=True)
                mm.then_inc(scored, 1)

            def value(i, t):
                pe.wait_ge(weighted, T * i + t + 1 + GIVEN)
                if t == 0:
                    pe.wait_ge(o_kept, i + 1)
                for hd in range(HEADS):
                    mm = nc.tensor.matmul(o_ps[0:DH + 1, hd * P:(hd + 1) * P], v_all[:, t, hd, :], e[:, e_buf[t], hd * P:(hd + 1) * P],
                                          start=t == 0 and hd == 0, stop=t == T - 1 and hd == HEADS - 1, skip_group_check=True)
                mm.then_inc(summed, 1)

            def turn_sums():
                pe.sem_inc(turn_begun, 1)
                for hd in range(HEADS):
                    tr = nc.tensor.transpose(r_ps[:, hd * (DH + 1):(hd + 1) * (DH + 1)], o_sb[:, hd * P:(hd + 1) * P], c.ident[0:DH + 1, 0:DH + 1])
                tr.then_inc(o_turned, 1)

            pe.sem_inc(scored, GIVEN)
            pe.wait_ge(kv_loaded, 32)
            for hd in range(HEADS):
                mm = nc.tensor.matmul(o_ps[0:DH + 1, hd * P:(hd + 1) * P], v_all[:, 0, hd, :], c.ident[:, :], start=True, stop=True)
            mm.then_inc(summed, GIVEN)
            pe.wait_ge(q_loaded, 16)
            score(0, 0, 0)
            score(0, 1, 0)
            with pe.Fori(0, T) as i:
                for t in range(T):
                    if t + 2 < T:
                        score(i, t + 2, T * i)
                    else:
                        if t + 2 == T:
                            pe.wait_ge(q_loaded, 16 * (i + 2))
                        score((i + 1) % T, t + 2 - T, T * i + T)
                    value(i, t)
                    if t == 1:
                        pe.wait_ge(o_kept, i + 1)
                        turn_sums()
            pe.wait_ge(o_kept, T + 1)
            turn_sums()

        @block.scalar
        def _(act):
            def exp(t, given):
                act.wait_ge(scored, given + t + 1 + GIVEN)
                act.wait_ge(summed, given + last_use(e_buf, t) + 1 + GIVEN)
                nc.scalar.activation(e[:, e_buf[t], :], s_ps[buf[t]][:, :], ACT.Exp).then_inc(exped, 1)

            nc.scalar.activation(first_exp[:, :], c.ones[:, 0:1], ACT.Exp)
            act.sem_inc(exped, GIVEN)
            with act.Fori(0, T) as i:
                for t in range(T):
                    exp(t, T * i)
                    if t == 1:
                        act.wait_ge(summed, T * i + GIVEN)
                        nc.scalar.activation(o_sb[:, :], o_ps[0:DH + 1, :], ACT.Copy).then_inc(o_kept, 1)
                    if t == 4:
                        act.wait_ge(o_turned, i + 1)
            act.wait_ge(summed, T * T + GIVEN)
            nc.scalar.activation(o_sb[:, :], o_ps[0:DH + 1, :], ACT.Copy).then_inc(o_kept, 1)

        @block.vector
        def _(dve):
            def clip(t, given):
                dve.wait_ge(exped, given + t + 1 + GIVEN)
                nc.vector.tensor_scalar(e[:, e_buf[t], :], e[:, e_buf[t], :], math.exp(10.0), math.exp(-10.0), ALU.min, ALU.max).then_inc(clipped, 1)

            def weight(i, t):
                dve.wait_ge(clipped, T * i + t + 1)
                tile = e[:, e_buf[t], :].rearrange("p (h n) -> p h n", h=HEADS)
                nc.vector.tensor_tensor(tile, tile, a_ps[buf[t]][:, 0:P].unsqueeze(1).to_broadcast([P, HEADS, P]),
                                        ALU.mult).then_inc(weighted, 1)

            def divide(i):
                dve.wait_ge(o_turned, i + 1)
                sums = r_ps[:, 0:HEADS * (DH + 1)].rearrange("p (h f) -> p h f", h=HEADS)
                nc.vector.tensor_scalar(inv[:, :], sums[:, :, DH], 1e-8, None, ALU.add).then_inc(d_step, 1)
                dve.wait_ge(d_step, 2 * i + 1)
                nc.vector.reciprocal(inv[:, :], inv[:, :]).then_inc(d_step, 1)
                dve.wait_ge(d_step, 2 * i + 2)
                dve.wait_ge(res_stored, 16 * (i + 1))
                nc.vector.tensor_tensor(res[:, :, :], sums[:, :, 0:DH], inv[:, :].unsqueeze(2).to_broadcast([P, HEADS, DH]),
                                        ALU.mult).then_inc(res_ready, 1)

            dve.sem_inc(weighted, GIVEN)
            with dve.Fori(0, T) as i:
                for t in range(T):
                    clip(t, T * i)
                    weight(i, t)
                    if t == 3:
                        divide(i)
            divide(T)


QUARTER = 4
HALF = QUARTER * GROUP
PIECES = (7, 6, 6, 6)


def max_pass(nc, c, name, table_dram, src_cols, same_dram, rows_dram, tables_dram, weights_dram, part):
    assert LOOPS == T and RING == QUARTER and HALF * 2 == P and sum(PIECES) == T
    with stack() as ctx:
        sb = lambda n, shape, dt: ctx.enter_context(nc.sbuf_tensor(f"{name}_{n}", shape, dt))
        ps = lambda n: ctx.enter_context(nc.psum_tensor(f"{name}_{n}", [P, 512], F32))
        sem = lambda n: ctx.enter_context(nc.semaphore(f"{name}_{n}"))
        index = [sb(f"index{i}", [P, 8], I32) for i in range(2)]
        row = [sb(f"row{i}", [P, 4, D], F32) for i in range(RING)]
        src_rows = sb("src_rows", [P, CHUNKS], I32)
        same = [sb(f"same{i}", [D, BLK], F16) for i in range(2)]
        run = [sb(f"run{i}", [D, BLK], F32) for i in range(2)]
        out = [sb(f"out{i}", [P, 4, D], F32) for i in range(2)]
        col_ps = [ps(f"col{i}") for i in range(2)]
        back_ps = [ps(f"back{i}") for i in range(2)]
        index_ready = sem("index_ready")
        gathered = [c.gather_sem(f"{name}_gathered{i}") for i in range(RING)]
        listed = [sem(f"listed{i}") for i in range(2)]
        written = [sem(f"written{i}") for i in range(2)]
        turned, scanned, listed_src, back, kept, zero_out, gather_begun = (
            sem("turned"), sem("scanned"), sem("listed_src"), sem("back"), sem("kept"), sem("zero_out"), sem("gather_begun"))
        steps = QUARTER * WIN
        tables = sb("tables", [P, 4, T, steps], F32)
        key_hot = sb("key_hot", [P, WIN, KEYS], F16)
        lane_w = sb("lane_w", [P, WIN, 2, P], F16)
        strip = sb("strip", [P, 2, T, 2, HALF], F16)
        rows_w = sb("rows_w", [P, T, P], F16)
        strip_ps = [ps(f"strip_ps{i}") for i in range(2)]
        piece_ps = [ctx.enter_context(nc.psum_tensor(f"{name}_piece{i}", [P, 1024], F16)) for i in range(2)]
        tables_loaded, hots_ready, hots_used, hi_kept, lo_kept, piece_turned, piece_kept, rows_stored, cleared = (
            sem("tables_loaded"), sem("hots_ready"), sem("hots_used"), sem("hi_kept"), sem("lo_kept"),
            sem("piece_turned"), sem("piece_kept"), sem("rows_stored"), sem("cleared"))
        block = ctx.enter_context(nc.Block())
        first_tile = [sum(PIECES[:n]) for n in range(len(PIECES))]
        strip_at = lambda h, i: strip[:, bass.ds(i % 2, 1), :, h, :].rearrange("p a k d -> p (a k) d")

        @block.gpsimd
        def _(pool):
            pool.wait_ge(listed_src, 16)
            with pool.Fori(0, LOOPS) as i:
                for b in range(RING):
                    if b % 2 == 0:
                        pool.wait_ge(turned, RING * i + b + 2)
                        nc.gpsimd.tensor_copy(index[b // 2][:, :], src_rows[:, bass.ds(4 * RING * i + 4 * b, 8)]).then_inc(index_ready, 1)
                        pool.wait_ge(index_ready, 2 * i + b // 2 + 1)
                        pool.sem_inc(gather_begun, 1)
                    for j in range(4):
                        nc.gpsimd.indirect_dma_start(row[b][:, j, :], None, table_dram,
                                                     bass.IndirectOffsetOnAxis(ap=index[b // 2][:, 4 * (b % 2) + j:4 * (b % 2) + j + 1], axis=0)
                                                     ).then_inc(gathered[b], 16)
            for b in range(RING):
                pool.wait_ge(gathered[b], 64 * LOOPS)

        @block.tensor
        def _(pe):
            def lay_out(i, g):
                pe.wait_ge(lo_kept, QUARTER * i + g + 1)
                for w in range(WIN):
                    s = WIN * g + w
                    pe.wait_ge(hots_ready, steps * i + s + 1)
                    for h in range(2):
                        mm = nc.tensor.matmul(strip_ps[g % 2][:, 0:KEYS], lane_w[:, w, h, :], key_hot[:, w, :],
                                              start=w == 0 and h == 0, stop=w == WIN - 1 and h == 1)
                    mm.then_inc(hots_used, 1)

            def turn(i, q):
                pe.wait_ge(piece_kept, 4 * i + q + 1)
                for k in range(PIECES[q]):
                    tr = nc.tensor.transpose(piece_ps[q % 2][:, k * P:(k + 1) * P],
                                             strip[:, bass.ds((i + 1) % 2, 1), first_tile[q] + k, :, :].rearrange("p a h d -> p (a h d)"), c.ident16[:, :])
                tr.then_inc(piece_turned, 1)

            pe.sem_inc(turned, RING)
            pe.sem_inc(back, 2)
            pe.sem_inc(piece_turned, 4)
            pe.wait_ge(cleared, 1)
            with pe.Fori(0, LOOPS) as i:
                for b in range(RING):
                    n = RING * i + b
                    pe.wait_ge(gathered[b], 64 * (i + 1))
                    pe.wait_ge(scanned, n + 1)
                    for j in range(4):
                        tr = nc.tensor.transpose(col_ps[b % 2][0:D, j * P:(j + 1) * P], row[b][:, j, :], c.ident[:, :])
                    tr.then_inc(turned, 1)
                    lay_out(i, b)
                    if b == 0:
                        pe.wait_ge(lo_kept, QUARTER * i + 2)
                    turn(i, b)
                    pe.wait_ge(scanned, n + 3)
                    pe.wait_ge(kept, n + 1)
                    for j in range(4):
                        tr = nc.tensor.transpose(back_ps[b % 2][:, j * D:(j + 1) * D], run[b % 2][:, j * P:(j + 1) * P], c.ident[0:D, 0:D])
                    tr.then_inc(back, 1)
            pe.wait_ge(lo_kept, QUARTER * T + 2)
            for q in range(4):
                turn(T, q)

        @block.vector
        def _(dve):
            def hots(i, g, given):
                for w in range(WIN):
                    s = WIN * g + w
                    at = lambda n: tables[:, n, bass.ds(i, 1), s]
                    dve.wait_ge(hots_used, given + s + 1)
                    nc.vector.tensor_scalar(key_hot[:, w, :], c.iota16[:, :], at(0), None, ALU.is_equal)
                    for h in range(2):
                        one_hot = nc.vector.tensor_scalar(lane_w[:, w, h, :], c.iota16[:, 0:P], at(1), at(2 + h), ALU.is_equal, ALU.mult)
                    one_hot.then_inc(hots_ready, 1)

            def low_part(i, g):
                dve.wait_ge(hi_kept, QUARTER * i + g + 1)
                d = slice(g * GROUP, (g + 1) * GROUP)
                nc.vector.tensor_tensor(strip_at(1, i)[:, :, d], strip_ps[g % 2][:, 0:KEYS].rearrange("p (d k) -> p k d", d=GROUP),
                                        strip_at(0, i)[:, :, d], ALU.subtract).then_inc(lo_kept, 1)

            dve.sem_inc(lo_kept, 2)
            nc.vector.memset(run[1][:, BLK - 1:BLK], 0.0).then_inc(scanned, 2)
            dve.wait_ge(scanned, 2)
            nc.vector.memset(strip[:, 1, :, :, :], 0.0).then_inc(cleared, 1)
            dve.wait_ge(tables_loaded, 64)
            hots(0, 0, 0)
            with dve.Fori(0, LOOPS) as i:
                for b in range(RING):
                    n = RING * i + b
                    dve.wait_ge(listed[b % 2], 16 * (2 * i + b // 2 + 1))
                    dve.wait_ge(turned, n + RING + 1)
                    dve.wait_ge(back, n + 1)
                    dve.wait_ge(scanned, n + 2)
                    nc.vector.tensor_tensor_scan(run[b % 2][:, :], same[b % 2][:, :], col_ps[b % 2][0:D, :],
                                                 run[1 - b % 2][:, BLK - 1:BLK], ALU.mult, ALU.max).then_inc(scanned, 1)
                    if b + 1 < RING:
                        hots(i, b + 1, steps * i)
                    else:
                        hots((i + 1) % T, 0, steps * i + steps)
                    low_part(i, b)

        @block.scalar
        def _(act):
            def high_part(i, g):
                act.wait_ge(hots_used, steps * i + WIN * (g + 2))
                if g == 0:
                    act.wait_ge(piece_turned, 4 * i + 4)
                nc.scalar.activation(strip_at(0, i)[:, :, g * GROUP:(g + 1) * GROUP],
                                     strip_ps[g % 2][:, 0:KEYS].rearrange("p (d k) -> p k d", d=GROUP), ACT.Copy).then_inc(hi_kept, 1)

            def keep_piece(i, q):
                act.wait_ge(piece_turned, 4 * i + q + 5)
                if q == 0:
                    act.wait_ge(rows_stored, 16 * (i + 1))
                nc.scalar.activation(rows_w[:, first_tile[q]:first_tile[q] + PIECES[q], :].rearrange("d k p -> d (k p)"),
                                     piece_ps[q % 2][:, 0:PIECES[q] * P], ACT.Copy).then_inc(piece_kept, 1)

            act.sem_inc(kept, 2)
            act.sem_inc(hots_used, WIN)
            act.sem_inc(piece_kept, 2)
            with act.Fori(0, LOOPS) as i:
                for b in range(RING):
                    high_part(i, b)
                    keep_piece(i, b)
                    act.wait_ge(back, RING * i + b + 3)
                    act.wait_ge(written[b % 2], 16 * (2 * i + b // 2 + 1))
                    nc.scalar.activation(out[b % 2][:, :, :].rearrange("p j d -> p (j d)"), back_ps[b % 2][:, 0:4 * D], ACT.Copy).then_inc(kept, 1)
            for q in range(4):
                keep_piece(T, q)

        @block.sync
        def _(sp):
            def store_rows(i):
                sp.wait_ge(piece_kept, 4 * i + 6)
                sp.dma_start(weights_dram[part, bass.ds(i * P, P), :], rows_w[:, :, :].rearrange("d k p -> d (k p)")).then_inc(rows_stored, 16)

            sp.sem_inc(written[0], 16)
            sp.sem_inc(written[1], 16)
            sp.sem_inc(rows_stored, 16)
            sp.dma_start(src_rows[:, :], src_cols).then_inc(listed_src, 16)
            for n in range(4):
                sp.dma_start(tables[:, n, :, :], tables_dram[:, n, :].rearrange("p (t q s) -> p t q s", t=T, q=2)[:, :, part, :]).then_inc(tables_loaded, 16)
            sp.dma_start(rows_dram[ZERO_ROW:ZERO_ROW + 1, :], c.ident[P - 1:P, 0:D]).then_inc(zero_out, 16)

            def load_list(n, b):
                sp.dma_start(same[b][:, :], same_dram[bass.ds(n * BLK, BLK)].rearrange("(a e) -> a e", a=1).to_broadcast([D, BLK])).then_inc(listed[b], 16)

            load_list(0, 0)
            load_list(1, 1)
            with sp.Fori(0, LOOPS) as i:
                for b in range(RING):
                    n = RING * i + b
                    sp.wait_ge(kept, n + 3)
                    sp.dma_start(rows_dram[bass.ds(n * BLK, BLK), :].rearrange("(j p) d -> p j d", p=P), out[b % 2][:, :, :]).then_inc(written[b % 2], 16)
                    load_list(n + 2, b % 2)
                store_rows(i)
            store_rows(T)
            sp.wait_ge(rows_stored, 16 * (T + 2))
            for b in range(2):
                sp.wait_ge(written[b], 16 * (1 + NBLK // 2))
                sp.wait_ge(listed[b], 16 * (1 + NBLK // 2))
            sp.wait_ge(zero_out, 16)


ROW_SCALE = 64.0


def split_rows(nc, rows, parts):
    with nc.semaphore("rows_split") as split, nc.Block() as block:
        @block.vector
        def _(dve):
            nc.vector.tensor_scalar(rows[:, :, :], rows[:, :, :], ROW_SCALE, None, ALU.mult).then_inc(split, 1)
            dve.wait_ge(split, 1)
            nc.vector.tensor_copy(parts[:, :, 0, :], rows[:, :, :]).then_inc(split, 1)
            dve.wait_ge(split, 2)
            nc.vector.tensor_tensor(parts[:, :, 1, :], rows[:, :, :], parts[:, :, 0, :], ALU.subtract).then_inc(split, 1)


def weighted_sum(nc, c, parts, weights_dram, total):
    banks = [(n, min(512, NP - n)) for n in range(0, NP, 512)]
    with stack() as ctx:
        sem = lambda n: ctx.enter_context(nc.semaphore(f"ws_{n}"))
        w = ctx.enter_context(nc.sbuf_tensor("ws_w", [P, 2, 2, NP], F16))
        sums_ps = [ctx.enter_context(nc.psum_tensor(f"ws_sums{n}", [P, 512], F32)) for n in range(len(banks))]
        back_ps = ctx.enter_context(nc.psum_tensor("ws_back", [P, 512], F32))
        loaded = [[sem(f"loaded{b}{h}") for h in range(2)] for b in range(2)]
        used, kept, turned, drained = sem("used"), sem("kept"), sem("turned"), sem("drained")
        block = ctx.enter_context(nc.Block())
        sumsT = w[0:D, 0, :, :].rearrange("p h n -> p (h n)").bitcast(F32)

        @block.sync
        def _(sp):
            def load(t, b, h):
                for half in range(2):
                    sp.dma_start(w[half * HALF:(half + 1) * HALF, b, h, :],
                                 weights_dram[half, bass.ds((t + 1) * P + h * HALF, HALF), :]).then_inc(loaded[b][h], 16)

            for b in range(2):
                for h in range(2):
                    load(b, b, h)
            with sp.Fori(1, T // 2) as i:
                for b in range(2):
                    for h in range(2):
                        sp.wait_ge(used, 4 * (i - 1) + 2 * b + h + 1)
                        load(2 * i + b, b, h)
            for h in range(2):
                sp.wait_ge(used, 2 * (T - 3) + h + 1)
                load(T - 1, 0, h)

        @block.tensor
        def _(pe):
            def add(i, b, first=False, last=False):
                tile = parts[:, bass.ds(2 * i + b, 1), :, :].rearrange("p a r d -> p (a r) d")
                for h in range(2):
                    pe.wait_ge(loaded[b][h], 32 * (i + 1))
                    for r in range(2):
                        for n, (begin, size) in enumerate(banks):
                            mm = nc.tensor.matmul(sums_ps[n][0:D, 0:size], tile[:, r, :], w[:, b, h, begin:begin + size],
                                                  start=first and h == r == 0, stop=last and h == r == 1, skip_group_check=True)
                    mm.then_inc(used, 1)

            add(0, 0, first=True)
            add(0, 1)
            with pe.Fori(1, T // 2) as i:
                for b in range(2):
                    add(i, b)
            add(T // 2, 0, last=True)
            pe.wait_ge(kept, len(banks))
            for t in range(T):
                if t >= 2:
                    pe.wait_ge(drained, t - 1)
                ps = back_ps if t % 2 == 0 else sums_ps[0]
                nc.tensor.transpose(ps[:, 0:D], sumsT[:, t * P:(t + 1) * P], c.ident[0:D, 0:D]).then_inc(turned, 1)

        @block.vector
        def _(dve):
            dve.wait_ge(used, 2 * T)
            for n, (begin, size) in enumerate(banks):
                nc.vector.tensor_scalar(sumsT[:, begin:begin + size], sums_ps[n][0:D, 0:size], 1.0 / (W_SCALE * ROW_SCALE), None, ALU.mult).then_inc(kept, 1)
            for t in range(T):
                dve.wait_ge(turned, t + 1)
                nc.vector.tensor_copy(total[:, t, :], back_ps[:, 0:D] if t % 2 == 0 else sums_ps[0][:, 0:D]).then_inc(drained, 1)


SUM_SCALE = 1024.0


def sum_pass(nc, c, overflow, table_dram, src_cols, dst_cols, w_cols, total):
    banks = [(n, min(512, NP - n)) for n in range(0, NP, 512)]
    with stack() as ctx:
        sb = lambda n, shape, dt: ctx.enter_context(nc.sbuf_tensor(f"sum_{n}", shape, dt))
        sem = lambda n: ctx.enter_context(nc.semaphore(f"sum_{n}"))
        index = [sb(f"index{i}", [P, 8], I32) for i in range(2)]
        row = [sb(f"row{i}", [P, 4, D], F32) for i in range(RING)]
        term = [sb(f"term{i}", [P, D], F32) for i in range(2)]
        hi = [sb(f"hi{i}", [P, D], F16) for i in range(2)]
        lo = [sb(f"lo{i}", [P, D], F16) for i in range(2)]
        hots = sb("hots", [P, 2, NP], F16)
        hot = [hots[:, i, :] for i in range(2)]
        nodes = sb("nodes", [P, NP], F16)
        nodes_i = hots[:, :, :].rearrange("p a n -> p (a n)").bitcast(I32)
        src_mid = sb("src_mid", [P, CHUNKS], F32)
        src_rows = sb("src_rows", [P, CHUNKS], I32)
        dst_rows, w_rows = sb("dst_rows", [P, CHUNKS], I32), sb("w_rows", [P, CHUNKS], F32)
        no_term = sb("no_term", [P, D], F16)
        sums_ps = [ctx.enter_context(nc.psum_tensor(f"sums{n}", [P, 512], F32)) for n in range(len(banks))]
        back_ps = ctx.enter_context(nc.psum_tensor("sums_back", [P, 512], F32))
        index_ready = sem("index_ready")
        gathered = [c.gather_sem(f"sum_gathered{i}") for i in range(RING)]
        ready, terms, split, used, gather_begun, kept, turned, drained, numbers = (
            sem("ready"), sem("terms"), sem("split"), sem("used"), sem("gather_begun"), sem("kept"), sem("turned"), sem("drained"), sem("numbers"))
        listed = sem("listed")
        block = ctx.enter_context(nc.Block())
        taken = lambda eng: eng.value_load(overflow[0:1, 0:1], min_val=0, max_val=NP) > 0
        sumsT = hots[0:D, :, :].rearrange("p a n -> p (a n)").bitcast(F32)

        @block.gpsimd
        def _(pool):
            with pool.If(taken(pool)):
                nc.gpsimd.iota(nodes_i, [[1, NP]], base=-NP // 2, channel_multiplier=0).then_inc(numbers, 1)
                pool.wait_ge(listed, 48)
                with pool.Fori(0, LOOPS) as i:
                    for b in range(RING):
                        if b % 2 == 0:
                            pool.wait_ge(terms, 16 * i + 4 * b + 8)
                            nc.gpsimd.tensor_copy(index[b // 2][:, :], dst_rows[:, bass.ds(4 * RING * i + 4 * b, 8)]).then_inc(index_ready, 1)
                            pool.wait_ge(index_ready, 2 * i + b // 2 + 1)
                            pool.sem_inc(gather_begun, 1)
                        for j in range(4):
                            nc.gpsimd.indirect_dma_start(row[b][:, j, :], None, table_dram,
                                                         bass.IndirectOffsetOnAxis(ap=index[b // 2][:, 4 * (b % 2) + j:4 * (b % 2) + j + 1], axis=0)
                                                         ).then_inc(gathered[b], 16)
                for b in range(RING):
                    pool.wait_ge(gathered[b], 64 * LOOPS)

        @block.sync
        def _(sp):
            with sp.If(taken(sp)):
                sp.dma_start(src_rows[:, :], src_cols).then_inc(listed, 16)
                sp.dma_start(dst_rows[:, :], dst_cols).then_inc(listed, 16)
                sp.dma_start(w_rows[:, :], w_cols).then_inc(listed, 16)

        @block.vector
        def _(dve):
            with dve.If(taken(dve)):
                dve.sem_inc(terms, 16)
                dve.wait_ge(listed, 48)
                dve.wait_ge(numbers, 1)
                nc.vector.tensor_copy(nodes[:, :], nodes_i).then_inc(drained, 1)
                nc.vector.tensor_copy(src_mid[:, :], src_rows[:, :]).then_inc(drained, 1)
                nc.vector.memset(no_term[:, :], 0.0).then_inc(ready, 1)
                dve.wait_ge(drained, 2)
                nc.vector.tensor_scalar(src_mid[:, :], src_mid[:, :], float(-NP // 2), None, ALU.add).then_inc(drained, 1)
                dve.wait_ge(drained, 3)
                with dve.Fori(0, LOOPS) as i:
                    for b in range(RING):
                        for j in range(4):
                            k = 4 * b + j
                            chunk = 16 * i + k
                            dve.wait_ge(used, chunk + 1)
                            nc.vector.tensor_scalar(hot[k % 2][:, :], nodes[:, :], src_mid[:, bass.ds(chunk, 1)], None, ALU.is_equal)
                            if j == 0:
                                dve.wait_ge(gathered[b], 64 * (i + 1))
                            t = nc.vector.tensor_scalar(term[k % 2][:, :], row[b][:, j, :], w_rows[:, bass.ds(chunk, 1)], SUM_SCALE, ALU.mult, ALU.mult)
                            t.then_inc(terms, 1)
                            dve.wait_ge(terms, chunk + 17)
                            nc.vector.tensor_copy(hi[k % 2][:, :], term[k % 2][:, :]).then_inc(split, 1)
                            dve.wait_ge(split, chunk + 1)
                            nc.vector.tensor_tensor(lo[k % 2][:, :], term[k % 2][:, :], hi[k % 2][:, :], ALU.subtract).then_inc(ready, 1)
                dve.wait_ge(used, CHUNKS + 3)
                for n, (first, size) in enumerate(banks):
                    nc.vector.tensor_scalar(sumsT[:, first:first + size], sums_ps[n][0:D, 0:size], 1.0 / SUM_SCALE, None, ALU.mult).then_inc(kept, 1)
                for t in range(T):
                    dve.wait_ge(turned, t + 1)
                    nc.vector.tensor_copy(total[:, t, :], back_ps[:, 0:D] if t % 2 == 0 else sums_ps[0][:, 0:D]).then_inc(drained, 1)

        @block.tensor
        def _(pe):
            with pe.If(taken(pe)):
                pe.sem_inc(used, 2)
                pe.wait_ge(ready, 1)
                for n, (first, size) in enumerate(banks):
                    nc.tensor.matmul(sums_ps[n][0:D, 0:size], no_term[:, :], nodes[:, first:first + size], start=True, stop=False, skip_group_check=True)
                with pe.Fori(0, LOOPS) as i:
                    for k in range(16):
                        chunk = 16 * i + k
                        pe.wait_ge(ready, chunk + 2)
                        for part in (hi, lo):
                            for n, (first, size) in enumerate(banks):
                                mm = nc.tensor.matmul(sums_ps[n][0:D, 0:size], part[k % 2][:, :], hot[k % 2][:, first:first + size],
                                                      start=False, stop=False, skip_group_check=True)
                        mm.then_inc(used, 1)
                for n, (first, size) in enumerate(banks):
                    mm = nc.tensor.matmul(sums_ps[n][0:D, 0:size], no_term[:, :], nodes[:, first:first + size], start=False, stop=True, skip_group_check=True)
                mm.then_inc(used, 1)
                pe.wait_ge(kept, len(banks))
                for t in range(T):
                    if t >= 2:
                        pe.wait_ge(drained, 3 + t - 1)
                    ps = back_ps if t % 2 == 0 else sums_ps[0]
                    nc.tensor.transpose(ps[:, 0:D], sumsT[:, t * P:(t + 1) * P], c.ident[0:D, 0:D]).then_inc(turned, 1)


def load_nodes(nc, c, name, pairs, rows_dram=None, agg=None):
    with (
        nc.semaphore(name + "_loaded") as loaded,
        nc.Block() as block,
    ):
        picked = c.gather_sem(name + "_picked") if rows_dram is not None else None

        @block.sync
        def _(sp):
            for tile, dram in pairs:
                sp.dma_start(tile[:, :, :], node_view(dram)).then_inc(loaded, 16)
            sp.wait_ge(loaded, 16 * len(pairs))

        @block.gpsimd
        def _(pool):
            if rows_dram is not None:
                for t in range(T):
                    nc.gpsimd.indirect_dma_start(agg[:, t, :], None, rows_dram, bass.IndirectOffsetOnAxis(ap=c.end_row[:, t:t + 1], axis=0)).then_inc(picked, 16)
                pool.wait_ge(picked, 16 * T)


def add_nodes(nc, name, x, terms, store=None, bias_dram=None):
    with (
        nc.sbuf_tensor(name + "_bias", [P, D], F32) as bias,
        nc.semaphore(name + "_added") as added,
        nc.semaphore(name + "_bias_loaded") as bias_loaded,
        nc.semaphore(name + "_stored") as stored,
        nc.Block() as block,
    ):
        steps = len(terms) + (bias_dram is not None)

        @block.sync
        def _(sp):
            if bias_dram is not None:
                sp.dma_start(bias[:, :], bias_dram.rearrange("(a d) -> a d", a=1).to_broadcast([P, D])).then_inc(bias_loaded, 16)
            sp.wait_ge(added, steps)
            if store is not None:
                sp.dma_start(node_view(store), x[:, :, :]).then_inc(stored, 16)
                sp.wait_ge(stored, 16)

        @block.vector
        def _(dve):
            for n, term in enumerate(terms[1:]):
                if n:
                    dve.wait_ge(added, n)
                nc.vector.tensor_tensor(terms[0][:, :, :], terms[0][:, :, :], term[:, :, :], ALU.add).then_inc(added, 1)
            n = len(terms) - 1
            if bias_dram is not None:
                dve.wait_ge(bias_loaded, 16)
                if n:
                    dve.wait_ge(added, n)
                nc.vector.tensor_tensor(terms[0][:, :, :], terms[0][:, :, :], bias[:, :].unsqueeze(1).to_broadcast([P, T, D]), ALU.add).then_inc(added, 1)
                n += 1
            if n:
                dve.wait_ge(added, n)
            nc.vector.tensor_tensor(x[:, :, :], x[:, :, :], terms[0][:, :, :], ALU.add).then_inc(added, 1)


def l2_normalise(nc, name, h, sq, relu, store=None):
    with (
        nc.sbuf_tensor(name + "_norm", [P, T], F32) as norm,
        nc.semaphore(name + "_dve") as dve_step,
        nc.semaphore(name + "_root") as root_ready,
        nc.semaphore(name + "_stored") as stored,
        nc.Block() as block,
    ):
        r = 1 if relu else 0

        @block.vector
        def _(dve):
            if relu:
                nc.vector.tensor_scalar(h[:, :, :], h[:, :, :], 0.0, None, ALU.max).then_inc(dve_step, 1)
                dve.wait_ge(dve_step, 1)
            nc.vector.tensor_tensor(sq[:, :, :], h[:, :, :], h[:, :, :], ALU.mult).then_inc(dve_step, 1)
            dve.wait_ge(dve_step, r + 1)
            nc.vector.tensor_reduce(norm[:, :], sq[:, :, :], AX.X, ALU.add).then_inc(dve_step, 1)
            dve.wait_ge(root_ready, 1)
            nc.vector.tensor_scalar(norm[:, :], norm[:, :], 1e-12, None, ALU.max).then_inc(dve_step, 1)
            dve.wait_ge(dve_step, r + 3)
            nc.vector.reciprocal(norm[:, :], norm[:, :]).then_inc(dve_step, 1)
            dve.wait_ge(dve_step, r + 4)
            nc.vector.tensor_tensor(h[:, :, :], h[:, :, :], norm[:, :].unsqueeze(2).to_broadcast([P, T, D]), ALU.mult).then_inc(dve_step, 1)

        @block.scalar
        def _(act):
            act.wait_ge(dve_step, r + 2)
            nc.scalar.activation(norm[:, :], norm[:, :], ACT.Sqrt).then_inc(root_ready, 1)

        @block.sync
        def _(sp):
            if store is not None:
                sp.wait_ge(dve_step, r + 5)
                sp.dma_start(node_view(store), h[:, :, :]).then_inc(stored, 16)
                sp.wait_ge(stored, 16)


def propagate_setup(nc, c, adj, h, base, g, state, coef, root):
    with stack() as ctx:
        sb = lambda n, shape, dt: ctx.enter_context(nc.sbuf_tensor(n, shape, dt))
        inv = sb("inv_deg", [P, T], F32)
        sem = lambda n: ctx.enter_context(nc.semaphore(n))
        d_step, rooted = sem("ps_step"), sem("ps_rooted")
        block = ctx.enter_context(nc.Block())

        @block.gpsimd
        def _(pool):
            for t in range(T):
                own = adj[:, t, t * P:(t + 1) * P]
                nc.gpsimd.tensor_tensor(own, own, c.ident16[:, :], ALU.add)

        @block.vector
        def _(dve):
            done = [0]

            def then_wait(ins):
                done[0] += 1
                ins.then_inc(d_step, 1)
                dve.wait_ge(d_step, done[0])

            then_wait(nc.vector.tensor_scalar(inv[:, :], c.deg[:, :], 1.0, None, ALU.add))
            dve.wait_ge(rooted, 1)
            then_wait(nc.vector.reciprocal(inv[:, :], inv[:, :]))
            then_wait(nc.vector.tensor_scalar(coef[:, :], inv[:, :], 1.0 - ALPHA, None, ALU.mult))
            then_wait(nc.vector.reciprocal(inv[:, :], root[:, :]))
            then_wait(nc.vector.tensor_tensor(state[:, :, :], h[:, :, :], inv[:, :].unsqueeze(2).to_broadcast([P, T, D]), ALU.mult))
            then_wait(nc.vector.tensor_scalar(state[:, :, :], state[:, :, :], GSCALE, None, ALU.mult))
            then_wait(nc.vector.tensor_scalar(root[:, :], root[:, :], 1.0 / GSCALE, None, ALU.mult))
            then_wait(nc.vector.tensor_copy(g[:, :, 0, :], state[:, :, :]))
            then_wait(nc.vector.tensor_tensor(g[:, :, 1, :], state[:, :, :], g[:, :, 0, :], ALU.subtract))
            then_wait(nc.vector.tensor_scalar(base[:, :, :], state[:, :, :], ALPHA, None, ALU.mult))

        @block.scalar
        def _(act):
            act.wait_ge(d_step, 1)
            nc.scalar.activation(root[:, :], inv[:, :], ACT.Sqrt).then_inc(rooted, 1)


def propagate(nc, c, adj, base, g, state, coef):
    BANKS, SIDE = 5, 3
    with stack() as ctx:
        ps = [ctx.enter_context(nc.psum_tensor(f"prop{i}", [P, 512], F32)) for i in range(BANKS)]
        part = ctx.enter_context(nc.sbuf_tensor("part", [P, 2, D], F32))
        sem = lambda n: ctx.enter_context(nc.semaphore(n))
        summed, low_added, state_ready, hi_ready, updated = sem("pr_summed"), sem("pr_low"), sem("pr_state"), sem("pr_hi"), sem("pr_updated")
        block = ctx.enter_context(nc.Block())

        @block.tensor
        def _(pe):
            with pe.Fori(0, K_PROP // 2) as i:
                for half in range(2):
                    step = 2 * i + half
                    def products(tiles):
                        for t in tiles:
                            pe.wait_ge(state_ready, T * step + T + t - BANKS + 1)
                        for k in range(T):
                            if tiles[0] == 0:
                                pe.wait_ge(updated, T * step + k + 1)
                            for t in tiles:
                                mm = nc.tensor.matmul(ps[t % BANKS][:, 0:2 * D], adj[:, k, t * P:(t + 1) * P],
                                                      g[half][:, k, :, :].rearrange("p a d -> p (a d)"), start=k == 0, stop=k == T - 1)
                                if k == T - 1:
                                    mm.then_inc(summed, 1)

                    products(range(SIDE))
                    for t in range(SIDE, T):
                        products([t])

        @block.vector
        def _(dve):
            dve.sem_inc(updated, T)
            dve.sem_inc(state_ready, T)
            with dve.Fori(0, K_PROP // 2) as i:
                for half in range(2):
                    step = 2 * i + half

                    def new_state(t):
                        dve.wait_ge(summed, T * step + t + 1)
                        nc.vector.scalar_tensor_tensor(part[:, t % 2, :], ps[t % BANKS][:, D:2 * D], coef[:, t:t + 1], base[:, t, :], ALU.mult, ALU.add).then_inc(low_added, 1)
                        dve.wait_ge(low_added, T * step + t + 1)
                        nc.vector.scalar_tensor_tensor(state[:, t, :], ps[t % BANKS][:, 0:D], coef[:, t:t + 1], part[:, t % 2, :], ALU.mult, ALU.add).then_inc(state_ready, 1)

                    def low_part(t):
                        dve.wait_ge(hi_ready, T * step + t + 1)
                        nc.vector.tensor_tensor(g[1 - half][:, t, 1, :], state[:, t, :], g[1 - half][:, t, 0, :], ALU.subtract).then_inc(updated, 1)

                    for t in range(T):
                        new_state(t)
                        low_part(t)

        @block.scalar
        def _(act):
            with act.Fori(0, K_PROP // 2) as i:
                for half in range(2):
                    for t in range(T):
                        act.wait_ge(state_ready, T * (2 * i + half) + T + t + 1)
                        nc.scalar.activation(g[1 - half][:, t, 0, :], state[:, t, :], ACT.Copy).then_inc(hi_ready, 1)


def finish(nc, x, state, root, x_dram, out):
    with (
        nc.semaphore("x_back") as x_back,
        nc.semaphore("scaled") as scaled,
        nc.semaphore("out_written") as out_written,
        nc.Block() as block,
    ):
        @block.sync
        def _(sp):
            sp.dma_start(x, node_view(x_dram)).then_inc(x_back, 16)
            sp.wait_ge(scaled, 2)
            sp.dma_start(out[0:(T - 1) * P, :].rearrange("(t p) d -> p t d", p=P), state[:, 0:T - 1, :]).then_inc(out_written, 16)
            sp.dma_start(out[(T - 1) * P:N, :], state[0:LAST, T - 1, :]).then_inc(out_written, 16)
            sp.wait_ge(out_written, 32)

        @block.vector
        def _(dve):
            nc.vector.tensor_tensor(state[:, :, :], state[:, :, :], root[:, :].unsqueeze(2).to_broadcast([P, T, D]), ALU.mult).then_inc(scaled, 1)
            dve.wait_ge(scaled, 1)
            dve.wait_ge(x_back, 16)
            nc.vector.tensor_tensor(state[:, :, :], state[:, :, :], x, ALU.add).then_inc(scaled, 1)


def gnn(nc, x, src, dst, edge_weight, qW, kW, vW, Wp1, bp1, Ws1, Wn1, b1, Wp2, bp2, Ws2, Wn2, b2, G, bG, out):
    scratch = lambda name, shape, dt=F32: nc.dram_tensor(name, shape, dt).ap()
    src_pad, dst_pad = scratch("src_pad", (CHUNKS + 1, P), I32), scratch("dst_pad", (CHUNKS + 1, P), I32)
    win_dram, tables_dram = scratch("win_dram", (WROWS, 3, P), I32), scratch("tables_dram", (P, 4, NSTEP))
    dst_ext = scratch("dst_ext", (1 + EXT,), I32)
    w_pad = scratch("w_pad", (EXT,))
    same_dram = scratch("same_dram", (EXT,), F16)
    src_cols, dst_cols, w_cols = scratch("src_cols", (P, CHUNKS), I32), scratch("dst_cols", (P, CHUNKS), I32), scratch("w_cols", (P, CHUNKS))
    weights_dram = scratch("weights", (2, (T + 1) * P, NP), F16)
    group_dram = scratch("group_dram", (SPAD,), I32)
    q_dram, k_dram = scratch("q_dram", (D, T, 512), F16), scratch("k_dram", (D, T, 512), F16)
    v_dram = scratch("v_dram", (P, T * HEADS * (DH + 1)))
    h_dram, x_dram, table = (scratch(n, (NP, D)) for n in ("h_dram", "x_dram", "table"))
    res_dram = scratch("res_dram", (P + NP, D))
    rows_dram = scratch("rows_dram", (EP + 1, D))

    with stack() as ctx:
        c = make_constants(nc, ctx)
        attention_inputs(nc, c, x, qW, kW, vW, h_dram, q_dram, k_dram, v_dram)
        adj = ctx.enter_context(nc.sbuf_tensor("adj", [P, T, NP], F16))
        overflow = ctx.enter_context(nc.sbuf_tensor("overflow", [1, 1], I32))
        with stack() as own:
            first_row = own.enter_context(nc.sbuf_tensor("first_row", [1, PHASES, CHUNKS], F32))
            edge_lists(nc, c, src, dst, edge_weight, src_pad, dst_pad, dst_ext, w_pad, src_cols, dst_cols, w_cols, same_dram, win_dram, first_row)
            tables = own.enter_context(nc.sbuf_tensor("tables", [P, 4, NSTEP], F32))
            adjacency_windows(nc, c, win_dram, first_row, tables, tables_dram, overflow)
            build_adjacency(nc, c, adj, tables)
        walk_adjacency(nc, c, adj, overflow, src_pad, dst_pad, group_dram)
        degrees(nc, c, adj)
        attention(nc, c, adj, q_dram, k_dram, v_dram, res_dram)

        def node_tiles(own, name, n):
            return [own.enter_context(nc.sbuf_tensor(f"{name}{i}", [P, T, D], F32)) for i in range(n)]

        with stack() as own:
            xt, h, r = node_tiles(own, "n1_", 3)
            with nc.semaphore("x_in") as x_in, nc.semaphore("x_zeroed") as x_zeroed, nc.Block() as block:
                @block.vector
                def _(dve):
                    nc.vector.memset(xt[:, T - 1, :], 0.0).then_inc(x_zeroed, 1)

                @block.sync
                def _(sp):
                    sp.dma_start(xt[:, 0:T - 1, :], x[0:(T - 1) * P, :].rearrange("(t p) d -> p t d", p=P)).then_inc(x_in, 16)
                    sp.wait_ge(x_zeroed, 1)
                    sp.dma_start(xt[0:LAST, T - 1, :], x[(T - 1) * P:N, :]).then_inc(x_in, 16)
                    sp.wait_ge(x_in, 32)
            load_nodes(nc, c, "ld1", ((h, h_dram), (r, res_dram[P:P + NP, :])))
            add_nodes(nc, "add1", xt, (h, r), store=x_dram)
            layernorm_relu(nc, "ln1", xt, h, r, to_store=((h_dram, h),))
            project(nc, c, "pool1", ((h, Wp1),), bp1, r, to_store=table, relu=True)
        clear_semaphores(nc)
        max_pass(nc, c, "max1", table, src_cols, same_dram, rows_dram, tables_dram, weights_dram, 0)
        with stack() as own:
            h, agg, o = node_tiles(own, "n2_", 3)
            load_nodes(nc, c, "ld2", ((h, h_dram),), rows_dram, agg)
            project(nc, c, "sage1", ((h, Ws1), (agg, Wn1)), b1, o)
            l2_normalise(nc, "l2a", o, h, relu=True, store=h_dram)
            project(nc, c, "pool2", ((o, Wp2),), bp2, agg, to_store=table, relu=True)
        max_pass(nc, c, "max2", table, src_cols, same_dram, rows_dram, tables_dram, weights_dram, 1)
        with stack() as own:
            state, = node_tiles(own, "n4_", 1)
            with stack() as sums:
                support = sums.enter_context(nc.sbuf_tensor("support_parts", [P, T, 2, D], F16))
                with stack() as nodes:
                    h, o = node_tiles(nodes, "n3_", 2)
                    agg = state
                    load_nodes(nc, c, "ld3", ((h, h_dram),), rows_dram, agg)
                    project(nc, c, "sage2", ((h, Ws2), (agg, Wn2)), b2, o)
                    l2_normalise(nc, "l2b", o, h, relu=False)
                    load_nodes(nc, c, "ld4", ((h, x_dram),))
                    add_nodes(nc, "add2", h, (o,), store=x_dram)
                    layernorm_relu(nc, "ln2", h, o, agg)
                    project(nc, c, "support", ((o, G),), None, agg, to_store=table)
                    split_rows(nc, agg, support)
                clear_semaphores(nc)
                weighted_sum(nc, c, support, weights_dram, state)
            sum_pass(nc, c, overflow, table, src_cols, dst_cols, w_cols, state)
            base, = node_tiles(own, "n6_", 1)
            coef, root = (own.enter_context(nc.sbuf_tensor(n, [P, T], F32)) for n in ("coef", "root"))
            with stack() as ln:
                h, = node_tiles(ln, "n5_", 1)
                load_nodes(nc, c, "ld5", ((h, x_dram),))
                add_nodes(nc, "add3", h, (state,), store=x_dram, bias_dram=bG)
                layernorm_relu(nc, "ln3", h, base, state)
            g = [own.enter_context(nc.sbuf_tensor(f"g{i}", [P, T, 2, D], F16)) for i in range(2)]
            propagate_setup(nc, c, adj, base, base, g[0], state, coef, root)
            propagate(nc, c, adj, base, g, state, coef)
            xb = g[1][:, :, :, :].rearrange("p t a d -> p (t a d)").bitcast(F32).rearrange("p (t d) -> p t d", t=T)
            finish(nc, xb, state, root, x_dram, out)


_INS = ["x", "src", "dst", "edge_weight", "L0_gnn_qW", "L0_gnn_kW", "L0_gnn_vW", "L1_gnn_Wp1", "L1_gnn_bp1", "L1_gnn_Ws1",
        "L1_gnn_Wn1", "L1_gnn_b1", "L1_gnn_Wp2", "L1_gnn_bp2", "L1_gnn_Ws2", "L1_gnn_Wn2", "L1_gnn_b2",
        "L2_gnn_weight_G", "L2_gnn_bias_G"]


def kernel(**inputs):
    import numpy as np
    import concourse.bacc as bacc
    from concourse.bass_utils import run_bass_kernel_spmd

    nc = bacc.Bacc("TRN2", target_bir_lowering=False, num_devices=1)
    arrays, args = {}, []
    for name in _INS:
        a = np.ascontiguousarray(inputs[name])
        arrays[f"in_{name}_dram"] = a
        args.append(nc.dram_tensor(f"in_{name}_dram", a.shape, mybir.dt.from_np(a.dtype), kind="ExternalInput").ap())
    out = nc.dram_tensor("out_0_dram", (N, D), F32, kind="ExternalOutput").ap()
    gnn(nc, *args, out)
    r = run_bass_kernel_spmd(nc, [arrays], core_ids=[0])
    return r.results[0]["out_0_dram"]
```

```python
import math
from contextlib import ExitStack

import concourse.bass as bass
from concourse import mybir

F32 = mybir.dt.float32
F16 = mybir.dt.float16
I32 = mybir.dt.int32
ALU = mybir.AluOpType
ACT = mybir.ActivationFunctionType
AX = mybir.AxisListType

N = 3125
E = 50000
D = 96
HEADS = 4
DH = D // HEADS
P = 128
T = -(-N // P)
NP = T * P
LAST = N - (T - 1) * P

BLK = 4 * P
RING = 4
LOOPS = -(-E // (BLK * RING))
NBLK = LOOPS * RING
EP = NBLK * BLK
CHUNKS = EP // P
LAST_BLOCKS = -(-E // BLK) - (LOOPS - 1) * RING
PAD_DST = 4000
EXT = EP + 2 * BLK
ZERO_ROW = EP

GROUP = 16
NGROUP = NP // GROUP
KEYS = GROUP * T
WIN = 3
PHASES = 4
WROWS = CHUNKS * PHASES
NSTEP = NGROUP * WIN
GT = -(-NGROUP // P)
USED = -(-E // P)
STEPS = (USED + NGROUP - 1) | 1
STILES = -(-STEPS // P)
SPAD = STILES * P

W_SCALE = 1024.0
K_PROP = 16
ALPHA = 0.1
GSCALE = 4096.0


class Consts:
    pass


def stack():
    return ExitStack()


def node_view(dram):
    if dram.shape[0] == P:
        return dram.rearrange("p (t d) -> p t d", d=D)
    return dram.rearrange("(t p) d -> p t d", p=P)


def clear_semaphores(nc):
    used = sorted(nc.released_uncleared_semaphores)
    with nc.Block() as block:
        @block.gpsimd
        def _(pool):
            first = 0
            for n in range(len(used)):
                if n + 1 == len(used) or used[n + 1] != used[n] + 1:
                    nc.gpsimd.sem_clear(range(used[first], used[n] + 1))
                    first = n + 1


def make_constants(nc, ctx):
    c = Consts()
    c.gather_sem = lambda name: ctx.enter_context(nc.semaphore(name))
    sb = lambda name, shape, dt: ctx.enter_context(nc.sbuf_tensor(name, shape, dt))
    c.ident = sb("ident", [P, P], F32)
    c.ident16 = sb("ident16", [P, P], F16)
    c.ones = sb("ones", [P, P], F32)
    c.ones16 = sb("ones16", [P, 1], F16)
    c.iota16 = sb("iota16", [P, KEYS], F16)
    c.deg = sb("deg", [P, T], F32)
    c.end_row = sb("end_row", [P, T], I32)
    with (
        nc.semaphore("const_step") as const_step,
        nc.sbuf_tensor("iota_i", [P, KEYS], I32) as iota_i,
        nc.Block() as block,
    ):
        @block.gpsimd
        def _(pool):
            nc.gpsimd.memset(c.ident[:, :], 0.0)
            nc.gpsimd.memset(c.ones[:, :], 1.0)
            nc.gpsimd.memset(c.ones16[:, :], 1.0)
            nc.gpsimd.iota(iota_i[:, :], [[1, KEYS]], base=0, channel_multiplier=0).then_inc(const_step, 1)
            pool.wait_ge(const_step, 1)
            nc.gpsimd.affine_select(out=c.ident[:, :], in_=c.ident[:, :], compare_op=ALU.not_equal, fill=1.0,
                                    base=0, pattern=[[-1, P]], channel_multiplier=1)
            nc.gpsimd.tensor_copy(c.iota16[:, :], iota_i[:, :]).then_inc(const_step, 1)
            pool.wait_ge(const_step, 2)
            nc.gpsimd.tensor_copy(c.ident16[:, :], c.ident[:, :])
    return c


def layernorm_relu(nc, name, x, h, sq, load=(), term=None, bias_dram=None, count_degrees=None):
    with stack() as ctx:
        mean, var = (ctx.enter_context(nc.sbuf_tensor(f"{name}_{n}", [P, T], F32)) for n in ("mean", "var"))
        bias = ctx.enter_context(nc.sbuf_tensor(name + "_bias", [P, D], F32))
        sem = lambda n: ctx.enter_context(nc.semaphore(f"{name}_{n}"))
        dve_step, variance_ready, std_ready, loaded = sem("dve"), sem("variance_ready"), sem("std_ready"), sem("loaded")
        block = ctx.enter_context(nc.Block())
        by_node = lambda a: a[:, :].unsqueeze(2).to_broadcast([P, T, D])
        nload = len(load) + (bias_dram is not None)

        @block.sync
        def _(sp):
            for tile, dram in load:
                sp.dma_start(tile[:, :, :], node_view(dram)).then_inc(loaded, 16)
            if bias_dram is not None:
                sp.dma_start(bias[:, :], bias_dram.rearrange("(a d) -> a d", a=1).to_broadcast([P, D])).then_inc(loaded, 16)

        @block.vector
        def _(dve):
            done = [0]

            def then_wait(ins):
                done[0] += 1
                ins.then_inc(dve_step, 1)
                dve.wait_ge(dve_step, done[0])

            if nload:
                dve.wait_ge(loaded, 16 * nload)
            if bias_dram is not None:
                then_wait(nc.vector.tensor_tensor(term[:, :, :], term[:, :, :], bias[:, :].unsqueeze(1).to_broadcast([P, T, D]), ALU.add))
            if term is not None:
                then_wait(nc.vector.tensor_tensor(x[:, :, :], x[:, :, :], term[:, :, :], ALU.add))
            then_wait(nc.vector.tensor_reduce(mean[:, :], x[:, :, :], AX.X, ALU.add))
            then_wait(nc.vector.tensor_scalar(mean[:, :], mean[:, :], 1.0 / D, None, ALU.mult))
            then_wait(nc.vector.tensor_tensor(h[:, :, :], x[:, :, :], by_node(mean), ALU.subtract))
            then_wait(nc.vector.tensor_tensor(sq[:, :, :], h[:, :, :], h[:, :, :], ALU.mult))
            then_wait(nc.vector.tensor_reduce(var[:, :], sq[:, :, :], AX.X, ALU.add))
            nc.vector.tensor_scalar(var[:, :], var[:, :], 1.0 / D, 1e-5, ALU.mult, ALU.add).then_inc(variance_ready, 1)
            dve.wait_ge(std_ready, 1)
            then_wait(nc.vector.reciprocal(var[:, :], var[:, :]))
            nc.vector.scalar_tensor_tensor(h[:, :, :], h[:, :, :], 0.0, by_node(var), ALU.max, ALU.mult)

        @block.tensor
        def _(pe):
            if count_degrees is not None:
                adj, c, deg_ps = count_degrees
                for t in range(T):
                    for k in range(T):
                        nc.tensor.matmul(deg_ps[:, t:t + 1], adj[:, k, t * P:(t + 1) * P], c.ones16[:, :], start=k == 0, stop=k == T - 1)

        @block.scalar
        def _(act):
            act.wait_ge(variance_ready, 1)
            nc.scalar.activation(var[:, :], var[:, :], ACT.Sqrt).then_inc(std_ready, 1)


def project(nc, c, name, pairs, bias_dram, out, to_store=None, relu=False, load=(), pick=None, keep=()):
    ns = len(pairs)
    AHEAD, RINGS = 3, 4
    PART = 5
    LAG = 5
    assert T % PART == 0
    with stack() as ctx:
        weights = [ctx.enter_context(nc.sbuf_tensor(f"{name}_w{i}", [D, D], F32)) for i in range(ns)]
        bias = ctx.enter_context(nc.sbuf_tensor(name + "_b", [P, D], F32))
        xT = ctx.enter_context(nc.sbuf_tensor(name + "_xT", [D, RINGS, P], F32))
        xT_ps = [ctx.enter_context(nc.psum_tensor(f"{name}_xTps{i}", [P, 512], F32)) for i in range(RINGS)]
        sum_ps = [ctx.enter_context(nc.psum_tensor(f"{name}_sum{i}", [P, 512], F32)) for i in range(2)]
        sem = lambda n: ctx.enter_context(nc.semaphore(f"{name}_{n}"))
        nodes_loaded, loaded, transposed, copied, summed, drained, stored = (
            sem("nodes_loaded"), sem("loaded"), sem("transposed"), sem("copied"), sem("summed"), sem("drained"), sem("stored"))
        rectified = sem("rectified")
        picked = [c.gather_sem(f"{name}_picked{i}") for i in range(T // PART)] if pick else []
        block = ctx.enter_context(nc.Block())
        nload = 16 * (ns + (bias_dram is not None))

        @block.sync
        def _(sp):
            for tile, dram in load:
                sp.dma_start(tile[:, :, :], node_view(dram)).then_inc(nodes_loaded, 16)
            for w, (_, w_dram) in zip(weights, pairs):
                sp.dma_start(w[:, :], w_dram).then_inc(loaded, 16)
            if bias_dram is not None:
                sp.dma_start(bias[:, :], bias_dram.rearrange("(a d) -> a d", a=1).to_broadcast([P, D])).then_inc(loaded, 16)
            stores = len(keep)
            for dram, tile in keep:
                sp.dma_start(node_view(dram), tile[:, :, :]).then_inc(stored, 16)
            if to_store is not None:
                for t in range(0, T, PART):
                    sp.wait_ge(rectified if relu else drained, t + PART)
                    sp.dma_start(node_view(to_store)[:, t:t + PART, :], out[:, t:t + PART, :]).then_inc(stored, 16)
                    stores += 1
            if stores:
                sp.wait_ge(stored, 16 * stores)

        @block.gpsimd
        def _(pool):
            if pick:
                tile, rows_dram = pick
                for t in range(T):
                    nc.gpsimd.indirect_dma_start(tile[:, t, :], None, rows_dram, bass.IndirectOffsetOnAxis(ap=c.end_row[:, t:t + 1], axis=0)).then_inc(picked[t // PART], 16)
                for p in picked:
                    pool.wait_ge(p, 16 * PART)

        @block.tensor
        def _(pe):
            def transpose(i):
                t, s = i // ns, i % ns
                if pick and pairs[s][0] is pick[0]:
                    pe.wait_ge(picked[t // PART], 16 * PART)
                if i >= RINGS:
                    pe.wait_ge(copied, i - RINGS + 1)
                nc.tensor.transpose(xT_ps[i % RINGS][0:D, 0:P], pairs[s][0][:, t, :], c.ident[:, :]).then_inc(transposed, 1)

            def product(i):
                t, s = i // ns, i % ns
                if s == 0 and t >= 2:
                    pe.wait_ge(drained, t - 1)
                pe.wait_ge(copied, i + 1)
                last = s == ns - 1
                mm = nc.tensor.matmul(sum_ps[t % 2][:, 0:D], xT[:, i % RINGS, :], weights[s][:, :], start=s == 0,
                                      stop=last)
                if last:
                    mm.then_inc(summed, 1)

            if load:
                pe.wait_ge(nodes_loaded, 16 * len(load))
            for i in range(AHEAD):
                transpose(i)
            pe.wait_ge(loaded, nload)
            for i in range(T * ns):
                if i + AHEAD < T * ns:
                    transpose(i + AHEAD)
                product(i)

        @block.scalar
        def _(act):
            def rectify(t):
                act.wait_ge(drained, t + 1)
                nc.scalar.activation(out[:, t, :], out[:, t, :], ACT.Relu).then_inc(rectified, 1)

            for i in range(T * ns):
                act.wait_ge(transposed, i + 1)
                if i >= RINGS:
                    act.wait_ge(summed, (i - RINGS) // ns + 1)
                nc.scalar.activation(xT[:, i % RINGS, :], xT_ps[i % RINGS][0:D, 0:P], ACT.Copy).then_inc(copied, 1)
                if relu and i % ns == 0 and i // ns >= LAG:
                    rectify(i // ns - LAG)
            if relu:
                for t in range(T - LAG, T):
                    rectify(t)

        @block.vector
        def _(dve):
            if bias_dram is not None:
                dve.wait_ge(loaded, nload)
            for t in range(T):
                dve.wait_ge(summed, t + 1)
                if bias_dram is not None:
                    nc.vector.tensor_tensor(out[:, t, :], sum_ps[t % 2][:, 0:D], bias[:, :], ALU.add).then_inc(drained, 1)
                else:
                    nc.vector.tensor_copy(out[:, t, :], sum_ps[t % 2][:, 0:D]).then_inc(drained, 1)


def attention_inputs(nc, c, x_dram, qW, kW, vW, xh_dram, q_dram, k_dram, v_dram):
    with stack() as ctx:
        sb = lambda name, shape, dt: ctx.enter_context(nc.sbuf_tensor(name, shape, dt))
        x = sb("x0", [P, T, D], F32)
        h = sb("h0", [P, T, D], F32)
        sq = sb("sq0", [P, T, D], F32)
        w_rep = [sb(f"w_rep{i}", [D, HEADS, 4, DH], F32) for i in range(2)]
        w_in = [sb(f"w_in{i}", [D, D], F32) for i in range(3)]
        row_i = sb("row_i", [D, 1], I32)
        row = sb("row", [D, 1], F32)
        step = sb("step", [D, 3], F32)
        neg_lo = sb("neg_lo", [D, 2], F32)
        hT = sb("hT", [D, 2, P], F32)
        hi = sb("hi", [D, 2, 2, 512], F16)
        q_st = sb("q_st", [D, 2, 512], F16)
        k_st = sb("k_st", [D, 2, 512], F16)
        v_all = sb("v_all", [P, T, HEADS, DH + 1], F32)
        with (
            nc.semaphore("x_loaded") as x_loaded,
            nc.semaphore("pad_zeroed") as pad_zeroed,
            nc.semaphore("w_copied") as w_copied,
            nc.semaphore("row_made") as row_made,
            nc.Block() as block,
        ):
            @block.sync
            def _(sp):
                sp.dma_start(x[:, 0:T - 1, :], x_dram[0:(T - 1) * P, :].rearrange("(t p) d -> p t d", p=P)).then_inc(x_loaded, 16)
                sp.wait_ge(pad_zeroed, 1)
                sp.dma_start(x[0:LAST, T - 1, :], x_dram[(T - 1) * P:N, :]).then_inc(x_loaded, 16)
                for w, dram in zip(w_in, (qW, kW, vW)):
                    sp.dma_start(w[:, :], dram).then_inc(x_loaded, 16)
                sp.wait_ge(x_loaded, 80)

            @block.gpsimd
            def _(pool):
                nc.gpsimd.memset(v_all[:, :, :, :], 1.0)
                nc.gpsimd.iota(row_i[:, :], [[0, 1]], base=0, channel_multiplier=1).then_inc(row_made, 1)

            @block.vector
            def _(dve):
                nc.vector.memset(x[:, T - 1, :], 0.0).then_inc(pad_zeroed, 1)
                dve.wait_ge(row_made, 1)
                nc.vector.tensor_copy(row[:, :], row_i[:, :]).then_inc(w_copied, 1)
                dve.wait_ge(w_copied, 1)
                for j in range(3):
                    nc.vector.tensor_scalar(step[:, j:j + 1], row[:, :], float((j + 1) * DH), None, ALU.is_ge).then_inc(w_copied, 1)
                dve.wait_ge(w_copied, 4)
                nc.vector.tensor_tensor(neg_lo[:, 0:1], step[:, 1:2], step[:, 0:1], ALU.subtract).then_inc(w_copied, 1)
                nc.vector.tensor_scalar(neg_lo[:, 1:2], step[:, 1:2], -1.0, None, ALU.mult)
                dve.wait_ge(w_copied, 5)
                nc.vector.tensor_tensor(neg_lo[:, 0:1], neg_lo[:, 0:1], step[:, 2:3], ALU.subtract)
                dve.wait_ge(x_loaded, 80)
                for i in range(2):
                    for j in range(4):
                        nc.vector.tensor_copy(w_rep[i][:, :, j, :], w_in[i][:, :].rearrange("p (h f) -> p h f", h=HEADS))

        layernorm_relu(nc, "ln0", x, h, sq)

        tr_ps = [ctx.enter_context(nc.psum_tensor(f"a_tr{i}", [P, 512], F32)) for i in range(2)]
        q_ps, k_ps, v_ps = ([ctx.enter_context(nc.psum_tensor(f"a_{n}{i}", [P, 512], F32)) for i in range(2)] for n in "qkv")
        sem = lambda name: ctx.enter_context(nc.semaphore(name))
        transposed, copied = sem("a_transposed"), sem("a_copied")
        q_made, k_made, v_made = sem("a_q_made"), sem("a_k_made"), sem("a_v_made")
        hi_made, parts_made, v_kept = sem("a_hi_made"), sem("a_parts_made"), sem("a_v_kept")
        qk_stored = [sem("a_qk_stored0"), sem("a_qk_stored1")]
        v_stored, xh_made = sem("a_v_stored"), sem("a_xh_made")
        block = ctx.enter_context(nc.Block())

        @block.tensor
        def _(pe):
            def transpose_tile(t):
                if t >= 2:
                    pe.wait_ge(copied, t - 1)
                nc.tensor.transpose(tr_ps[t % 2][0:D, 0:P], h[:, t, :], c.ident[:, :]).then_inc(transposed, 1)

            transpose_tile(0)
            for t in range(T):
                if t + 1 < T:
                    transpose_tile(t + 1)
                pe.wait_ge(copied, t + 1)
                for j, (ps, w, made) in enumerate(((q_ps, w_rep[0], q_made), (k_ps, w_rep[1], k_made))):
                    if t >= 2:
                        pe.wait_ge(parts_made, 2 * t - 3 + j)
                    for hd in range(HEADS):
                        mm = nc.tensor.matmul(ps[t % 2][0:D, hd * P:(hd + 1) * P], w[:, hd, :, :].rearrange("p j f -> p (j f)"),
                                              hT[:, t % 2, :], start=True, stop=True)
                    mm.then_inc(made, 1)
                if t >= 2:
                    pe.wait_ge(v_kept, t - 1)
                nc.tensor.matmul(v_ps[t % 2][:, 0:D], hT[:, t % 2, :], w_in[2][:, :], start=True, stop=True).then_inc(v_made, 1)

        @block.gpsimd
        def _(pool):
            nc.gpsimd.tensor_tensor(x[:, :, :], x[:, :, :], h[:, :, :], ALU.add).then_inc(xh_made, 1)

        @block.scalar
        def _(act):
            def copy_turned(t):
                act.wait_ge(transposed, t + 1)
                if t >= 2:
                    act.wait_ge(v_made, t - 1)
                nc.scalar.activation(hT[:, t % 2, :], tr_ps[t % 2][0:D, 0:P], ACT.Copy).then_inc(copied, 1)

            copy_turned(0)
            for t in range(T):
                if t + 1 < T:
                    copy_turned(t + 1)
                for j, (ps, made) in enumerate(((q_ps, q_made), (k_ps, k_made))):
                    act.wait_ge(made, t + 1)
                    if t >= 2:
                        act.wait_ge(parts_made, 2 * t - 3 + j)
                    nc.scalar.activation(hi[:, j, t % 2, :], ps[t % 2][0:D, :], ACT.Copy).then_inc(hi_made, 1)

        @block.vector
        def _(dve):
            for t in range(T):
                for j, (ps, st) in enumerate(((q_ps, q_st), (k_ps, k_st))):
                    dve.wait_ge(hi_made, 2 * t + j + 1)
                    if j == 0 and t >= 2:
                        dve.wait_ge(qk_stored[t % 2], 32 * (t // 2))
                    nc.vector.scalar_tensor_tensor(st[:, t % 2, :], hi[:, j, t % 2, :], neg_lo[:, j:j + 1], ps[t % 2][0:D, :],
                                                   ALU.mult, ALU.add).then_inc(parts_made, 1)
                dve.wait_ge(v_made, t + 1)
                nc.vector.tensor_copy(v_all[:, t, :, 0:DH], v_ps[t % 2][:, 0:D].rearrange("p (h f) -> p h f", h=HEADS)).then_inc(v_kept, 1)

        @block.sync
        def _(sp):
            sp.wait_ge(xh_made, 1)
            sp.dma_start(node_view(xh_dram), x[:, :, :]).then_inc(v_stored, 16)
            for t in range(T):
                sp.wait_ge(parts_made, 2 * t + 2)
                sp.dma_start(q_dram[:, t, :], q_st[:, t % 2, :]).then_inc(qk_stored[t % 2], 16)
                sp.dma_start(k_dram[:, t, :], k_st[:, t % 2, :]).then_inc(qk_stored[t % 2], 16)
            sp.wait_ge(v_kept, T)
            sp.dma_start(v_dram, v_all[:, :, :, :].rearrange("p t h f -> p (t h f)")).then_inc(v_stored, 16)
            sp.wait_ge(v_stored, 32)
            sp.wait_ge(qk_stored[0], 32 * ((T + 1) // 2))
            sp.wait_ge(qk_stored[1], 32 * (T // 2))


def edge_lists(nc, c, src, dst, weight, src_pad, dst_pad, dst_ext, w_pad, src_cols, dst_cols, w_cols, same_dram, win_dram, first_row):
    npad = EP + P - E
    quarter = CHUNKS // 4
    with stack() as ctx:
        sb = lambda name, shape, dt: ctx.enter_context(nc.sbuf_tensor(name, shape, dt))
        zero_i, far, before = sb("zero_i", [1, EXT - E], I32), sb("far", [1, EXT - E], I32), sb("before", [1, 1], I32)
        zero_f = zero_i[:, :].bitcast(F32)
        src_i, dst_i, before_i = (sb(n, [quarter, 4, P], I32) for n in ("src_c", "dst_c", "before_c"))
        same = sb("same_c", [quarter, 4, P], F16)
        src_f, dst_f, w_f = (sb(n, [quarter, 4, P], F32) for n in ("src_cf", "dst_cf", "w_cf"))
        src_t, dst_t, w_t = sb("src_t", [P, CHUNKS], I32), sb("dst_t", [P, CHUNKS], I32), sb("w_t", [P, CHUNKS], F32)
        rows_ps = [ctx.enter_context(nc.psum_tensor(f"rows_ps{i}", [P, 512], F32)) for i in range(3)]
        sem = lambda name: ctx.enter_context(nc.semaphore(name))
        pads, padded, rows_loaded, rows_cast, turned = sem("pads"), sem("padded"), sem("rows_loaded"), sem("rows_cast"), sem("turned")
        windowed, same_made, rows_stored = sem("windowed"), sem("same_made"), sem("rows_stored")
        block = ctx.enter_context(nc.Block())
        flat = lambda a: a.rearrange("(a e) -> a e", a=1)
        src_flat = src_pad.rearrange("c p -> (c p)")
        dst_flat = dst_pad.rearrange("c p -> (c p)")

        @block.vector
        def _(dve):
            nc.vector.memset(zero_i[:, :], 0)
            nc.vector.memset(far[:, :], PAD_DST)
            nc.vector.memset(before[:, :], -1).then_inc(pads, 1)
            dve.wait_ge(rows_loaded, 64)
            nc.vector.tensor_copy(src_f[:, :, :], src_i[:, :, :]).then_inc(rows_cast, 1)
            nc.vector.tensor_copy(dst_f[:, :, :], dst_i[:, :, :]).then_inc(rows_cast, 1)
            nc.vector.tensor_tensor(same[:, :, :], dst_i[:, :, :], before_i[:, :, :], ALU.is_equal).then_inc(same_made, 1)
            dve.wait_ge(turned, 12)
            nc.vector.tensor_copy(src_t[:, :], rows_ps[0][:, 0:CHUNKS]).then_inc(rows_cast, 1)
            for j in range(PHASES):
                nc.vector.tensor_copy(first_row[:, j, :], rows_ps[1][j * P // PHASES:j * P // PHASES + 1, 0:CHUNKS])
            nc.vector.tensor_scalar(dst_t[:, :], rows_ps[1][:, 0:CHUNKS], float(NP - 1), None, ALU.min).then_inc(rows_cast, 1)
            nc.vector.tensor_copy(w_t[:, :], rows_ps[2][:, 0:CHUNKS]).then_inc(rows_cast, 1)

        @block.sync
        def _(sp):
            sp.dma_start(flat(src_flat[0:E]), flat(src)).then_inc(padded, 16)
            sp.dma_start(flat(dst_flat[0:E]), flat(dst)).then_inc(padded, 16)
            sp.dma_start(flat(dst_ext[1:1 + E]), flat(dst)).then_inc(padded, 16)
            sp.dma_start(flat(w_pad[0:E]), flat(weight)).then_inc(padded, 16)
            sp.wait_ge(pads, 1)
            sp.dma_start(flat(src_flat[E:EP + P]), zero_i[:, 0:npad]).then_inc(padded, 16)
            sp.dma_start(flat(dst_flat[E:EP + P]), far[:, 0:npad]).then_inc(padded, 16)
            sp.dma_start(flat(dst_ext[1 + E:1 + EXT]), far[:, :]).then_inc(padded, 16)
            sp.dma_start(flat(dst_ext[0:1]), before[:, :]).then_inc(padded, 16)
            sp.dma_start(flat(w_pad[E:EXT]), zero_f).then_inc(padded, 16)
            sp.wait_ge(padded, 9 * 16)
            chunks = lambda a: a.rearrange("(a q) p -> q a p", q=quarter)
            sp.dma_start(src_i[:, :, :], chunks(src_pad[0:CHUNKS, :])).then_inc(rows_loaded, 16)
            sp.dma_start(dst_i[:, :, :], chunks(dst_pad[0:CHUNKS, :])).then_inc(rows_loaded, 16)
            sp.dma_start(w_f[:, :, :], chunks(w_pad[0:EP].rearrange("(c p) -> c p", p=P))).then_inc(rows_loaded, 16)
            sp.dma_start(before_i[:, :, :], chunks(dst_ext[0:EP].rearrange("(c p) -> c p", p=P))).then_inc(rows_loaded, 16)
            sp.dma_start(flat(same_dram[EP:EXT]), zero_i[:, 0:(EXT - EP) // 2].bitcast(F16)).then_inc(rows_stored, 16)
            sp.wait_ge(same_made, 1)
            sp.dma_start(chunks(same_dram[0:EP].rearrange("(c p) -> c p", p=P)), same[:, :, :]).then_inc(rows_stored, 16)
            sp.wait_ge(rows_cast, 5)
            sp.dma_start(src_cols, src_t[:, :]).then_inc(rows_stored, 16)
            sp.dma_start(dst_cols, dst_t[:, :]).then_inc(rows_stored, 16)
            sp.dma_start(w_cols, w_t[:, :]).then_inc(rows_stored, 16)
            sp.wait_ge(rows_stored, 80)

        @block.scalar
        def _(act):
            act.wait_ge(padded, 9 * 16)
            by_phase = win_dram.rearrange("(c j) l p -> j l c p", j=PHASES)
            for n, edges in enumerate((src_flat, dst_flat, w_pad.bitcast(I32))):
                for j in range(PHASES):
                    begin = j * P // PHASES
                    act.dma_start(by_phase[j, n, :, :], edges[begin:begin + EP].rearrange("(c p) -> c p", p=P)).then_inc(windowed, 16)
            act.wait_ge(windowed, 16 * 3 * PHASES)

        @block.tensor
        def _(pe):
            pe.wait_ge(rows_cast, 2)
            for rows, ps in zip((src_f, dst_f, w_f), rows_ps):
                for a in range(4):
                    nc.tensor.transpose(ps[:, a * quarter:(a + 1) * quarter], rows[:, a, :],
                                        c.ident[0:quarter, 0:quarter]).then_inc(turned, 1)


def adjacency_windows(nc, c, win_dram, first_row, tables, tables_dram, overflow):
    with stack() as ctx:
        sb = lambda name, shape, dt: ctx.enter_context(nc.sbuf_tensor("win_" + name, shape, dt))
        o_i, o_f = sb("o_i", [P, GT], I32), sb("o_f", [P, GT], F32)
        low, high = sb("low", [P, GT], F32), sb("high", [P, GT], F32)
        begin, end, over = sb("begin", [P, GT], F32), sb("end", [P, GT], F32), sb("over", [P, GT], F32)
        any_over = sb("any_over", [P, 1], F32)
        offset, below = sb("offset", [P, GT], F32), sb("below", [P, PHASES, CHUNKS], F16)
        row_f, row_i = sb("row_f", [P, GT, WIN], F32), sb("row_i", [P, GT, WIN], I32)
        edges = sb("edges", [P, GT, WIN, 3, P], I32)
        shape = [P, GT, WIN, P]
        int_part, tile_f = sb("int_part", shape, I32), sb("tile_f", shape, F32)
        lane_f, key_f = sb("lane_f", shape, F32), sb("key_f", shape, F32)
        weight16 = sb("weight16", [P, NSTEP], F16)
        first_ps = ctx.enter_context(nc.psum_tensor("win_first_ps", [P, PHASES, 512], F32))
        over_ps = ctx.enter_context(nc.psum_tensor("win_over_ps", [P, 512], F32))
        more_ps = [ctx.enter_context(nc.psum_tensor(f"win_more_ps{u}", [P, 512], F32)) for u in range(2)]
        turned_ps = [first_ps[:, n, :] for n in range(4)] + [ps[:, :] for ps in more_ps]
        sem = lambda name: ctx.enter_context(nc.semaphore("win_" + name))
        numbered, first_ready, d_step, over_kept, over_summed, row_ready, lanes_ready, keys_ready, turned, tables_kept, tables_stored = (
            sem("numbered"), sem("first_ready"), sem("step"), sem("over_kept"), sem("over_summed"), sem("row_ready"),
            sem("lanes_ready"), sem("keys_ready"), sem("turned"), sem("tables_kept"), sem("tables_stored"))
        gathered = c.gather_sem("win_gathered")
        block = ctx.enter_context(nc.Block())

        @block.gpsimd
        def _(pool):
            nc.gpsimd.iota(o_i[:, :], [[P, GT]], base=0, channel_multiplier=1).then_inc(numbered, 1)
            pool.wait_ge(row_ready, 1)
            for u in range(GT):
                for w in range(WIN):
                    nc.gpsimd.indirect_dma_start(edges[:, u, w, :, :].rearrange("p l e -> p (l e)"), None, win_dram.rearrange("r l p -> r (l p)"),
                                                 bass.IndirectOffsetOnAxis(ap=row_i[:, u, w:w + 1], axis=0)).then_inc(gathered, 16)
            pool.wait_ge(gathered, 16 * GT * WIN)

        @block.sync
        def _(sp):
            sp.wait_ge(tables_kept, 1)
            sp.dma_start(tables_dram, tables[:, :, :]).then_inc(tables_stored, 16)
            sp.wait_ge(tables_stored, 16)

        @block.vector
        def _(dve):
            done = [0]

            def then_wait(*ins):
                for i in ins:
                    done[0] += 1
                    i.then_inc(d_step, 1)
                dve.wait_ge(d_step, done[0])

            dve.wait_ge(numbered, 1)
            then_wait(nc.vector.tensor_copy(o_f[:, :], o_i[:, :]))
            then_wait(nc.vector.tensor_scalar(high[:, :], o_f[:, :], float(GROUP), float(GROUP), ALU.mult, ALU.add),
                      nc.vector.tensor_scalar(offset[:, :], o_f[:, :], float(-KEYS), None, ALU.mult),
                      nc.vector.tensor_scalar(low[:, :], o_f[:, :], float(GROUP), None, ALU.mult))
            then_wait(nc.vector.tensor_scalar(high[:, :], high[:, :], float(NP), None, ALU.min))
            dve.wait_ge(first_ready, 1)
            for limit, row in ((low, begin), (high, end)):
                for u in range(GT):
                    then_wait(nc.vector.tensor_scalar(below[:, :, :], first_ps[:, :, 0:CHUNKS], limit[:, u:u + 1], None, ALU.is_lt, ALU.add,
                                                      accum_out=row[:, u:u + 1]))
                then_wait(nc.vector.tensor_scalar(row[:, :], row[:, :], -1.0, 0.0, ALU.add, ALU.max))
            then_wait(*[nc.vector.tensor_scalar(row_f[:, :, w], begin[:, :], float(PHASES * w), float(WROWS - 1), ALU.add, ALU.min)
                        for w in range(WIN)])
            nc.vector.tensor_copy(row_i[:, :, :], row_f[:, :, :]).then_inc(row_ready, 1)
            then_wait(nc.vector.tensor_tensor(over[:, :], end[:, :], begin[:, :], ALU.subtract))
            then_wait(nc.vector.tensor_scalar(over[:, :], over[:, :], float(PHASES * WIN), None, ALU.is_ge))
            nc.vector.tensor_reduce(any_over[:, :], over[:, :], AX.X, ALU.add).then_inc(over_kept, 1)
            dve.wait_ge(over_summed, 1)
            nc.vector.tensor_copy(overflow[:, :], over_ps[0:1, 0:1])
            dve.wait_ge(gathered, 16 * GT * WIN)
            then_wait(nc.vector.tensor_scalar(int_part[:, :, :, :], edges[:, :, :, 0, :], P - 1, None, ALU.bitwise_and))
            then_wait(nc.vector.tensor_copy(lane_f[:, :, :, :], int_part[:, :, :, :]))
            dve.sem_inc(lanes_ready, 1)
            then_wait(nc.vector.tensor_scalar(int_part[:, :, :, :], edges[:, :, :, 0, :], 7, None, ALU.logical_shift_right))
            then_wait(nc.vector.tensor_copy(tile_f[:, :, :, :], int_part[:, :, :, :]),
                      nc.vector.tensor_copy(key_f[:, :, :, :], edges[:, :, :, 1, :]))
            for u in range(GT):
                then_wait(nc.vector.scalar_tensor_tensor(key_f[:, u, :, :], key_f[:, u, :, :], float(T), tile_f[:, u, :, :], ALU.mult, ALU.add))
                nc.vector.tensor_scalar(key_f[:, u, :, :], key_f[:, u, :, :], offset[:, u:u + 1], None, ALU.add).then_inc(keys_ready, 1)

            def keep(u, n, ps, table, scale):
                g = min(P, NGROUP - u * P)
                out = tables[:, table, u * P * WIN:(u * P + g) * WIN].rearrange("p (o w) -> p w o", w=WIN)
                return nc.vector.tensor_scalar(out, ps[:, 0:WIN * P].rearrange("p (w o) -> p w o", w=WIN)[:, :, 0:g], scale, None, ALU.mult)

            dve.wait_ge(turned, 3 * GT * WIN)
            then_wait(*[keep(u, n, turned_ps[n * GT + u], table, scale)
                        for n, (table, scale) in enumerate(((1, 1.0), (0, 1.0), (3, W_SCALE))) for u in range(GT)])
            then_wait(nc.vector.tensor_copy(weight16[:, :], tables[:, 3, :]))
            then_wait(nc.vector.tensor_copy(tables[:, 2, :], weight16[:, :]))
            then_wait(nc.vector.tensor_tensor(tables[:, 3, :], tables[:, 3, :], tables[:, 2, :], ALU.subtract))
            dve.sem_inc(tables_kept, 1)

        @block.tensor
        def _(pe):
            for j in range(PHASES):
                mm = nc.tensor.matmul(first_ps[:, j, 0:CHUNKS], c.ones[0:1, :], first_row[:, j, :], start=True, stop=True)
            mm.then_inc(first_ready, 1)
            pe.wait_ge(over_kept, 1)
            nc.tensor.matmul(over_ps[:, 0:1], c.ones[:, :], any_over[:, :], start=True, stop=True).then_inc(over_summed, 1)
            weight_f = edges[:, :, :, 2, :].bitcast(F32)
            for n, (table, ready, count) in enumerate(((lane_f, lanes_ready, 1), (key_f, keys_ready, GT), (weight_f, keys_ready, GT))):
                pe.wait_ge(ready, count)
                for u in range(GT):
                    for w in range(WIN):
                        nc.tensor.transpose(turned_ps[n * GT + u][:, w * P:(w + 1) * P], table[:, u, w, :], c.ident[:, :]).then_inc(turned, 1)


def build_adjacency(nc, c, adj, tables):
    TURN, RINGS = 8, 4
    with stack() as ctx:
        sb = lambda name, shape, dt: ctx.enter_context(nc.sbuf_tensor(name, shape, dt))
        lane_hot, key_hot = sb("lane_hot", [P, RINGS, WIN, P], F16), sb("key_hot", [P, RINGS, WIN, KEYS], F16)
        count_ps = [ctx.enter_context(nc.psum_tensor(f"count{i}", [P, 512], F32)) for i in range(2)]
        sem = lambda name: ctx.enter_context(nc.semaphore(name))
        hot_ready, counted, kept = sem("hot_ready"), sem("adj_counted"), sem("adj_kept")
        distance = sb("lane_distance", [P, 2, P], F16)
        distance_made, lane_made = sem("distance_made"), sem("lane_made")
        block = ctx.enter_context(nc.Block())

        @block.vector
        def _(dve):
            with dve.Fori(0, NGROUP // TURN) as i:
                for b in range(TURN):
                    dve.wait_ge(counted, TURN * i + b + 1)
                    for w in range(WIN):
                        at = bass.ds(TURN * WIN * i + WIN * b + w, 1)
                        if w:
                            nc.vector.tensor_scalar(lane_hot[:, b % RINGS, w, :], c.iota16[:, 0:P], tables[:, 1, at], None, ALU.is_equal)
                        nc.vector.tensor_scalar(key_hot[:, b % RINGS, w, :], c.iota16[:, :], tables[:, 0, at], None, ALU.is_equal).then_inc(hot_ready, 1)

        @block.tensor
        def _(pe):
            pe.sem_inc(counted, RINGS)
            with pe.Fori(0, NGROUP // TURN) as i:
                for b in range(TURN):
                    pe.wait_ge(kept, TURN * i + b + 1)
                    pe.wait_ge(lane_made, TURN * i + b + 1)
                    for w in range(WIN):
                        pe.wait_ge(hot_ready, TURN * WIN * i + WIN * b + w + 1)
                        mm = nc.tensor.matmul(count_ps[b % 2][:, 0:KEYS], lane_hot[:, b % RINGS, w, :], key_hot[:, b % RINGS, w, :], start=w == 0, stop=w == WIN - 1)
                    mm.then_inc(counted, 1)

        @block.scalar
        def _(act):
            def first_lanes(g, b):
                nc.scalar.activation(distance[:, b % 2, :], c.iota16[:, 0:P], ACT.Abs, scale=-1.0, bias=tables[:, 1, bass.ds(WIN * (g % NGROUP), 1)]).then_inc(distance_made, 1)
                act.wait_ge(distance_made, g + 1)
                nc.scalar.activation(lane_hot[:, b, 0, :], distance[:, b % 2, :], ACT.Relu, scale=-1.0, bias=c.ones[:, 0:1]).then_inc(lane_made, 1)

            act.sem_inc(kept, 2)
            for b in range(RINGS):
                first_lanes(b, b)
            with act.Fori(0, NGROUP // TURN) as i:
                for b in range(TURN):
                    act.wait_ge(counted, TURN * i + b + RINGS + 1)
                    nc.scalar.activation(adj[:, :, bass.ds(TURN * GROUP * i + GROUP * b, GROUP)],
                                         count_ps[b % 2][:, 0:KEYS].rearrange("p (d k) -> p k d", d=GROUP), ACT.Copy).then_inc(kept, 1)
                    first_lanes(TURN * i + b + RINGS, b % RINGS)


def walk_adjacency(nc, c, adj, overflow, src_pad, dst_pad, group_dram):
    pairs = (STEPS - 1) // 2
    assert STEPS == 2 * pairs + 1
    half = T // 2
    with stack() as ctx:
        sb = lambda name, shape, dt: ctx.enter_context(nc.sbuf_tensor("walk_" + name, shape, dt))
        key_of, lane_of, group_row = sb("key_of", [P, SPAD], F32), sb("lane_of", [P, SPAD], F32), sb("group_row", [1, SPAD], I32)
        lane_hot = [sb(f"lane_hot{i}", [P, P], F16) for i in range(2)]
        key_hot = [sb(f"key_hot{i}", [P, KEYS], F16) for i in range(2)]
        dst_i, dst_f = sb("dst_i", [P, CHUNKS], I32), sb("dst_f", [P, CHUNKS], F32)
        below = sb("below", [P, CHUNKS], F32)
        o_i, o_f, limit = sb("o_i", [P, NGROUP], I32), sb("o_f", [P, NGROUP], F32), sb("limit", [P, NGROUP], F32)
        count = sb("count", [P, NGROUP], F32)
        first_i, first = sb("first_i", [P, NGROUP], I32), sb("first", [P, NGROUP], F32)
        s_i, s_f = sb("s_i", [P, STILES], I32), sb("s_f", [P, STILES], F32)
        group, offset = sb("group", [P, STILES], F32), sb("offset", [P, STILES], F32)
        chunk_f, chunk_i = sb("chunk_f", [P, STILES], F32), sb("chunk_i", [P, STILES], I32)
        src_g, dst_g = sb("src_g", [P, STILES, P], I32), sb("dst_g", [P, STILES, P], I32)
        tile_i, tile_f = sb("tile_i", [P, STILES, P], I32), sb("tile_f", [P, STILES, P], F32)
        lane_i, lane_f = sb("lane_i", [P, STILES, P], I32), sb("lane_f", [P, STILES, P], F32)
        key_f = sb("key_f", [P, STILES, P], F32)
        group_i = sb("group_i", [STILES, P], I32)
        ps = [ctx.enter_context(nc.psum_tensor(f"walk_ps{i}", [P, 512], F32)) for i in range(6)]
        part_ps = [ctx.enter_context(nc.psum_tensor(f"walk_part{i}", [P, 512], F32)) for i in range(2)]
        sem = lambda name: ctx.enter_context(nc.semaphore("walk_" + name))
        loaded, numbered, d_step, counted, summed, chunk_ready, keyed, turned, o_turned, o_cast, o_stored = (
            sem("loaded"), sem("numbered"), sem("step"), sem("counted"), sem("summed"), sem("chunk"), sem("keyed"),
            sem("turned"), sem("oturned"), sem("ocast"), sem("ostored"))
        zeroed, hot_ready, part_ready, added = sem("zeroed"), sem("hot_ready"), sem("part_ready"), sem("added")
        gathered = c.gather_sem("walk_gathered")
        block = ctx.enter_context(nc.Block())
        taken = lambda eng: eng.value_load(overflow[0:1, 0:1], min_val=0, max_val=NP) > 0

        @block.sync
        def _(sp):
            with sp.If(taken(sp)):
                sp.dma_start(dst_i[:, :], dst_pad[0:CHUNKS, :].rearrange("c p -> (c p)").rearrange("(p c) -> p c", p=P)).then_inc(loaded, 16)
                sp.wait_ge(o_cast, 1)
                sp.dma_start(group_dram.rearrange("(t p) -> t p", p=P), group_i[:, :]).then_inc(o_stored, 16)
                sp.wait_ge(o_stored, 16)
                sp.dma_start(group_row[:, :], group_dram.rearrange("(a s) -> a s", a=1)).then_inc(o_stored, 16)
                sp.wait_ge(o_stored, 32)

        @block.gpsimd
        def _(pool):
            with pool.If(taken(pool)):
                nc.gpsimd.memset(adj[:, 0:half, :], 0.0).then_inc(zeroed, 1)
                nc.gpsimd.iota(o_i[:, :], [[1, NGROUP]], base=0, channel_multiplier=0).then_inc(numbered, 1)
                nc.gpsimd.iota(s_i[:, :], [[P, STILES]], base=0, channel_multiplier=1).then_inc(numbered, 1)
                pool.wait_ge(chunk_ready, 1)
                for t in range(STILES):
                    at = bass.IndirectOffsetOnAxis(ap=chunk_i[:, t:t + 1], axis=0)
                    nc.gpsimd.indirect_dma_start(src_g[:, t, :], None, src_pad, at).then_inc(gathered, 16)
                    nc.gpsimd.indirect_dma_start(dst_g[:, t, :], None, dst_pad, at).then_inc(gathered, 16)
                pool.wait_ge(gathered, 32 * STILES)

        @block.vector
        def _(dve):
            done = [0]

            def then_wait(ins):
                done[0] += 1
                ins.then_inc(d_step, 1)
                dve.wait_ge(d_step, done[0])

            def schedule():
                dve.wait_ge(numbered, 2)
                nc.vector.tensor_copy(s_f[:, :], s_i[:, :])
                then_wait(nc.vector.tensor_copy(o_f[:, :], o_i[:, :]))
                then_wait(nc.vector.tensor_scalar(limit[:, :], o_f[:, :], float(GROUP), None, ALU.mult))
                dve.wait_ge(loaded, 16)
                then_wait(nc.vector.tensor_copy(dst_f[:, :], dst_i[:, :]))
                with dve.Fori(0, NGROUP) as o:
                    nc.vector.tensor_scalar(below[:, :], dst_f[:, :], limit[:, bass.ds(o, 1)], None, ALU.is_lt, ALU.add,
                                            accum_out=count[:, bass.ds(o, 1)]).then_inc(counted, 1)
                    dve.wait_ge(counted, o + 1)
                dve.wait_ge(summed, 1)
                then_wait(nc.vector.tensor_copy(first_i[:, :], ps[0][:, 0:NGROUP]))
                then_wait(nc.vector.tensor_scalar(first_i[:, :], first_i[:, :], 7, None, ALU.logical_shift_right))
                then_wait(nc.vector.tensor_copy(first[:, :], first_i[:, :]))
                then_wait(nc.vector.tensor_tensor(first[:, :], first[:, :], o_f[:, :], ALU.add))
                for t in range(STILES):
                    then_wait(nc.vector.tensor_scalar(below[:, 1:NGROUP], first[:, 1:NGROUP], s_f[:, t:t + 1], None, ALU.is_le, ALU.add,
                                                      accum_out=group[:, t:t + 1]))
                then_wait(nc.vector.tensor_tensor(chunk_f[:, :], s_f[:, :], group[:, :], ALU.subtract))
                then_wait(nc.vector.tensor_scalar(chunk_f[:, :], chunk_f[:, :], float(CHUNKS - 1), None, ALU.min))
                then_wait(nc.vector.tensor_copy(chunk_i[:, :], chunk_f[:, :]))
                dve.sem_inc(chunk_ready, 1)
                then_wait(nc.vector.tensor_scalar(offset[:, :], group[:, :], float(-KEYS), None, ALU.mult))
                then_wait(nc.vector.tensor_scalar(group[:, :], group[:, :], float(GROUP), None, ALU.mult))
                nc.vector.tensor_copy(chunk_f[:, :], group[:, :]).then_inc(keyed, 1)
                dve.wait_ge(o_turned, 1)
                nc.vector.tensor_copy(group_i[:, :], ps[1][0:STILES, 0:P]).then_inc(o_cast, 1)
                dve.wait_ge(gathered, 32 * STILES)
                nc.vector.tensor_scalar(tile_i[:, :, :], src_g[:, :, :], 7, None, ALU.logical_shift_right)
                then_wait(nc.vector.tensor_scalar(lane_i[:, :, :], src_g[:, :, :], P - 1, None, ALU.bitwise_and))
                nc.vector.tensor_copy(lane_f[:, :, :], lane_i[:, :, :])
                nc.vector.tensor_copy(tile_f[:, :, :], tile_i[:, :, :])
                then_wait(nc.vector.tensor_copy(key_f[:, :, :], dst_g[:, :, :]))
                for t in range(STILES):
                    then_wait(nc.vector.scalar_tensor_tensor(key_f[:, t, :], key_f[:, t, :], float(T), tile_f[:, t, :], ALU.mult, ALU.add))
                    nc.vector.tensor_scalar(key_f[:, t, :], key_f[:, t, :], offset[:, t:t + 1], None, ALU.add).then_inc(keyed, 1)
                dve.wait_ge(turned, 2 * STILES)
                for t in range(STILES):
                    bank = 2 + (t // 4) * 2
                    nc.vector.tensor_copy(lane_of[:, t * P:(t + 1) * P], ps[bank + 1][:, (t % 4) * P:(t % 4 + 1) * P])
                    then_wait(nc.vector.tensor_copy(key_of[:, t * P:(t + 1) * P], ps[bank][:, (t % 4) * P:(t % 4 + 1) * P]))
                dve.wait_ge(o_stored, 32)

            def one_hot(s, b, first):
                if not first:
                    dve.wait_ge(part_ready, s - 1)
                nc.vector.tensor_scalar(lane_hot[b][:, :], c.iota16[:, 0:P], lane_of[:, bass.ds(s, 1)], None, ALU.is_equal)
                nc.vector.tensor_scalar(key_hot[b][:, :], c.iota16[:, :], key_of[:, bass.ds(s, 1)], None, ALU.is_equal).then_inc(hot_ready, 1)

            def add(s, b, first=False):
                g = nc.values_load(group_row[0:1, bass.ds(s, 1)], engines=(mybir.EngineType.DVE,), min_val=0, max_val=NP - GROUP,
                                   skip_runtime_bounds_check_because="a step's group is below NGROUP")
                columns = adj[:, :, bass.ds(g, GROUP)]
                dve.wait_ge(part_ready, s + 1)
                if not first:
                    dve.wait_ge(added, s)
                nc.vector.tensor_tensor(columns, columns, part_ps[b][:, 0:KEYS].rearrange("p (d k) -> p k d", d=GROUP),
                                        ALU.add).then_inc(added, 1)

            with dve.If(taken(dve)):
                nc.vector.memset(adj[:, half:T, :], 0.0).then_inc(zeroed, 1)
                schedule()
                dve.wait_ge(zeroed, 2)
                one_hot(0, 0, True)
                one_hot(1, 1, True)
                add(0, 0, True)
                one_hot(2, 0, False)
                add(1, 1)
                with dve.Fori(1, pairs) as i:
                    one_hot(2 * i + 1, 1, False)
                    add(2 * i, 0)
                    one_hot(2 * i + 2, 0, False)
                    add(2 * i + 1, 1)
                add(STEPS - 1, 0)

        @block.tensor
        def _(pe):
            def product(s, b, first):
                pe.wait_ge(hot_ready, s + 1)
                if not first:
                    pe.wait_ge(added, s - 1)
                nc.tensor.matmul(part_ps[b][:, 0:KEYS], lane_hot[b][:, :], key_hot[b][:, :],
                                 start=True, stop=True).then_inc(part_ready, 1)

            with pe.If(taken(pe)):
                pe.wait_ge(counted, NGROUP)
                nc.tensor.matmul(ps[0][:, 0:NGROUP], c.ones[:, :], count[:, :], start=True, stop=True).then_inc(summed, 1)
                pe.wait_ge(keyed, 1)
                nc.tensor.transpose(ps[1][0:STILES, 0:P], chunk_f[:, :], c.ident[:, :]).then_inc(o_turned, 1)
                for t in range(STILES):
                    pe.wait_ge(keyed, t + 2)
                    bank = 2 + (t // 4) * 2
                    nc.tensor.transpose(ps[bank][:, (t % 4) * P:(t % 4 + 1) * P], key_f[:, t, :], c.ident[:, :]).then_inc(turned, 1)
                    nc.tensor.transpose(ps[bank + 1][:, (t % 4) * P:(t % 4 + 1) * P], lane_f[:, t, :], c.ident[:, :]).then_inc(turned, 1)
                product(0, 0, True)
                product(1, 1, True)
                with pe.Fori(1, pairs) as i:
                    product(2 * i, 0, False)
                    product(2 * i + 1, 1, False)
                product(STEPS - 1, 0, False)


def degrees(nc, c, deg_ps):
    with stack() as ctx:
        sb = lambda name, shape, dt: ctx.enter_context(nc.sbuf_tensor(name, shape, dt))
        upper = sb("upper", [P, P], F32)
        total, before, last, has = sb("total", [P, T], F32), sb("before_t", [P, T], F32), sb("last", [P, T], F32), sb("has", [P, T], F32)
        cum_ps = ctx.enter_context(nc.psum_tensor("cum_ps", [P, 512], F32))
        tot_ps = ctx.enter_context(nc.psum_tensor("tot_ps", [P, 512], F32))
        sem = lambda name: ctx.enter_context(nc.semaphore(name))
        deg_kept, cum_ready, d_step = sem("deg_kept"), sem("cum_ready"), sem("deg_step")
        upper_made = sem("upper_made")
        block = ctx.enter_context(nc.Block())

        @block.gpsimd
        def _(pool):
            nc.gpsimd.affine_select(out=upper[:, :], in_=c.ones[:, :], compare_op=ALU.is_ge, fill=0.0,
                                    base=0, pattern=[[1, P]], channel_multiplier=-1).then_inc(upper_made, 1)

        @block.tensor
        def _(pe):
            pe.wait_ge(deg_kept, 1)
            pe.wait_ge(upper_made, 1)
            nc.tensor.matmul(cum_ps[:, 0:T], upper[:, :], c.deg[:, :], start=True, stop=True).then_inc(cum_ready, 1)
            nc.tensor.matmul(tot_ps[:, 0:T], c.ones[:, :], c.deg[:, :], start=True, stop=True).then_inc(cum_ready, 1)

        @block.vector
        def _(dve):
            done = [0]

            def then_wait(ins):
                done[0] += 1
                ins.then_inc(d_step, 1)
                dve.wait_ge(d_step, done[0])

            nc.vector.tensor_copy(c.deg[:, :], deg_ps[:, 0:T]).then_inc(deg_kept, 1)
            dve.wait_ge(cum_ready, 2)
            then_wait(nc.vector.tensor_copy(total[:, :], tot_ps[:, 0:T]))
            then_wait(nc.vector.tensor_tensor_scan(before[:, :], c.ones[:, 0:T], total[:, :], 0.0, ALU.mult, ALU.add))
            then_wait(nc.vector.tensor_tensor(before[:, :], before[:, :], total[:, :], ALU.subtract))
            then_wait(nc.vector.tensor_tensor(last[:, :], before[:, :], cum_ps[:, 0:T], ALU.add))
            nc.vector.tensor_scalar(has[:, :], c.deg[:, :], 0.0, None, ALU.is_gt)
            then_wait(nc.vector.tensor_scalar(last[:, :], last[:, :], float(-1 - ZERO_ROW), None, ALU.add))
            then_wait(nc.vector.tensor_tensor(last[:, :], last[:, :], has[:, :], ALU.mult))
            then_wait(nc.vector.tensor_scalar(last[:, :], last[:, :], float(ZERO_ROW), None, ALU.add))
            nc.vector.tensor_copy(c.end_row[:, :], last[:, :])


def attention(nc, c, adj, q_dram, k_dram, v_dram, res_dram):
    RINGS, E_RINGS = 3, 5

    def ring(n):
        buf = [t % n for t in range(T)]
        if buf[T - 1] == 0:
            buf[T - 1] = next(b for b in range(1, n) if b not in buf[T + 1 - n:T - 1])
        return buf

    def last_use(buf, t):
        return max(u for u in range(t - T, t) if buf[u % T] == buf[t])

    buf, e_buf = ring(RINGS), ring(E_RINGS)
    GIVEN = 6
    with stack() as ctx:
        sb = lambda name, shape, dt: ctx.enter_context(nc.sbuf_tensor(name, shape, dt))
        k_st = sb("k_all", [D, T, 512], F16)
        v_all = sb("v_all2", [P, T, HEADS, DH + 1], F32)
        q_st = sb("q_tile", [D, 2, 512], F16)
        e = sb("e", [P, E_RINGS, 512], F32)
        o_sb = sb("o_sb", [DH + 1, 512], F32)
        first_exp = sb("first_exp", [P, 1], F32)
        inv = sb("inv", [P, HEADS], F32)
        res = sb("res", [P, HEADS, DH], F32)
        s_ps = [ctx.enter_context(nc.psum_tensor(f"s_ps{i}", [P, 512], F32)) for i in range(RINGS)]
        a_ps = [ctx.enter_context(nc.psum_tensor(f"a_ps{i}", [P, 1024], F16)) for i in range(RINGS)]
        o_ps = ctx.enter_context(nc.psum_tensor("o_ps", [P, 512], F32))
        r_ps = ctx.enter_context(nc.psum_tensor("r_ps", [P, 512], F32))
        sem = lambda name: ctx.enter_context(nc.semaphore(name))
        kv_loaded, q_loaded, scored, clipped, exped, weighted, summed, o_kept, o_turned, res_ready, res_stored, d_step, turn_begun = (
            sem("kv_loaded"), sem("q_loaded"), sem("scored"), sem("clipped"), sem("exped"), sem("weighted"), sem("summed"),
            sem("o_kept"), sem("o_turned"), sem("res_ready"), sem("res_stored"), sem("att_step"), sem("turn_begun"))
        block = ctx.enter_context(nc.Block())

        @block.sync
        def _(sp):
            sp.dma_start(k_st[:, :, :], k_dram).then_inc(kv_loaded, 16)
            sp.dma_start(v_all[:, :, :, :].rearrange("p t h f -> p (t h f)"), v_dram).then_inc(kv_loaded, 16)
            sp.dma_start(q_st[:, 0, :], q_dram[:, 0, :]).then_inc(q_loaded, 16)
            with sp.Fori(0, T) as i:
                sp.wait_ge(scored, T * i + GIVEN)
                sp.wait_ge(q_loaded, 16 * (i + 1))
                sp.dma_start(q_st[:, bass.ds((i + 1) % 2, 1), :].rearrange("p a n -> p (a n)"),
                             q_dram[:, bass.ds((i + 1) % T, 1), :].rearrange("p a n -> p (a n)")).then_inc(q_loaded, 16)
                sp.wait_ge(res_ready, i + 1)
                sp.dma_start(res_dram[:, bass.ds(i * D, D)], res[:, :, :].rearrange("p h f -> p (h f)")).then_inc(res_stored, 16)
            sp.wait_ge(res_ready, T + 1)
            sp.dma_start(res_dram[:, T * D:(T + 1) * D], res[:, :, :].rearrange("p h f -> p (h f)")).then_inc(res_stored, 16)
            sp.wait_ge(res_stored, 16 * (T + 2))
            sp.wait_ge(q_loaded, 16 * (T + 1))

        @block.gpsimd
        def _(pool):
            pool.sem_inc(res_stored, 16)

        @block.tensor
        def _(pe):
            def score(i, t, given):
                pe.wait_ge(weighted, given + last_use(buf, t) + 1 + GIVEN)
                nc.tensor.transpose(a_ps[buf[t]][:, 0:P], adj[:, bass.ds(i, 1), t * P:(t + 1) * P].rearrange("p a n -> p (a n)"), c.ident16[:, :])
                pe.wait_ge(exped, given + last_use(buf, t) + 1 + GIVEN)
                q = q_st[:, bass.ds(i % 2, 1), :].rearrange("p a n -> p (a n)")
                for hd in range(HEADS):
                    mm = nc.tensor.matmul(s_ps[buf[t]][:, hd * P:(hd + 1) * P], k_st[:, t, hd * P:(hd + 1) * P],
                                          q[:, hd * P:(hd + 1) * P], start=True, stop=True)
                mm.then_inc(scored, 1)

            def value(i, t):
                pe.wait_ge(weighted, T * i + t + 1 + GIVEN)
                if t == 0:
                    pe.wait_ge(o_kept, i + 1)
                for hd in range(HEADS):
                    mm = nc.tensor.matmul(o_ps[0:DH + 1, hd * P:(hd + 1) * P], v_all[:, t, hd, :], e[:, e_buf[t], hd * P:(hd + 1) * P],
                                          start=t == 0 and hd == 0, stop=t == T - 1 and hd == HEADS - 1, skip_group_check=True)
                mm.then_inc(summed, 1)

            def turn_sums():
                pe.sem_inc(turn_begun, 1)
                for hd in range(HEADS):
                    tr = nc.tensor.transpose(r_ps[:, hd * (DH + 1):(hd + 1) * (DH + 1)], o_sb[:, hd * P:(hd + 1) * P], c.ident[0:DH + 1, 0:DH + 1])
                tr.then_inc(o_turned, 1)

            pe.sem_inc(scored, GIVEN)
            pe.wait_ge(kv_loaded, 32)
            for hd in range(HEADS):
                mm = nc.tensor.matmul(o_ps[0:DH + 1, hd * P:(hd + 1) * P], v_all[:, 0, hd, :], c.ident[:, :], start=True, stop=True)
            mm.then_inc(summed, GIVEN)
            pe.wait_ge(q_loaded, 16)
            score(0, 0, 0)
            score(0, 1, 0)
            with pe.Fori(0, T) as i:
                for t in range(T):
                    if t + 2 < T:
                        score(i, t + 2, T * i)
                    else:
                        if t + 2 == T:
                            pe.wait_ge(q_loaded, 16 * (i + 2))
                        score((i + 1) % T, t + 2 - T, T * i + T)
                    value(i, t)
                    if t == 1:
                        pe.wait_ge(o_kept, i + 1)
                        turn_sums()
            pe.wait_ge(o_kept, T + 1)
            turn_sums()

        @block.scalar
        def _(act):
            def exp(t, given):
                act.wait_ge(scored, given + t + 1 + GIVEN)
                act.wait_ge(summed, given + last_use(e_buf, t) + 1 + GIVEN)
                nc.scalar.activation(e[:, e_buf[t], :], s_ps[buf[t]][:, :], ACT.Exp).then_inc(exped, 1)

            nc.scalar.activation(first_exp[:, :], c.ones[:, 0:1], ACT.Exp)
            act.sem_inc(exped, GIVEN)
            with act.Fori(0, T) as i:
                for t in range(T):
                    exp(t, T * i)
                    if t == 1:
                        act.wait_ge(summed, T * i + GIVEN)
                        nc.scalar.activation(o_sb[:, :], o_ps[0:DH + 1, :], ACT.Copy).then_inc(o_kept, 1)
                    if t == 4:
                        act.wait_ge(o_turned, i + 1)
            act.wait_ge(summed, T * T + GIVEN)
            nc.scalar.activation(o_sb[:, :], o_ps[0:DH + 1, :], ACT.Copy).then_inc(o_kept, 1)

        @block.vector
        def _(dve):
            def clip(t, given):
                dve.wait_ge(exped, given + t + 1 + GIVEN)
                nc.vector.tensor_scalar(e[:, e_buf[t], :], e[:, e_buf[t], :], math.exp(10.0), math.exp(-10.0), ALU.min, ALU.max).then_inc(clipped, 1)

            def weight(i, t):
                dve.wait_ge(clipped, T * i + t + 1)
                tile = e[:, e_buf[t], :].rearrange("p (h n) -> p h n", h=HEADS)
                nc.vector.tensor_tensor(tile, tile, a_ps[buf[t]][:, 0:P].unsqueeze(1).to_broadcast([P, HEADS, P]),
                                        ALU.mult).then_inc(weighted, 1)

            def divide(i):
                dve.wait_ge(o_turned, i + 1)
                sums = r_ps[:, 0:HEADS * (DH + 1)].rearrange("p (h f) -> p h f", h=HEADS)
                nc.vector.tensor_scalar(inv[:, :], sums[:, :, DH], 1e-8, None, ALU.add).then_inc(d_step, 1)
                dve.wait_ge(d_step, 2 * i + 1)
                nc.vector.reciprocal(inv[:, :], inv[:, :]).then_inc(d_step, 1)
                dve.wait_ge(d_step, 2 * i + 2)
                dve.wait_ge(res_stored, 16 * (i + 1))
                nc.vector.tensor_tensor(res[:, :, :], sums[:, :, 0:DH], inv[:, :].unsqueeze(2).to_broadcast([P, HEADS, DH]),
                                        ALU.mult).then_inc(res_ready, 1)

            dve.sem_inc(weighted, GIVEN)
            with dve.Fori(0, T) as i:
                for t in range(T):
                    clip(t, T * i)
                    weight(i, t)
                    if t == 3:
                        divide(i)
            divide(T)


QUARTER = 4
HALF = QUARTER * GROUP
PIECES = (7, 6, 6, 6)


def max_pass(nc, c, name, table_dram, src_cols, same_dram, rows_dram, tables_dram, weights_dram, part):
    assert LOOPS == T and RING == QUARTER and HALF * 2 == P and sum(PIECES) == T
    with stack() as ctx:
        sb = lambda n, shape, dt: ctx.enter_context(nc.sbuf_tensor(f"{name}_{n}", shape, dt))
        ps = lambda n: ctx.enter_context(nc.psum_tensor(f"{name}_{n}", [P, 512], F32))
        sem = lambda n: ctx.enter_context(nc.semaphore(f"{name}_{n}"))
        index = [sb(f"index{i}", [P, 8], I32) for i in range(2)]
        row = [sb(f"row{i}", [P, 4, D], F32) for i in range(RING)]
        src_rows = sb("src_rows", [P, CHUNKS], I32)
        same = [sb(f"same{i}", [D, BLK], F16) for i in range(2)]
        run = [sb(f"run{i}", [D, BLK], F32) for i in range(2)]
        out = [sb(f"out{i}", [P, 4, D], F32) for i in range(2)]
        col_ps = [ps(f"col{i}") for i in range(2)]
        back_ps = [ps(f"back{i}") for i in range(2)]
        index_ready = sem("index_ready")
        gathered = [c.gather_sem(f"{name}_gathered{i}") for i in range(RING)]
        listed = [sem(f"listed{i}") for i in range(2)]
        written = [sem(f"written{i}") for i in range(2)]
        turned, scanned, listed_src, back, kept, zero_out, gather_begun = (
            sem("turned"), sem("scanned"), sem("listed_src"), sem("back"), sem("kept"), sem("zero_out"), sem("gather_begun"))
        steps = QUARTER * WIN
        tables = sb("tables", [P, 4, T, steps], F32)
        key_hot = sb("key_hot", [P, WIN, KEYS], F16)
        lane_w = sb("lane_w", [P, WIN, 2, P], F16)
        strip = sb("strip", [P, 2, T, 2, HALF], F16)
        rows_w = sb("rows_w", [P, T, P], F16)
        strip_ps = [ps(f"strip_ps{i}") for i in range(2)]
        piece_ps = [ctx.enter_context(nc.psum_tensor(f"{name}_piece{i}", [P, 1024], F16)) for i in range(2)]
        tables_loaded, hots_ready, hots_used, hi_kept, lo_kept, piece_turned, piece_kept, rows_stored, cleared = (
            sem("tables_loaded"), sem("hots_ready"), sem("hots_used"), sem("hi_kept"), sem("lo_kept"),
            sem("piece_turned"), sem("piece_kept"), sem("rows_stored"), sem("cleared"))
        block = ctx.enter_context(nc.Block())
        first_tile = [sum(PIECES[:n]) for n in range(len(PIECES))]
        strip_at = lambda h, i: strip[:, bass.ds(i % 2, 1), :, h, :].rearrange("p a k d -> p (a k) d")

        @block.gpsimd
        def _(pool):
            pool.wait_ge(listed_src, 16)

            def gather(i, b):
                if b % 2 == 0:
                    pool.wait_ge(turned, RING * i + b + 2)
                    nc.gpsimd.tensor_copy(index[b // 2][:, :], src_rows[:, bass.ds(4 * RING * i + 4 * b, 8)]).then_inc(index_ready, 1)
                    pool.wait_ge(index_ready, 2 * i + b // 2 + 1)
                    pool.sem_inc(gather_begun, 1)
                for j in range(4):
                    nc.gpsimd.indirect_dma_start(row[b][:, j, :], None, table_dram,
                                                 bass.IndirectOffsetOnAxis(ap=index[b // 2][:, 4 * (b % 2) + j:4 * (b % 2) + j + 1], axis=0)
                                                 ).then_inc(gathered[b], 16)

            with pool.Fori(0, LOOPS - 1) as i:
                for b in range(RING):
                    gather(i, b)
            for b in range(LAST_BLOCKS):
                gather(LOOPS - 1, b)
            for b in range(RING):
                pool.wait_ge(gathered[b], 64 * (LOOPS if b < LAST_BLOCKS else LOOPS - 1))

        @block.tensor
        def _(pe):
            def lay_out(i, g):
                pe.wait_ge(lo_kept, QUARTER * i + g + 1)
                for w in range(WIN):
                    s = WIN * g + w
                    pe.wait_ge(hots_ready, steps * i + s + 1)
                    for h in range(2):
                        mm = nc.tensor.matmul(strip_ps[g % 2][:, 0:KEYS], lane_w[:, w, h, :], key_hot[:, w, :],
                                              start=w == 0 and h == 0, stop=w == WIN - 1 and h == 1)
                    mm.then_inc(hots_used, 1)

            def turn(i, q):
                pe.wait_ge(piece_kept, 4 * i + q + 1)
                for k in range(PIECES[q]):
                    tr = nc.tensor.transpose(piece_ps[q % 2][:, k * P:(k + 1) * P],
                                             strip[:, bass.ds((i + 1) % 2, 1), first_tile[q] + k, :, :].rearrange("p a h d -> p (a h d)"), c.ident16[:, :])
                tr.then_inc(piece_turned, 1)

            pe.sem_inc(turned, RING)
            pe.sem_inc(back, 2)
            pe.sem_inc(piece_turned, 4)
            pe.wait_ge(cleared, 1)
            def round_of(i, last=False):
                for b in range(RING):
                    n = RING * i + b
                    if not last or b < LAST_BLOCKS:
                        pe.wait_ge(gathered[b], 64 * (i + 1))
                    pe.wait_ge(scanned, n + 1)
                    for j in range(4):
                        tr = nc.tensor.transpose(col_ps[b % 2][0:D, j * P:(j + 1) * P], row[b][:, j, :], c.ident[:, :])
                    tr.then_inc(turned, 1)
                    lay_out(i, b)
                    if b == 0:
                        pe.wait_ge(lo_kept, QUARTER * i + 2)
                    turn(i, b)
                    pe.wait_ge(scanned, n + 3)
                    pe.wait_ge(kept, n + 1)
                    for j in range(4):
                        tr = nc.tensor.transpose(back_ps[b % 2][:, j * D:(j + 1) * D], run[b % 2][:, j * P:(j + 1) * P], c.ident[0:D, 0:D])
                    tr.then_inc(back, 1)

            with pe.Fori(0, LOOPS - 1) as i:
                round_of(i)
            round_of(LOOPS - 1, last=True)
            pe.wait_ge(lo_kept, QUARTER * T + 2)
            for q in range(4):
                turn(T, q)

        @block.vector
        def _(dve):
            def hots(i, g, given):
                for w in range(WIN):
                    s = WIN * g + w
                    at = lambda n: tables[:, n, bass.ds(i, 1), s]
                    dve.wait_ge(hots_used, given + s + 1)
                    nc.vector.tensor_scalar(key_hot[:, w, :], c.iota16[:, :], at(0), None, ALU.is_equal)
                    for h in range(2):
                        one_hot = nc.vector.tensor_scalar(lane_w[:, w, h, :], c.iota16[:, 0:P], at(1), at(2 + h), ALU.is_equal, ALU.mult)
                    one_hot.then_inc(hots_ready, 1)

            def low_part(i, g):
                dve.wait_ge(hi_kept, QUARTER * i + g + 1)
                d = slice(g * GROUP, (g + 1) * GROUP)
                nc.vector.tensor_tensor(strip_at(1, i)[:, :, d], strip_ps[g % 2][:, 0:KEYS].rearrange("p (d k) -> p k d", d=GROUP),
                                        strip_at(0, i)[:, :, d], ALU.subtract).then_inc(lo_kept, 1)

            dve.sem_inc(lo_kept, 2)
            nc.vector.memset(run[1][:, BLK - 1:BLK], 0.0).then_inc(scanned, 2)
            dve.wait_ge(scanned, 2)
            nc.vector.memset(strip[:, 1, :, :, :], 0.0).then_inc(cleared, 1)
            dve.wait_ge(tables_loaded, 64)
            hots(0, 0, 0)
            with dve.Fori(0, LOOPS) as i:
                for b in range(RING):
                    n = RING * i + b
                    dve.wait_ge(listed[b % 2], 16 * (2 * i + b // 2 + 1))
                    dve.wait_ge(turned, n + RING + 1)
                    dve.wait_ge(back, n + 1)
                    dve.wait_ge(scanned, n + 2)
                    nc.vector.tensor_tensor_scan(run[b % 2][:, :], same[b % 2][:, :], col_ps[b % 2][0:D, :],
                                                 run[1 - b % 2][:, BLK - 1:BLK], ALU.mult, ALU.max).then_inc(scanned, 1)
                    if b + 1 < RING:
                        hots(i, b + 1, steps * i)
                    else:
                        hots((i + 1) % T, 0, steps * i + steps)
                    low_part(i, b)

        @block.scalar
        def _(act):
            def high_part(i, g):
                act.wait_ge(hots_used, steps * i + WIN * (g + 2))
                if g == 0:
                    act.wait_ge(piece_turned, 4 * i + 4)
                nc.scalar.activation(strip_at(0, i)[:, :, g * GROUP:(g + 1) * GROUP],
                                     strip_ps[g % 2][:, 0:KEYS].rearrange("p (d k) -> p k d", d=GROUP), ACT.Copy).then_inc(hi_kept, 1)

            def keep_piece(i, q):
                act.wait_ge(piece_turned, 4 * i + q + 5)
                if q == 0:
                    act.wait_ge(rows_stored, 16 * (i + 1))
                nc.scalar.activation(rows_w[:, first_tile[q]:first_tile[q] + PIECES[q], :].rearrange("d k p -> d (k p)"),
                                     piece_ps[q % 2][:, 0:PIECES[q] * P], ACT.Copy).then_inc(piece_kept, 1)

            act.sem_inc(kept, 2)
            act.sem_inc(hots_used, WIN)
            act.sem_inc(piece_kept, 2)
            with act.Fori(0, LOOPS) as i:
                for b in range(RING):
                    high_part(i, b)
                    keep_piece(i, b)
                    act.wait_ge(back, RING * i + b + 3)
                    act.wait_ge(written[b % 2], 16 * (2 * i + b // 2 + 1))
                    nc.scalar.activation(out[b % 2][:, :, :].rearrange("p j d -> p (j d)"), back_ps[b % 2][:, 0:4 * D], ACT.Copy).then_inc(kept, 1)
            for q in range(4):
                keep_piece(T, q)

        @block.sync
        def _(sp):
            def store_rows(i):
                sp.wait_ge(piece_kept, 4 * i + 6)
                sp.dma_start(weights_dram[part, bass.ds(i * P, P), :], rows_w[:, :, :].rearrange("d k p -> d (k p)")).then_inc(rows_stored, 16)

            sp.sem_inc(written[0], 16)
            sp.sem_inc(written[1], 16)
            sp.sem_inc(rows_stored, 16)
            sp.dma_start(src_rows[:, :], src_cols).then_inc(listed_src, 16)
            for n in range(4):
                sp.dma_start(tables[:, n, :, :], tables_dram[:, n, :].rearrange("p (t q s) -> p t q s", t=T, q=2)[:, :, part, :]).then_inc(tables_loaded, 16)
            sp.dma_start(rows_dram[ZERO_ROW:ZERO_ROW + 1, :], c.ident[P - 1:P, 0:D]).then_inc(zero_out, 16)

            def load_list(n, b):
                sp.dma_start(same[b][:, :], same_dram[bass.ds(n * BLK, BLK)].rearrange("(a e) -> a e", a=1).to_broadcast([D, BLK])).then_inc(listed[b], 16)

            load_list(0, 0)
            load_list(1, 1)
            with sp.Fori(0, LOOPS) as i:
                for b in range(RING):
                    n = RING * i + b
                    sp.wait_ge(kept, n + 3)
                    sp.dma_start(rows_dram[bass.ds(n * BLK, BLK), :].rearrange("(j p) d -> p j d", p=P), out[b % 2][:, :, :]).then_inc(written[b % 2], 16)
                    load_list(n + 2, b % 2)
                store_rows(i)
            store_rows(T)
            sp.wait_ge(rows_stored, 16 * (T + 2))
            for b in range(2):
                sp.wait_ge(written[b], 16 * (1 + NBLK // 2))
                sp.wait_ge(listed[b], 16 * (1 + NBLK // 2))
            sp.wait_ge(zero_out, 16)


ROW_SCALE = 64.0


def split_rows(nc, rows, parts):
    with nc.semaphore("rows_split") as split, nc.Block() as block:
        @block.vector
        def _(dve):
            nc.vector.tensor_scalar(rows[:, :, :], rows[:, :, :], ROW_SCALE, None, ALU.mult).then_inc(split, 1)
            dve.wait_ge(split, 1)
            nc.vector.tensor_copy(parts[:, :, 0, :], rows[:, :, :]).then_inc(split, 1)
            dve.wait_ge(split, 2)
            nc.vector.tensor_tensor(parts[:, :, 1, :], rows[:, :, :], parts[:, :, 0, :], ALU.subtract).then_inc(split, 1)


def weighted_sum(nc, c, adj, parts, weights_dram, total):
    banks = [(n, min(512, NP - n)) for n in range(0, NP, 512)]
    with stack() as ctx:
        sem = lambda n: ctx.enter_context(nc.semaphore(f"ws_{n}"))
        w3 = ctx.enter_context(nc.sbuf_tensor("ws_w", [P, 3, NP], F16))
        place = total[:, :, :].rearrange("p t d -> p (t d)").bitcast(F16)[:, 0:NP]
        w = [[w3[:, 0, :], w3[:, 1, :]], [w3[:, 2, :], place]]
        sums_ps = [ctx.enter_context(nc.psum_tensor(f"ws_sums{n}", [P, 512], F32)) for n in range(len(banks))]
        back_ps = ctx.enter_context(nc.psum_tensor("ws_back", [P, 512], F32))
        loaded = [[sem(f"loaded{b}{h}") for h in range(2)] for b in range(2)]
        used, kept, turned, drained = sem("used"), sem("kept"), sem("turned"), sem("drained")
        block = ctx.enter_context(nc.Block())
        sumsT = w3[0:D, 0:2, :].rearrange("p h n -> p (h n)").bitcast(F32)

        @block.gpsimd
        def _(pool):
            for t in range(T):
                own = adj[:, t, t * P:(t + 1) * P]
                nc.gpsimd.tensor_tensor(own, own, c.ident16[:, :], ALU.add)

        @block.sync
        def _(sp):
            def load(t, b, h):
                for half in range(2):
                    sp.dma_start(w[b][h][half * HALF:(half + 1) * HALF, :],
                                 weights_dram[half, bass.ds((t + 1) * P + h * HALF, HALF), :]).then_inc(loaded[b][h], 16)

            for b in range(2):
                for h in range(2):
                    load(b, b, h)
            with sp.Fori(1, T // 2) as i:
                for b in range(2):
                    for h in range(2):
                        sp.wait_ge(used, 4 * (i - 1) + 2 * b + h + 1)
                        load(2 * i + b, b, h)
            for h in range(2):
                sp.wait_ge(used, 2 * (T - 3) + h + 1)
                load(T - 1, 0, h)

        @block.tensor
        def _(pe):
            def add(i, b, first=False, last=False):
                tile = parts[:, bass.ds(2 * i + b, 1), :, :].rearrange("p a r d -> p (a r) d")
                for h in range(2):
                    pe.wait_ge(loaded[b][h], 32 * (i + 1))
                    for r in range(2):
                        for n, (begin, size) in enumerate(banks):
                            mm = nc.tensor.matmul(sums_ps[n][0:D, 0:size], tile[:, r, :], w[b][h][:, begin:begin + size],
                                                  start=first and h == r == 0, stop=last and h == r == 1, skip_group_check=True)
                    mm.then_inc(used, 1)

            add(0, 0, first=True)
            add(0, 1)
            with pe.Fori(1, T // 2) as i:
                for b in range(2):
                    add(i, b)
            add(T // 2, 0, last=True)
            pe.wait_ge(kept, len(banks))
            for t in range(T):
                if t >= 2:
                    pe.wait_ge(drained, t - 1)
                ps = back_ps if t % 2 == 0 else sums_ps[0]
                nc.tensor.transpose(ps[:, 0:D], sumsT[:, t * P:(t + 1) * P], c.ident[0:D, 0:D]).then_inc(turned, 1)

        @block.vector
        def _(dve):
            dve.wait_ge(used, 2 * T)
            for n, (begin, size) in enumerate(banks):
                nc.vector.tensor_scalar(sumsT[:, begin:begin + size], sums_ps[n][0:D, 0:size], 1.0 / (W_SCALE * ROW_SCALE), None, ALU.mult).then_inc(kept, 1)
            for t in range(T):
                dve.wait_ge(turned, t + 1)
                nc.vector.tensor_copy(total[:, t, :], back_ps[:, 0:D] if t % 2 == 0 else sums_ps[0][:, 0:D]).then_inc(drained, 1)


SUM_SCALE = 1024.0


def sum_pass(nc, c, overflow, table_dram, src_cols, dst_cols, w_cols, total):
    banks = [(n, min(512, NP - n)) for n in range(0, NP, 512)]
    with stack() as ctx:
        sb = lambda n, shape, dt: ctx.enter_context(nc.sbuf_tensor(f"sum_{n}", shape, dt))
        sem = lambda n: ctx.enter_context(nc.semaphore(f"sum_{n}"))
        index = [sb(f"index{i}", [P, 8], I32) for i in range(2)]
        row = [total[:, 4 * i:4 * (i + 1), :] for i in range(RING)]
        term = [sb(f"term{i}", [P, D], F32) for i in range(2)]
        hi = [sb(f"hi{i}", [P, D], F16) for i in range(2)]
        lo = [sb(f"lo{i}", [P, D], F16) for i in range(2)]
        hots = sb("hots", [P, 2, NP], F16)
        hot = [hots[:, i, :] for i in range(2)]
        nodes = sb("nodes", [P, NP], F16)
        nodes_i = hots[:, :, :].rearrange("p a n -> p (a n)").bitcast(I32)
        src_mid = sb("src_mid", [P, CHUNKS], F32)
        src_rows = sb("src_rows", [P, CHUNKS], I32)
        dst_rows, w_rows = sb("dst_rows", [P, CHUNKS], I32), sb("w_rows", [P, CHUNKS], F32)
        no_term = sb("no_term", [P, D], F16)
        sums_ps = [ctx.enter_context(nc.psum_tensor(f"sums{n}", [P, 512], F32)) for n in range(len(banks))]
        back_ps = ctx.enter_context(nc.psum_tensor("sums_back", [P, 512], F32))
        index_ready = sem("index_ready")
        gathered = [c.gather_sem(f"sum_gathered{i}") for i in range(RING)]
        ready, terms, split, used, gather_begun, kept, turned, drained, numbers = (
            sem("ready"), sem("terms"), sem("split"), sem("used"), sem("gather_begun"), sem("kept"), sem("turned"), sem("drained"), sem("numbers"))
        listed = sem("listed")
        block = ctx.enter_context(nc.Block())
        taken = lambda eng: eng.value_load(overflow[0:1, 0:1], min_val=0, max_val=NP) > 0
        sumsT = hots[0:D, :, :].rearrange("p a n -> p (a n)").bitcast(F32)

        @block.gpsimd
        def _(pool):
            with pool.If(taken(pool)):
                nc.gpsimd.iota(nodes_i, [[1, NP]], base=-NP // 2, channel_multiplier=0).then_inc(numbers, 1)
                pool.wait_ge(listed, 48)
                with pool.Fori(0, LOOPS) as i:
                    for b in range(RING):
                        if b % 2 == 0:
                            pool.wait_ge(terms, 16 * i + 4 * b + 8)
                            nc.gpsimd.tensor_copy(index[b // 2][:, :], dst_rows[:, bass.ds(4 * RING * i + 4 * b, 8)]).then_inc(index_ready, 1)
                            pool.wait_ge(index_ready, 2 * i + b // 2 + 1)
                            pool.sem_inc(gather_begun, 1)
                        for j in range(4):
                            nc.gpsimd.indirect_dma_start(row[b][:, j, :], None, table_dram,
                                                         bass.IndirectOffsetOnAxis(ap=index[b // 2][:, 4 * (b % 2) + j:4 * (b % 2) + j + 1], axis=0)
                                                         ).then_inc(gathered[b], 16)
                for b in range(RING):
                    pool.wait_ge(gathered[b], 64 * LOOPS)

        @block.sync
        def _(sp):
            with sp.If(taken(sp)):
                sp.dma_start(src_rows[:, :], src_cols).then_inc(listed, 16)
                sp.dma_start(dst_rows[:, :], dst_cols).then_inc(listed, 16)
                sp.dma_start(w_rows[:, :], w_cols).then_inc(listed, 16)

        @block.vector
        def _(dve):
            with dve.If(taken(dve)):
                dve.sem_inc(terms, 16)
                dve.wait_ge(listed, 48)
                dve.wait_ge(numbers, 1)
                nc.vector.tensor_copy(nodes[:, :], nodes_i).then_inc(drained, 1)
                nc.vector.tensor_copy(src_mid[:, :], src_rows[:, :]).then_inc(drained, 1)
                nc.vector.memset(no_term[:, :], 0.0).then_inc(ready, 1)
                dve.wait_ge(drained, 2)
                nc.vector.tensor_scalar(src_mid[:, :], src_mid[:, :], float(-NP // 2), None, ALU.add).then_inc(drained, 1)
                dve.wait_ge(drained, 3)
                with dve.Fori(0, LOOPS) as i:
                    for b in range(RING):
                        for j in range(4):
                            k = 4 * b + j
                            chunk = 16 * i + k
                            dve.wait_ge(used, chunk + 1)
                            nc.vector.tensor_scalar(hot[k % 2][:, :], nodes[:, :], src_mid[:, bass.ds(chunk, 1)], None, ALU.is_equal)
                            if j == 0:
                                dve.wait_ge(gathered[b], 64 * (i + 1))
                            t = nc.vector.tensor_scalar(term[k % 2][:, :], row[b][:, j, :], w_rows[:, bass.ds(chunk, 1)], SUM_SCALE, ALU.mult, ALU.mult)
                            t.then_inc(terms, 1)
                            dve.wait_ge(terms, chunk + 17)
                            nc.vector.tensor_copy(hi[k % 2][:, :], term[k % 2][:, :]).then_inc(split, 1)
                            dve.wait_ge(split, chunk + 1)
                            nc.vector.tensor_tensor(lo[k % 2][:, :], term[k % 2][:, :], hi[k % 2][:, :], ALU.subtract).then_inc(ready, 1)
                dve.wait_ge(used, CHUNKS + 3)
                for n, (first, size) in enumerate(banks):
                    nc.vector.tensor_scalar(sumsT[:, first:first + size], sums_ps[n][0:D, 0:size], 1.0 / SUM_SCALE, None, ALU.mult).then_inc(kept, 1)
                for t in range(T):
                    dve.wait_ge(turned, t + 1)
                    nc.vector.tensor_copy(total[:, t, :], back_ps[:, 0:D] if t % 2 == 0 else sums_ps[0][:, 0:D]).then_inc(drained, 1)

        @block.tensor
        def _(pe):
            with pe.If(taken(pe)):
                pe.sem_inc(used, 2)
                pe.wait_ge(ready, 1)
                for n, (first, size) in enumerate(banks):
                    nc.tensor.matmul(sums_ps[n][0:D, 0:size], no_term[:, :], nodes[:, first:first + size], start=True, stop=False, skip_group_check=True)
                with pe.Fori(0, LOOPS) as i:
                    for k in range(16):
                        chunk = 16 * i + k
                        pe.wait_ge(ready, chunk + 2)
                        for part in (hi, lo):
                            for n, (first, size) in enumerate(banks):
                                mm = nc.tensor.matmul(sums_ps[n][0:D, 0:size], part[k % 2][:, :], hot[k % 2][:, first:first + size],
                                                      start=False, stop=False, skip_group_check=True)
                        mm.then_inc(used, 1)
                for n, (first, size) in enumerate(banks):
                    mm = nc.tensor.matmul(sums_ps[n][0:D, 0:size], no_term[:, :], nodes[:, first:first + size], start=False, stop=True, skip_group_check=True)
                mm.then_inc(used, 1)
                pe.wait_ge(kept, len(banks))
                for t in range(T):
                    if t >= 2:
                        pe.wait_ge(drained, 3 + t - 1)
                    ps = back_ps if t % 2 == 0 else sums_ps[0]
                    nc.tensor.transpose(ps[:, 0:D], sumsT[:, t * P:(t + 1) * P], c.ident[0:D, 0:D]).then_inc(turned, 1)


def l2_normalise(nc, name, h, sq, load=()):
    with (
        nc.sbuf_tensor(name + "_norm", [P, T], F32) as norm,
        nc.semaphore(name + "_dve") as dve_step,
        nc.semaphore(name + "_root") as root_ready,
        nc.semaphore(name + "_loaded") as loaded,
        nc.Block() as block,
    ):
        @block.vector
        def _(dve):
            nc.vector.tensor_tensor(sq[:, :, :], h[:, :, :], h[:, :, :], ALU.mult).then_inc(dve_step, 1)
            dve.wait_ge(dve_step, 1)
            nc.vector.tensor_reduce(norm[:, :], sq[:, :, :], AX.X, ALU.add).then_inc(dve_step, 1)
            dve.wait_ge(root_ready, 1)
            nc.vector.tensor_scalar(norm[:, :], norm[:, :], 1e-12, None, ALU.max).then_inc(dve_step, 1)
            dve.wait_ge(dve_step, 3)
            nc.vector.reciprocal(norm[:, :], norm[:, :]).then_inc(dve_step, 1)
            dve.wait_ge(dve_step, 4)
            nc.vector.tensor_tensor(h[:, :, :], h[:, :, :], norm[:, :].unsqueeze(2).to_broadcast([P, T, D]), ALU.mult)

        @block.scalar
        def _(act):
            act.wait_ge(dve_step, 2)
            nc.scalar.activation(norm[:, :], norm[:, :], ACT.Sqrt).then_inc(root_ready, 1)

        @block.sync
        def _(sp):
            for tile, dram in load:
                sp.dma_start(tile[:, :, :], node_view(dram)).then_inc(loaded, 16)
            if load:
                sp.wait_ge(loaded, 16 * len(load))


def propagate_setup(nc, c, h, base, g, state, coef, root):
    with stack() as ctx:
        sb = lambda n, shape, dt: ctx.enter_context(nc.sbuf_tensor(n, shape, dt))
        deg, inv = sb("deg_loop", [P, T], F32), sb("inv_root", [P, T], F32)
        sem = lambda n: ctx.enter_context(nc.semaphore(n))
        d_step, deg_ready, rooted, state_made, base_made = sem("ps_step"), sem("ps_deg"), sem("ps_rooted"), sem("ps_state"), sem("ps_base")
        block = ctx.enter_context(nc.Block())

        @block.vector
        def _(dve):
            done = [0]

            def then_wait(ins):
                done[0] += 1
                ins.then_inc(d_step, 1)
                dve.wait_ge(d_step, done[0])

            nc.vector.tensor_scalar(deg[:, :], c.deg[:, :], 1.0, None, ALU.add).then_inc(deg_ready, 1)
            dve.wait_ge(rooted, 1)
            then_wait(nc.vector.tensor_scalar(root[:, :], root[:, :], 1.0 / GSCALE, None, ALU.mult))
            then_wait(nc.vector.reciprocal(inv[:, :], root[:, :]))
            nc.vector.tensor_tensor(state[:, :, :], h[:, :, :], inv[:, :].unsqueeze(2).to_broadcast([P, T, D]), ALU.mult).then_inc(state_made, 1)
            then_wait(nc.vector.reciprocal(coef[:, :], deg[:, :]))
            then_wait(nc.vector.tensor_scalar(coef[:, :], coef[:, :], 1.0 - ALPHA, None, ALU.mult))
            dve.wait_ge(state_made, 1)
            then_wait(nc.vector.tensor_copy(g[:, :, 0, :], state[:, :, :]))
            then_wait(nc.vector.tensor_tensor(g[:, :, 1, :], state[:, :, :], g[:, :, 0, :], ALU.subtract))

        @block.scalar
        def _(act):
            act.wait_ge(deg_ready, 1)
            nc.scalar.activation(root[:, :], deg[:, :], ACT.Sqrt).then_inc(rooted, 1)
            act.wait_ge(state_made, 1)
            nc.scalar.activation(base[:, :, :], state[:, :, :], ACT.Copy, scale=ALPHA).then_inc(base_made, 1)


def propagate(nc, c, adj, base, g, state, coef):
    BANKS, SIDE = 5, 3
    with stack() as ctx:
        ps = [ctx.enter_context(nc.psum_tensor(f"prop{i}", [P, 512], F32)) for i in range(BANKS)]
        part = ctx.enter_context(nc.sbuf_tensor("part", [P, 2, D], F32))
        sem = lambda n: ctx.enter_context(nc.semaphore(n))
        summed, low_added, state_ready, hi_ready, updated = sem("pr_summed"), sem("pr_low"), sem("pr_state"), sem("pr_hi"), sem("pr_updated")
        block = ctx.enter_context(nc.Block())

        @block.tensor
        def _(pe):
            with pe.Fori(0, K_PROP // 2) as i:
                for half in range(2):
                    step = 2 * i + half
                    def products(tiles):
                        for t in tiles:
                            pe.wait_ge(state_ready, T * step + T + t - BANKS + 1)
                        for k in range(T):
                            if tiles[0] == 0:
                                pe.wait_ge(updated, T * step + k + 1)
                            for t in tiles:
                                mm = nc.tensor.matmul(ps[t % BANKS][:, 0:2 * D], adj[:, k, t * P:(t + 1) * P],
                                                      g[half][:, k, :, :].rearrange("p a d -> p (a d)"), start=k == 0, stop=k == T - 1)
                                if k == T - 1:
                                    mm.then_inc(summed, 1)

                    products(range(SIDE))
                    for t in range(SIDE, T):
                        products([t])

        @block.vector
        def _(dve):
            dve.sem_inc(updated, T)
            dve.sem_inc(state_ready, T)
            with dve.Fori(0, K_PROP // 2) as i:
                for half in range(2):
                    step = 2 * i + half

                    def new_state(t):
                        dve.wait_ge(summed, T * step + t + 1)
                        nc.vector.scalar_tensor_tensor(part[:, t % 2, :], ps[t % BANKS][:, D:2 * D], coef[:, t:t + 1], base[:, t, :], ALU.mult, ALU.add).then_inc(low_added, 1)
                        dve.wait_ge(low_added, T * step + t + 1)
                        nc.vector.scalar_tensor_tensor(state[:, t, :], ps[t % BANKS][:, 0:D], coef[:, t:t + 1], part[:, t % 2, :], ALU.mult, ALU.add).then_inc(state_ready, 1)

                    def low_part(t):
                        dve.wait_ge(hi_ready, T * step + t + 1)
                        nc.vector.tensor_tensor(g[1 - half][:, t, 1, :], state[:, t, :], g[1 - half][:, t, 0, :], ALU.subtract).then_inc(updated, 1)

                    for t in range(T):
                        new_state(t)
                        low_part(t)

        @block.scalar
        def _(act):
            with act.Fori(0, K_PROP // 2) as i:
                for half in range(2):
                    for t in range(T):
                        act.wait_ge(state_ready, T * (2 * i + half) + T + t + 1)
                        nc.scalar.activation(g[1 - half][:, t, 0, :], state[:, t, :], ACT.Copy).then_inc(hi_ready, 1)


def finish(nc, x, state, root, out):
    PART = 5
    with nc.semaphore("scaled") as scaled, nc.semaphore("out_ready") as out_ready, nc.semaphore("out_written") as out_written, nc.Block() as block:
        @block.sync
        def _(sp):
            for n, t in enumerate(range(0, T, PART)):
                sp.wait_ge(out_ready, n + 1)
                whole = min(t + PART, T - 1)
                sp.dma_start(out[t * P:whole * P, :].rearrange("(t p) d -> p t d", p=P), state[:, t:whole, :]).then_inc(out_written, 16)
            sp.dma_start(out[(T - 1) * P:N, :], state[0:LAST, T - 1, :]).then_inc(out_written, 16)
            sp.wait_ge(out_written, 16 * (T // PART + 1))

        @block.vector
        def _(dve):
            for n, t in enumerate(range(0, T, PART)):
                tiles = state[:, t:t + PART, :]
                nc.vector.tensor_tensor(tiles, tiles, root[:, t:t + PART].unsqueeze(2).to_broadcast([P, PART, D]), ALU.mult).then_inc(scaled, 1)
                dve.wait_ge(scaled, n + 1)
                nc.vector.tensor_tensor(tiles, tiles, x[:, t:t + PART, :], ALU.add).then_inc(out_ready, 1)


def gnn(nc, x, src, dst, edge_weight, qW, kW, vW, Wp1, bp1, Ws1, Wn1, b1, Wp2, bp2, Ws2, Wn2, b2, G, bG, out):
    scratch = lambda name, shape, dt=F32: nc.dram_tensor(name, shape, dt).ap()
    src_pad, dst_pad = scratch("src_pad", (CHUNKS + 1, P), I32), scratch("dst_pad", (CHUNKS + 1, P), I32)
    win_dram, tables_dram = scratch("win_dram", (WROWS, 3, P), I32), scratch("tables_dram", (P, 4, NSTEP))
    dst_ext = scratch("dst_ext", (1 + EXT,), I32)
    w_pad = scratch("w_pad", (EXT,))
    same_dram = scratch("same_dram", (EXT,), F16)
    src_cols, dst_cols, w_cols = scratch("src_cols", (P, CHUNKS), I32), scratch("dst_cols", (P, CHUNKS), I32), scratch("w_cols", (P, CHUNKS))
    weights_dram = scratch("weights", (2, (T + 1) * P, NP), F16)
    group_dram = scratch("group_dram", (SPAD,), I32)
    q_dram, k_dram = scratch("q_dram", (D, T, 512), F16), scratch("k_dram", (D, T, 512), F16)
    v_dram = scratch("v_dram", (P, T * HEADS * (DH + 1)))
    xh_dram, h_dram, x_dram = (scratch(n, (P, T * D)) for n in ("xh_dram", "h_dram", "x_dram"))
    res_dram = scratch("res_dram", (P, (T + 1) * D))
    table = scratch("table", (NP, D))
    rows_dram = scratch("rows_dram", (EP + 1, D))

    with stack() as ctx:
        c = make_constants(nc, ctx)
        attention_inputs(nc, c, x, qW, kW, vW, xh_dram, q_dram, k_dram, v_dram)
        adj = ctx.enter_context(nc.sbuf_tensor("adj", [P, T, NP], F16))
        overflow = ctx.enter_context(nc.sbuf_tensor("overflow", [1, 1], I32))
        with stack() as own:
            first_row = own.enter_context(nc.sbuf_tensor("first_row", [1, PHASES, CHUNKS], F32))
            edge_lists(nc, c, src, dst, edge_weight, src_pad, dst_pad, dst_ext, w_pad, src_cols, dst_cols, w_cols, same_dram, win_dram, first_row)
            tables = own.enter_context(nc.sbuf_tensor("tables", [P, 4, NSTEP], F32))
            adjacency_windows(nc, c, win_dram, first_row, tables, tables_dram, overflow)
            build_adjacency(nc, c, adj, tables)
        walk_adjacency(nc, c, adj, overflow, src_pad, dst_pad, group_dram)
        attention(nc, c, adj, q_dram, k_dram, v_dram, res_dram)

        def node_tiles(own, name, n):
            return [own.enter_context(nc.sbuf_tensor(f"{name}{i}", [P, T, D], F32)) for i in range(n)]

        with stack() as own:
            xt, h, r = node_tiles(own, "n1_", 3)
            deg_ps = own.enter_context(nc.psum_tensor("deg_ps", [P, 512], F32))
            layernorm_relu(nc, "ln1", xt, h, r, load=((xt, xh_dram), (r, res_dram[:, D:(T + 1) * D])), term=r,
                           count_degrees=(adj, c, deg_ps))
            degrees(nc, c, deg_ps)
            project(nc, c, "pool1", ((h, Wp1),), bp1, r, to_store=table, relu=True, keep=((x_dram, xt), (h_dram, h)))
        clear_semaphores(nc)
        max_pass(nc, c, "max1", table, src_cols, same_dram, rows_dram, tables_dram, weights_dram, 0)
        with stack() as own:
            h, agg, o = node_tiles(own, "n2_", 3)
            project(nc, c, "sage1", ((h, Ws1), (agg, Wn1)), b1, o, relu=True, load=((h, h_dram),), pick=(agg, rows_dram))
            l2_normalise(nc, "l2a", o, h)
            project(nc, c, "pool2", ((o, Wp2),), bp2, agg, to_store=table, relu=True, keep=((h_dram, o),))
        max_pass(nc, c, "max2", table, src_cols, same_dram, rows_dram, tables_dram, weights_dram, 1)
        with stack() as own:
            state, xt = node_tiles(own, "n4_", 2)
            with stack() as sums:
                h, = node_tiles(sums, "n5_", 1)
                support = h[:, :, :].rearrange("p t d -> p (t d)").bitcast(F16).rearrange("p (t r d) -> p t r d", t=T, r=2)
                with stack() as nodes:
                    o, = node_tiles(nodes, "n3_", 1)
                    agg = state
                    project(nc, c, "sage2", ((h, Ws2), (agg, Wn2)), b2, o, load=((h, h_dram),), pick=(agg, rows_dram))
                    l2_normalise(nc, "l2b", o, h, load=((xt, x_dram),))
                    layernorm_relu(nc, "ln2", xt, h, agg, term=o)
                    project(nc, c, "support", ((h, G),), None, o, to_store=table)
                    split_rows(nc, o, support)
                clear_semaphores(nc)
                weighted_sum(nc, c, adj, support, weights_dram, state)
            sum_pass(nc, c, overflow, table, src_cols, dst_cols, w_cols, state)
            base, = node_tiles(own, "n6_", 1)
            coef, root = (own.enter_context(nc.sbuf_tensor(n, [P, T], F32)) for n in ("coef", "root"))
            g = [own.enter_context(nc.sbuf_tensor(f"g{i}", [P, T, 2, D], F16)) for i in range(2)]
            layernorm_relu(nc, "ln3", xt, base, state, term=state, bias_dram=bG)
            propagate_setup(nc, c, base, base, g[0], state, coef, root)
            propagate(nc, c, adj, base, g, state, coef)
            finish(nc, xt, state, root, out)


_INS = ["x", "src", "dst", "edge_weight", "L0_gnn_qW", "L0_gnn_kW", "L0_gnn_vW", "L1_gnn_Wp1", "L1_gnn_bp1", "L1_gnn_Ws1",
        "L1_gnn_Wn1", "L1_gnn_b1", "L1_gnn_Wp2", "L1_gnn_bp2", "L1_gnn_Ws2", "L1_gnn_Wn2", "L1_gnn_b2",
        "L2_gnn_weight_G", "L2_gnn_bias_G"]


def kernel(**inputs):
    import numpy as np
    import concourse.bacc as bacc
    from concourse.bass_utils import run_bass_kernel_spmd

    nc = bacc.Bacc("TRN2", target_bir_lowering=False, num_devices=1)
    arrays, args = {}, []
    for name in _INS:
        a = np.ascontiguousarray(inputs[name])
        arrays[f"in_{name}_dram"] = a
        args.append(nc.dram_tensor(f"in_{name}_dram", a.shape, mybir.dt.from_np(a.dtype), kind="ExternalInput").ap())
    out = nc.dram_tensor("out_0_dram", (N, D), F32, kind="ExternalOutput").ap()
    gnn(nc, *args, out)
    r = run_bass_kernel_spmd(nc, [arrays], core_ids=[0])
    return r.results[0]["out_0_dram"]
```
